# Optimizing a Trainium2 kernel written in Bass

```python
import numpy as np
import jax
import jax.numpy as jnp

def _softmax(x, axis=-1):
    return jax.nn.softmax(x, axis=axis)

def _gelu(x):
    return jax.nn.gelu(x, approximate=True)

def _silu(x):
    return jax.nn.silu(x)

def _sigmoid(x):
    return jax.nn.sigmoid(x)

def _layernorm(x, axis=-1, eps=1e-05):
    m = jnp.mean(x, axis=axis, keepdims=True)
    v = jnp.var(x, axis=axis, keepdims=True)
    return (x - m) / jnp.sqrt(v + eps)

def _scatter_add(tgt, idx, src, axis=0):
    return tgt.at[idx].add(src)

def _segment_sum(src, seg, n):
    return jax.ops.segment_sum(src, seg, n)
kernel_name = 'mk_gnn_ffn_d1_gnn_r32_8a3d21'

def setup_inputs(seed: int=0):
    np.random.seed(seed)
    _w = jnp.asarray

    def _rec_inputs():
        import jax
        import jax.numpy as jnp
        _gk = jax.random.key(seed)
        x = -8.776e-05 + 1 * jax.random.normal(jax.random.fold_in(_gk, 1), (10000, 512), jnp.float32)
        src = jax.random.randint(jax.random.fold_in(_gk, 2), (10000,), 0, 10000, jnp.int32)
        dst = jnp.minimum((10000 * jax.random.uniform(jax.random.fold_in(_gk, 3), (10000,)) ** 2.0).astype(jnp.int32), 9999)
        _o = jnp.argsort(dst, stable=True)
        src = src[_o]
        dst = dst[_o]
        edge_attr_512 = -8.513e-05 + 0.999844 * jax.random.normal(jax.random.fold_in(_gk, 11), (10000, 512), jnp.float32)
        return (x, src, dst, edge_attr_512)
    x, src, dst, edge_attr_512 = _rec_inputs()

    def _L0_gnn_setup():
        import jax, jax.numpy as jnp
        import numpy as np
        N = 10000
        E = 5000
        D = 512
        key = jax.random.key(seed)
        k1, k2, k3, k4, k5 = jax.random.split(key, 5)
        node_tokens = jax.random.normal(k1, (N, D), dtype=jnp.float32)
        relation_tokens = jax.random.normal(k2, (E, D), dtype=jnp.float32)
        edge_index = jax.random.randint(k3, (2, E), 0, N, dtype=jnp.int64)
        lim_m = float(np.sqrt(6.0 / (D + D)))
        Wm = jax.random.uniform(k4, (D, D), minval=-lim_m, maxval=lim_m, dtype=jnp.float32)
        bm = jnp.zeros((D,), dtype=jnp.float32)
        lim_u = float(np.sqrt(6.0 / (2 * D + D)))
        Wu = jax.random.uniform(k5, (D, 2 * D), minval=-lim_u, maxval=lim_u, dtype=jnp.float32)
        bu = jnp.zeros((D,), dtype=jnp.float32)
        gamma = jnp.ones((D,), dtype=jnp.float32)
        beta = jnp.zeros((D,), dtype=jnp.float32)
        return {'node_tokens': node_tokens, 'relation_tokens': relation_tokens, 'edge_index': edge_index, 'num_nodes': N, 'Wm': Wm, 'bm': bm, 'Wu': Wu, 'bu': bu, 'gamma': gamma, 'beta': beta}
    _L0_gnn_all = _L0_gnn_setup()
    _L0_gnn_in = {k: v for k, v in _L0_gnn_all.items() if k in ('Wm', 'bm', 'Wu', 'bu', 'gamma', 'beta')}
    del _L0_gnn_all

    def _L0_ffn_setup():
        import jax, jax.numpy as jnp
        import numpy as np
        D, H, E, B, S = (512, 64, 16, 8, 256)
        MAX_GROUP_SIZE = 128
        MIN_CAPACITY = 8
        CAPACITY_FACTOR = 1.0

        def _group_dims(num_tokens, num_experts):
            num_groups = -(-num_tokens // MAX_GROUP_SIZE)
            while num_tokens % num_groups != 0 or num_groups % num_experts != 0:
                num_groups += 1
            return (num_tokens // num_groups, num_groups)
        key = jax.random.key(seed)
        ks = jax.random.split(key, 6)
        s = 0.02
        return {'x': jax.random.normal(ks[0], (B, S, D), jnp.float32), 'gate_w': jax.random.normal(ks[1], (D, E), jnp.float32) * s, 'w1': jax.random.normal(ks[2], (E, D, H), jnp.float32) * s, 'b1': jnp.zeros((E, H), jnp.float32), 'w2': jax.random.normal(ks[3], (E, H, D), jnp.float32) * s, 'b2': jnp.zeros((E, D), jnp.float32), 'sw1': jax.random.normal(ks[4], (D, H), jnp.float32) * s, 'sb1': jnp.zeros((H,), jnp.float32), 'sw2': jax.random.normal(ks[5], (H, D), jnp.float32) * s, 'sb2': jnp.zeros((D,), jnp.float32)}
    _L0_ffn_all = _L0_ffn_setup()
    _L0_ffn_in = {k: v for k, v in _L0_ffn_all.items() if k in ('gate_w', 'w1', 'b1', 'w2', 'b2', 'sw1', 'sb1', 'sw2', 'sb2')}
    del _L0_ffn_all
    return {'x': x, 'src': src, 'dst': dst, 'edge_attr_512': edge_attr_512, 'L0_gnn_Wm': _L0_gnn_in['Wm'], 'L0_gnn_bm': _L0_gnn_in['bm'], 'L0_gnn_Wu': _L0_gnn_in['Wu'], 'L0_gnn_bu': _L0_gnn_in['bu'], 'L0_gnn_gamma': _L0_gnn_in['gamma'], 'L0_gnn_beta': _L0_gnn_in['beta'], 'L0_ffn_gate_w': _L0_ffn_in['gate_w'], 'L0_ffn_w1': _L0_ffn_in['w1'], 'L0_ffn_b1': _L0_ffn_in['b1'], 'L0_ffn_w2': _L0_ffn_in['w2'], 'L0_ffn_b2': _L0_ffn_in['b2'], 'L0_ffn_sw1': _L0_ffn_in['sw1'], 'L0_ffn_sb1': _L0_ffn_in['sb1'], 'L0_ffn_sw2': _L0_ffn_in['sw2'], 'L0_ffn_sb2': _L0_ffn_in['sb2']}

def reference(x, src, dst, edge_attr_512, L0_gnn_Wm, L0_gnn_bm, L0_gnn_Wu, L0_gnn_bu, L0_gnn_gamma, L0_gnn_beta, L0_ffn_gate_w, L0_ffn_w1, L0_ffn_b1, L0_ffn_w2, L0_ffn_b2, L0_ffn_sw1, L0_ffn_sb1, L0_ffn_sw2, L0_ffn_sb2):
    import jax
    import jax.numpy as jnp

    def _L0_gnn_ref(node_tokens, relation_tokens, edge_index, num_nodes, Wm, bm, Wu, bu, gamma, beta):
        import jax, jax.numpy as jnp
        import numpy as np
        N = 10000
        E = 5000
        D = 512
        head = edge_index[0]
        tail = edge_index[1]
        msg = node_tokens[head] + relation_tokens
        msg = msg @ Wm.T + bm
        agg = jax.ops.segment_sum(msg, tail, num_segments=num_nodes)
        deg = jax.ops.segment_sum(jnp.ones((msg.shape[0],), dtype=msg.dtype), tail, num_segments=num_nodes)
        agg = agg / jnp.maximum(deg, 1.0)[:, None]
        update_in = jnp.concatenate((node_tokens, agg), axis=-1)
        update = update_in @ Wu.T + bu
        out = node_tokens + jax.nn.gelu(update, approximate=False)
        mean = jnp.mean(out, axis=-1, keepdims=True)
        var = jnp.var(out, axis=-1, keepdims=True)
        return (out - mean) / jnp.sqrt(var + 1e-05) * gamma + beta

    def _L0_ffn_ref(x, gate_w, w1, b1, w2, b2, sw1, sb1, sw2, sb2):
        import jax, jax.numpy as jnp
        import numpy as np
        D, H, E, B, S = (512, 64, 16, 8, 256)
        MAX_GROUP_SIZE = 128
        MIN_CAPACITY = 8
        CAPACITY_FACTOR = 1.0

        def _group_dims(num_tokens, num_experts):
            num_groups = -(-num_tokens // MAX_GROUP_SIZE)
            while num_tokens % num_groups != 0 or num_groups % num_experts != 0:
                num_groups += 1
            return (num_tokens // num_groups, num_groups)
        Bn, Sn, Dn = x.shape
        En = gate_w.shape[1]
        T = Bn * Sn
        group_size, num_groups = _group_dims(T, En)
        cap = max(int(round(CAPACITY_FACTOR * group_size * num_groups / En)), MIN_CAPACITY)
        xg = x.reshape(num_groups, group_size, Dn)
        logits = jnp.einsum('gsd,de->gse', xg, gate_w)
        probs = jax.nn.softmax(logits, axis=-1)
        flat_probs = probs.transpose(2, 0, 1).reshape(En, T)
        scores, tok_idx = jax.lax.top_k(flat_probs, cap)
        xf = x.reshape(T, Dn)
        toks = xf[tok_idx]
        h = jax.nn.gelu(jnp.einsum('ecd,edh->ech', toks, w1) + b1[:, None, :])
        y = jnp.einsum('ech,ehd->ecd', h, w2) + b2[:, None, :]
        y = y * scores[..., None]
        routed = jnp.zeros_like(xf).at[tok_idx.reshape(-1)].add(y.reshape(-1, Dn))
        shared = jax.nn.gelu(xf @ sw1 + sb1) @ sw2 + sb2
        out = (routed + shared).reshape(Bn, Sn, Dn)
        return out
    edge_index = jnp.stack([src, dst])
    x = x + _L0_gnn_ref(_layernorm(x, axis=-1), edge_attr_512, edge_index, 10000, L0_gnn_Wm, L0_gnn_bm, L0_gnn_Wu, L0_gnn_bu, L0_gnn_gamma, L0_gnn_beta)
    x = x + _L0_ffn_ref(_layernorm(x, axis=-1)[None], L0_ffn_gate_w, L0_ffn_w1, L0_ffn_b1, L0_ffn_w2, L0_ffn_b2, L0_ffn_sw1, L0_ffn_sb1, L0_ffn_sw2, L0_ffn_sb2)[0]
    return x

_drawn_inputs = setup_inputs


def setup_inputs(seed=0):
    import zlib

    import numpy as np

    out = dict(_drawn_inputs(seed))
    spreads = {'L0_gnn_bm': (0.0, 0.464),
     'L0_gnn_bu': (0.0, 0.1),
     'L0_gnn_gamma': (1.0, 0.2),
     'L0_gnn_beta': (0.0, 0.1),
     'L0_ffn_b1': (0.0, 0.8),
     'L0_ffn_b2': (0.0, 0.8),
     'L0_ffn_sb1': (0.0, 2.0),
     'L0_ffn_sb2': (0.0, 0.1)}
    factors = {'L0_ffn_gate_w': 7.599, 'L0_ffn_w1': 8.0, 'L0_ffn_w2': 8.0, 'L0_ffn_sw1': 2.742}
    for name, (base, spread) in spreads.items():
        noise = np.random.default_rng([zlib.crc32(name.encode()), seed]).standard_normal(out[name].shape)
        drawn = base * np.exp(spread * noise) if base else spread * noise
        out[name] = jnp.asarray(drawn.astype(out[name].dtype))
    for name, factor in factors.items():
        out[name] = (out[name] * factor).astype(out[name].dtype)
    return out
```

```python
from contextlib import ExitStack

import concourse.bass as bass
from concourse import mybir

P = 128
ALU = mybir.AluOpType
ACT = mybir.ActivationFunctionType
F32 = mybir.dt.float32
I32 = mybir.dt.int32
AX_X = mybir.AxisListType.X
EPS = 1e-5
CREDIT = 2


class At:

    def __init__(self, pair, half):
        self.pair, self.half = pair, half

    def __add__(self, d):
        return At(self.pair + (self.half + d) // 2, (self.half + d) % 2)

    @property
    def n(self):
        return self.pair * 2 + self.half

    @property
    def static(self):
        return isinstance(self.pair, int)

    def within(self, count):
        return not self.static or 0 <= self.n < count

    @property
    def done(self):
        return self.n + CREDIT + 1

    @property
    def freed(self):
        return self.n + 1

    @property
    def landed(self):
        return (self.pair + 1) * 16

    @property
    def landed_before(self):
        return self.pair * 16


def alone(eng):
    eng.nop(nofuse=True)


def for_tiles(eng, count, lead, lag, step):
    first = (lag + 1) // 2 * 2
    pairs_end = (count - lead) // 2
    for k in range(-lead, first):
        step(At(k // 2, k % 2))
    with eng.Fori(first // 2, pairs_end) as pair:
        step(At(pair, 0))
        step(At(pair, 1))
    for k in range(2 * pairs_end, count + lag):
        step(At(k // 2, k % 2))


def gnn_then_expert_choice_ffn(nc, x, src, dst, dst_c, edge_attr, WmN, bm, WuT, bu, gamma, beta,
                               gate, w1, b1, w2, b2, sw1, sb1, sw2, sb2, out):
    N, D = x.shape
    EDGES = edge_attr.shape[0]
    DC = D // P
    _, NT = src.shape
    TAIL = N - (NT - 1) * P
    assert EDGES == N and NT * P >= N
    E, _, H = w1.shape
    CAP = N // E
    SLOT_P = 125
    SLOT_G = CAP // SLOT_P
    assert SLOT_P * SLOT_G == CAP and D == DC * P
    TOK = NT * P
    CH = P // E
    CL = TOK // CH
    RQ = 16
    RL = CL // RQ
    RR = CH * RQ
    assert CH * CL == TOK and RQ * RL == CL
    AW = D + 1
    TW = D + E
    AROWS = P * (N // P + 2)
    TRASH = N + 1
    assert TRASH + P <= AROWS

    agg = nc.dram_tensor("agg", (AROWS, AW), F32, kind="Internal").ap()
    fused_w_d = nc.dram_tensor("fused_w_d", (P, DC * D), F32, kind="Internal").ap()
    fused_b_d = nc.dram_tensor("fused_b_d", (P, D), F32, kind="Internal").ap()
    table = nc.dram_tensor("table", (TOK, TW), F32, kind="Internal").ap()
    hidden_d = nc.dram_tensor("hidden_d", (H, TOK), F32, kind="Internal").ap()
    logit_d = nc.dram_tensor("logit_d", (P, NT * E), F32, kind="Internal").ap()
    prob_d = nc.dram_tensor("prob_d", (E, TOK), F32, kind="Internal").ap()
    rank_d = nc.dram_tensor("rank_d", (E * RR, RL), F32, kind="Internal").ap()
    ends_d = nc.dram_tensor("ends_d", (1, E * RR), F32, kind="Internal").ap()

    with ExitStack() as whole:
        def sb(name, shape, dt=F32, scope=whole):
            return scope.enter_context(nc.sbuf_tensor(name, shape, dt))

        def sem(name):
            return whole.enter_context(nc.semaphore(name))

        def pair_of(name):
            return [sem(f"{name}0"), sem(f"{name}1")]

        bank = [whole.enter_context(nc.psum_tensor(f"bank{i}", [P, 512], F32)) for i in range(8)]

        ident = sb("ident", [P, P])
        neg_half = sb("neg_half", [P, 1])
        nodes_scope = whole.enter_context(ExitStack())
        nodes = sb("nodes", [P, NT * D], scope=nodes_scope)

        def node_slot(t):
            return nodes[:, bass.ds(t.n * D, D)]

        def rows(ap, t, last):
            return ap[(NT - 1) * P:(NT - 1) * P + TAIL, :] if last else ap[bass.ds(t.n * P, P), :]

        zeros_done, const_in, fused_stored = sem("zeros_done"), sem("const_in"), sem("fused_stored")
        p0_pool, p0_dve, p0_pe, fused_copied = sem("p0_pool"), sem("p0_dve"), sem("p0_pe"), sem("fused_copied")
        with ExitStack() as scope, nc.Block() as block:
            zeros = nodes[:, NT * D - AW:NT * D]
            bm_col = sb("bm_col", [P, DC], scope=scope)
            bm_wide = sb("bm_wide", [P, DC, P], scope=scope)
            wm_sb = nodes[:, 0:DC * D].rearrange("p (c n) -> p c n", c=DC)
            wur_sb = nodes[:, DC * D:2 * DC * D].rearrange("p (c n) -> p c n", c=DC)
            fused_sb = nodes[:, 2 * DC * D:3 * DC * D].rearrange("p (c n) -> p c n", c=DC)
            fused_b_sb = nodes[:, 3 * DC * D:3 * DC * D + D]

            @block.sync
            def _(sp):
                sp.dma_start(wm_sb, WmN.rearrange("(c p) n -> p c n", p=P)).then_inc(const_in, 16)
                sp.dma_start(wur_sb, WuT[D:2 * D, :].rearrange("(c p) n -> p c n", p=P)).then_inc(const_in, 16)
                sp.dma_start(bm_col[:], bm).then_inc(const_in, 16)
                sp.wait_ge(fused_copied, DC + 1)
                sp.dma_start(fused_w_d, nodes[:, 2 * DC * D:3 * DC * D]).then_inc(fused_stored, 16)
                sp.dma_start(fused_b_d, fused_b_sb).then_inc(fused_stored, 16)
                sp.wait_ge(fused_stored, 32)

            @block.gpsimd
            def _(pool):
                nc.gpsimd.memset(ident[:], 0.0).then_inc(p0_pool, 1)
                nc.gpsimd.memset(neg_half[:], -0.5)
                pool.wait_ge(p0_pool, 1)
                nc.gpsimd.affine_select(out=ident[:], in_=ident[:], compare_op=ALU.not_equal, fill=1.0, base=0,
                                        pattern=[[-1, P]], channel_multiplier=1).then_inc(p0_pool, 1)

            @block.scalar
            def _(act):
                act.wait_ge(p0_dve, 1)
                act.dma_start(agg.rearrange("(p r) w -> p r w", p=P),
                              zeros.unsqueeze(1).to_broadcast([P, AROWS // P, AW])).then_inc(zeros_done, 16)

            @block.vector
            def _(dve):
                nc.vector.memset(zeros, 0.0).then_inc(p0_dve, 1)
                dve.wait_ge(const_in, 48)
                nc.vector.tensor_copy(bm_wide[:], bm_col[:].unsqueeze(2).to_broadcast([P, DC, P])).then_inc(p0_dve, 1)
                for c in range(DC + 1):
                    dve.wait_ge(p0_pe, c + 1)
                    nc.vector.tensor_copy(fused_sb[:, c, :] if c < DC else fused_b_sb, bank[c][:]).then_inc(fused_copied, 1)

            @block.tensor
            def _(pe):
                pe.wait_ge(const_in, 48)
                for c in range(DC):
                    for j in range(DC):
                        last = nc.tensor.matmul(bank[c][:], wm_sb[:, j, c * P:(c + 1) * P], wur_sb[:, j, :],
                                                start=(j == 0), stop=(j == DC - 1))
                    last.then_inc(p0_pe, 1)
                pe.wait_ge(p0_dve, 2)
                for j in range(DC):
                    last = nc.tensor.matmul(bank[DC][:], bm_wide[:, j, :], wur_sb[:, j, :], start=(j == 0), stop=(j == DC - 1))
                last.then_inc(p0_pe, 1)

        w1_in = sem("w1_in")
        x_in, xg_in, ea_in, dr_in = pair_of("x_in"), pair_of("xg_in"), pair_of("ea_in"), pair_of("dr_in")
        scattered = pair_of("scattered")
        p1_const = sem("p1_const")
        src_picked = sem("src_picked")
        x_raw, x_stats, x_eps, x_pow, x_rstd = sem("x_raw"), sem("x_stats"), sem("x_eps"), sem("x_pow"), sem("x_rstd")
        g_raw, g_stats, g_eps, g_pow, g_rstd = sem("g_raw"), sem("g_stats"), sem("g_eps"), sem("g_pow"), sem("g_rstd")
        x_norm, x_turned, x_turned_sb = sem("x_norm"), sem("x_turned"), sem("x_turned_sb")
        g_norm, msg_ready, same_ready, earlier = sem("g_norm"), sem("msg_ready"), sem("same_ready"), sem("earlier")
        idx_step, idx_ready = sem("idx_step"), sem("idx_ready")
        sums, sums_sb, left, left_sb = sem("sums"), sem("sums_sb"), sem("left"), sem("left_sb")

        def rstd_on_pool(pool, t, stats, stats_done, eps_sem, pow_sem, out_sem):
            pool.wait_ge(stats_done, t.done)
            alone(pool)
            nc.gpsimd.tensor_scalar(stats[:, 2:3], stats[:, 1:2], EPS, None, ALU.add).then_inc(eps_sem, 1)
            pool.wait_ge(eps_sem, t.done)
            nc.gpsimd.tensor_tensor(stats[:, 3:4], stats[:, 2:3], neg_half[:], ALU.pow).then_inc(pow_sem, 1)
            pool.wait_ge(pow_sem, t.done)
            alone(pool)
            nc.gpsimd.tensor_scalar(stats[:, 4:5], stats[:, 0:1], stats[:, 3:4], -1.0, ALU.mult, ALU.mult).then_inc(out_sem, 1)

        def credit(eng, *sems):
            for s in sems:
                eng.sem_inc(s, CREDIT)

        with ExitStack() as scope, nc.Block() as block:
            def two(name, shape, dt=F32):
                return [sb(f"{name}{b}", shape, dt, scope) for b in range(2)]

            wul_sb = sb("wul_sb", [P, DC, D], scope=scope)
            bu_sb = sb("bu_sb", [P, D], scope=scope)
            src_col = sb("src_col", [P, NT], I32, scope)
            dst_col = sb("dst_col", [P, NT], I32, scope)
            dst_f = sb("dst_f", [P, NT], scope=scope)
            to_trash = sb("to_trash", [P, NT], scope=scope)
            trash_row = sb("trash_row", [P, 1], scope=scope)
            before = sb("before", [P, P], scope=scope)
            x_t, xg, ea = two("x_t", [P, D]), two("xg", [P, D]), two("ea", [P, D])
            dst_row = two("dst_row", [P, P], I32)
            src_idx, dst_idx = two("src_idx", [P, 1], I32), two("dst_idx", [P, 1], I32)
            xs6, gs6 = two("xs6", [P, 6]), two("gs6", [P, 6])
            xs, gs = two("xs", [P, 5]), two("gs", [P, 5])
            xn, msg, xT = two("xn", [P, D]), two("msg", [P, D]), two("xT", [P, D])
            same, prior, n_prior, moved = two("same", [P, P]), sb("prior", [P, P], scope=scope), two("n_prior", [P, 1]), two("moved", [P, 1])
            sum_sb = two("sum_sb", [P, AW])
            ps_turn, ps_left, ps_sum = bank[0:2], bank[2:4], bank[4:6]

            @block.sync
            def _(sp):
                sp.dma_start(src_col[:], src).then_inc(w1_in, 16)
                sp.dma_start(dst_col[:], dst_c).then_inc(w1_in, 16)
                sp.dma_start(wul_sb[:], WuT[0:D, :].rearrange("(c p) n -> p c n", p=P)).then_inc(w1_in, 16)
                sp.dma_start(bu_sb[:], bu.partition_broadcast(P)).then_inc(w1_in, 16)

                def loads(t):
                    last = t.static and t.n == NT - 1
                    r = TAIL if last else P
                    sp.wait_ge(x_norm, t.freed)
                    sp.dma_start(x_t[t.half][0:r, :], rows(x, t, last)).then_inc(x_in[t.half], 16)
                    sp.wait_ge(same_ready, t.freed)
                    alone(sp)
                    sp.dma_start(dst_row[t.half][:], dst[bass.ds(t.n * P, P)].partition_broadcast(P)).then_inc(dr_in[t.half], 16)
                    sp.wait_ge(msg_ready, t.freed)
                    sp.dma_start(ea[t.half][0:r, :], rows(edge_attr, t, last)).then_inc(ea_in[t.half], 16)

                for_tiles(sp, NT, 0, 0, loads)

            @block.gpsimd
            def _(pool):
                nc.gpsimd.memset(before[:], 1.0).then_inc(p1_const, 1)
                nc.gpsimd.iota(trash_row[:], pattern=[[0, 1]], base=TRASH, channel_multiplier=1,
                               allow_small_or_imprecise_dtypes=True).then_inc(p1_const, 1)
                pool.wait_ge(p1_const, 1)
                nc.gpsimd.affine_select(out=before[:], in_=before[:], compare_op=ALU.is_gt, fill=0.0, base=0,
                                        pattern=[[-1, P]], channel_multiplier=1).then_inc(p1_const, 1)
                credit(pool, src_picked, x_eps, x_pow, x_rstd, g_eps, g_pow, g_rstd)
                pool.wait_ge(w1_in, 64)
                pool.wait_ge(zeros_done, 16)

                def step(k):
                    t = k + 1
                    if t.within(NT):
                        rstd_on_pool(pool, t, xs[t.half], x_stats, x_eps, x_pow, x_rstd)
                    if k.within(NT):
                        rstd_on_pool(pool, k, gs[k.half], g_stats, g_eps, g_pow, g_rstd)
                    t = k + 2
                    if t.within(NT):
                        pool.wait_ge(xg_in[t.half], t.landed_before)
                        nc.gpsimd.tensor_copy(src_idx[t.half][:], src_col[:, bass.ds(t.n, 1)]).then_inc(src_picked, 1)
                        pool.wait_ge(src_picked, t.done)
                        pool.wait_ge(g_norm, t.freed)
                        alone(pool)
                        nc.gpsimd.indirect_dma_start(
                            xg[t.half][:], None, x, bass.IndirectOffsetOnAxis(src_idx[t.half][:], 0),
                        ).then_inc(xg_in[t.half], 16)
                    if k.within(NT):
                        pool.wait_ge(sums_sb, k.done)
                        pool.wait_ge(idx_ready, k.done)
                        t = k + -1
                        if not (k.static and k.n == 0):
                            pool.wait_ge(scattered[t.half], t.landed)
                        alone(pool)
                        nc.gpsimd.indirect_dma_start(
                            agg, bass.IndirectOffsetOnAxis(dst_idx[k.half][:], 0), sum_sb[k.half][:], None,
                            compute_op=ALU.add).then_inc(scattered[k.half], 16)

                for_tiles(pool, NT, 2, 1, step)
                for t in (At((NT - 2) // 2, (NT - 2) % 2), At((NT - 1) // 2, (NT - 1) % 2)):
                    pool.wait_ge(scattered[t.half], t.landed)

            @block.scalar
            def _(act):
                credit(act, x_norm, g_norm, x_turned_sb, sums_sb)

                def step(k):
                    t = k + 1
                    if t.within(NT):
                        act.wait_ge(x_rstd, t.done)
                        act.wait_ge(x_turned, t.freed)
                        nc.scalar.activation(xn[t.half][:], x_t[t.half][:], ACT.Identity, bias=xs[t.half][:, 4:5],
                                             scale=xs[t.half][:, 3:4]).then_inc(x_norm, 1)
                    if k.within(NT):
                        act.wait_ge(g_rstd, k.done)
                        act.wait_ge(sums, k.freed)
                        nc.scalar.activation(msg[k.half][:], xg[k.half][:], ACT.Identity, bias=gs[k.half][:, 4:5],
                                             scale=gs[k.half][:, 3:4]).then_inc(g_norm, 1)
                    if t.within(NT):
                        act.wait_ge(x_turned, t.done)
                        act.wait_ge(left, t.freed)
                        nc.scalar.copy(xT[t.half][:], ps_turn[t.half][:]).then_inc(x_turned_sb, 1)
                    if k.within(NT):
                        act.wait_ge(sums, k.done)
                        act.wait_ge(scattered[k.half], k.landed_before)
                        nc.scalar.copy(sum_sb[k.half][:, 0:D], ps_sum[k.half][:]).then_inc(sums_sb, 1)

                for_tiles(act, NT, 1, 1, step)

            @block.vector
            def _(dve):
                credit(dve, x_raw, x_stats, g_raw, g_stats, msg_ready, same_ready, earlier, idx_step, idx_ready, left_sb)
                dve.wait_ge(w1_in, 64)
                dve.wait_ge(p1_const, 3)
                nc.vector.tensor_copy(dst_f[:], dst_col[:]).then_inc(p1_const, 1)
                dve.wait_ge(p1_const, 4)
                nc.vector.tensor_scalar(to_trash[:], dst_f[:], -1.0, trash_row[:], ALU.mult, ALU.add).then_inc(p1_const, 1)
                dve.wait_ge(p1_const, 5)

                def stats(t, data, arrived, six, raw, two_, stats_done, free):
                    dve.wait_ge(arrived[t.half], t.landed)
                    alone(dve)
                    nc.vector.bn_stats(six[t.half][:], data[t.half][:]).then_inc(raw, 1)
                    dve.wait_ge(raw, t.done)
                    dve.wait_ge(free, t.freed)
                    alone(dve)
                    nc.vector.bn_aggr(two_[t.half][:, 0:2], six[t.half][:]).then_inc(stats_done, 1)

                def step(k):
                    t = k + 1
                    if t.within(NT):
                        stats(t, x_t, x_in, xs6, x_raw, xs, x_stats, x_norm)
                    if not k.within(NT):
                        return
                    stats(k, xg, xg_in, gs6, g_raw, gs, g_stats, g_norm)
                    b, column = k.half, bass.ds(k.n, 1)
                    dve.wait_ge(dr_in[b], k.landed)
                    dve.wait_ge(sums, k.freed)
                    dve.wait_ge(scattered[b], k.landed_before)
                    nc.vector.tensor_scalar(same[b][:], dst_row[b][:], dst_f[:, column], 0.0, ALU.is_equal, ALU.add,
                                            accum_out=sum_sb[b][:, D:D + 1]).then_inc(same_ready, 1)
                    dve.wait_ge(same_ready, k.done)
                    nc.vector.tensor_tensor_reduce(out=prior[:], in0=same[b][:], in1=before[:], scale=1.0, scalar=0.0,
                                                   op0=ALU.mult, op1=ALU.add, accum_out=n_prior[b][:]).then_inc(earlier, 1)
                    dve.wait_ge(earlier, k.done)
                    nc.vector.tensor_scalar(moved[b][:], n_prior[b][:], 1.0, to_trash[:, column], ALU.min, ALU.mult).then_inc(idx_step, 1)
                    dve.wait_ge(idx_step, k.done)
                    nc.vector.tensor_tensor(dst_idx[b][:], moved[b][:], dst_f[:, column], ALU.add).then_inc(idx_ready, 1)
                    dve.wait_ge(g_norm, k.done)
                    dve.wait_ge(ea_in[b], k.landed)
                    nc.vector.tensor_tensor(msg[b][:], msg[b][:], ea[b][:], ALU.add).then_inc(msg_ready, 1)
                    dve.wait_ge(left, k.done)
                    nc.vector.tensor_tensor(node_slot(k), ps_left[b][:], bu_sb[:], ALU.add).then_inc(left_sb, 1)

                for_tiles(dve, NT, 1, 1, step)

            @block.tensor
            def _(pe):
                credit(pe, x_turned, left, sums)
                pe.wait_ge(w1_in, 64)

                def step(k):
                    b = k.half
                    if k.within(NT):
                        pe.wait_ge(x_turned_sb, k.done)
                        pe.wait_ge(left_sb, k.freed)
                        for c in range(DC):
                            mm = nc.tensor.matmul(ps_left[b][:], xT[b][:, c * P:(c + 1) * P], wul_sb[:, c, :],
                                                  start=(c == 0), stop=(c == DC - 1))
                        mm.then_inc(left, 1)
                    t = k + 1
                    if t.within(NT):
                        pe.wait_ge(x_norm, t.done)
                        pe.wait_ge(x_turned_sb, t.freed)
                        for c in range(DC):
                            mm = nc.tensor.transpose(ps_turn[t.half][:, c * P:(c + 1) * P], xn[t.half][:, c * P:(c + 1) * P], ident[:])
                        mm.then_inc(x_turned, 1)
                    if k.within(NT):
                        pe.wait_ge(msg_ready, k.done)
                        pe.wait_ge(same_ready, k.done)
                        pe.wait_ge(sums_sb, k.freed)
                        nc.tensor.matmul(ps_sum[b][:], same[b][:], msg[b][:], start=True, stop=True).then_inc(sums, 1)

                for_tiles(pe, NT, 1, 0, step)

        c2_in = sem("c2_in")
        ag_in, y_in, xr_in = pair_of("ag_in"), pair_of("y_in"), pair_of("xr_in")
        table_stored, hidden_stored, logit_stored = pair_of("table_stored"), pair_of("hidden_stored"), pair_of("logit_stored")
        ag_turned, ag_turned_sb, upd = sem("ag_turned"), sem("ag_turned_sb"), sem("upd")
        deg_max, deg_inv, has_edge, bias_part, left_biased = sem("deg_max"), sem("deg_inv"), sem("has_edge"), sem("bias_part"), sem("left_biased")
        y_raw, y_stats, y_eps, y_pow, y_rstd, y_norm = [sem(f"y_{s}") for s in ("raw", "stats", "eps", "pow", "rstd", "norm")]
        o_raw, o_stats, o_eps, o_pow, o_rstd = [sem(f"o_{s}") for s in ("raw", "stats", "eps", "pow", "rstd")]
        z_raw, z_stats, z_eps, z_pow, z_rstd = [sem(f"z_{s}") for s in ("raw", "stats", "eps", "pow", "rstd")]
        u_ready, u_gelu, o_ready, o_gamma, x1_ready, res_ready = [sem(s) for s in ("u_ready", "u_gelu", "o_ready", "o_gamma", "x1_ready", "res_ready")]
        z_norm, z_turned, z_turned_sb, hidden, logits, hidden_sb, logit_sb = [
            sem(s) for s in ("z_norm", "z_turned", "z_turned_sb", "hidden", "logits", "hidden_sb", "logit_sb")]

        with ExitStack() as scope, nc.Block() as block:
            def two(name, shape, dt=F32):
                return [sb(f"{name}{b}", shape, dt, scope) for b in range(2)]

            fused_sb = sb("fused_sb", [P, DC, D], scope=scope)
            fused_b_sb, gamma_sb, beta_sb = [sb(n, [P, D], scope=scope) for n in ("fused_b_sb", "gamma_sb", "beta_sb")]
            sw1_sb = sb("sw1_sb", [P, DC, H], scope=scope)
            gate_sb = sb("gate_sb", [P, DC, E], scope=scope)
            ag, agT = two("ag", [P, AW]), two("agT", [P, D])
            y_t, yn, res = two("y_t", [P, D]), two("yn", [P, D]), two("res", [P, D])
            upd_sb, z, zT = two("upd_sb", [P, D]), two("z", [P, D]), sb("zT", [P, D], scope=scope)
            bias_sb = sb("bias_sb", [P, D], scope=scope)
            deg = two("deg", [P, 3])
            ys6, os6, zs6 = two("ys6", [P, 6]), two("os6", [P, 6]), two("zs6", [P, 6])
            ys, os_, zs = two("ys", [P, 5]), two("os_", [P, 5]), two("zs", [P, 5])
            hid = two("hid", [H, P])
            lg = two("lg", [P, E])
            ps_agT, ps_upd, ps_zT, ps_hidden, ps_logits = bank[0:2], bank[2:4], bank[4], bank[5], bank[6:8]

            @block.sync
            def _(sp):
                sp.dma_start(fused_sb[:].rearrange("p c n -> p (c n)"), fused_w_d).then_inc(c2_in, 16)
                sp.dma_start(fused_b_sb[:], fused_b_d).then_inc(c2_in, 16)
                sp.dma_start(gamma_sb[:], gamma.partition_broadcast(P)).then_inc(c2_in, 16)
                sp.dma_start(beta_sb[:], beta.partition_broadcast(P)).then_inc(c2_in, 16)
                sp.dma_start(sw1_sb[:], sw1.rearrange("(c p) n -> p c n", p=P)).then_inc(c2_in, 16)
                sp.dma_start(gate_sb[:], gate.rearrange("(c p) n -> p c n", p=P)).then_inc(c2_in, 16)

                def step(k):
                    t = k + 2
                    if t.within(NT):
                        last = t.static and t.n == NT - 1
                        r = TAIL if last else P
                        sp.wait_ge(ag_turned, t.freed)
                        sp.wait_ge(deg_max, t.freed)
                        sp.wait_ge(has_edge, t.freed)
                        sp.dma_start(ag[t.half][:], agg[bass.ds(t.n * P, P), :]).then_inc(ag_in[t.half], 16)
                        sp.wait_ge(y_norm, t.freed)
                        sp.dma_start(y_t[t.half][0:r, :], rows(x, t, last)).then_inc(y_in[t.half], 16)
                    t = k
                    if t.within(NT):
                        last = t.static and t.n == NT - 1
                        r = TAIL if last else P
                        sp.wait_ge(x1_ready, t.freed)
                        sp.dma_start(res[t.half][0:r, :], rows(x, t, last)).then_inc(xr_in[t.half], 16)
                    t = k + -3
                    if t.within(NT):
                        sp.wait_ge(z_norm, t.done)
                        sp.dma_start(table[bass.ds(t.n * P, P), 0:D], z[t.half][:]).then_inc(table_stored[t.half], 16)
                    t = k + -4
                    if t.within(NT):
                        sp.wait_ge(hidden_sb, t.done)
                        alone(sp)
                        sp.dma_start(hidden_d[:, bass.ds(t.n * P, P)], hid[t.half][:]).then_inc(hidden_stored[t.half], 16)
                        sp.wait_ge(logit_sb, t.done)
                        sp.dma_start(logit_d[:, bass.ds(t.n * E, E)], lg[t.half][:]).then_inc(logit_stored[t.half], 16)

                for_tiles(sp, NT, 2, 4, step)
                for t in (At((NT - 2) // 2, (NT - 2) % 2), At((NT - 1) // 2, (NT - 1) % 2)):
                    for s in (table_stored, hidden_stored, logit_stored):
                        sp.wait_ge(s[t.half], t.landed)

            @block.gpsimd
            def _(pool):
                credit(pool, has_edge, bias_part, left_biased, y_eps, y_pow, y_rstd, o_eps, o_pow, o_rstd,
                       z_eps, z_pow, z_rstd, res_ready)
                pool.wait_ge(c2_in, 96)

                def step(k):
                    if k.within(NT):
                        b = k.half
                        pool.wait_ge(ag_in[b], k.landed)
                        alone(pool)
                        nc.gpsimd.tensor_scalar(deg[b][:, 2:3], ag[b][:, D:D + 1], 1.0, None, ALU.min).then_inc(has_edge, 1)
                        pool.wait_ge(has_edge, k.done)
                        alone(pool)
                        nc.gpsimd.tensor_scalar(bias_sb[:], fused_b_sb[:], deg[b][:, 2:3], None, ALU.mult).then_inc(bias_part, 1)
                        pool.wait_ge(bias_part, k.done)
                        nc.gpsimd.tensor_tensor(node_slot(k), node_slot(k), bias_sb[:], ALU.add).then_inc(left_biased, 1)
                    t = k + -1
                    if t.within(NT):
                        b = t.half
                        pool.wait_ge(xr_in[b], t.landed)
                        nc.gpsimd.tensor_tensor(res[b][:], res[b][:], beta_sb[:], ALU.add).then_inc(res_ready, 1)
                    if (k + 1).within(NT):
                        rstd_on_pool(pool, k + 1, ys[(k + 1).half], y_stats, y_eps, y_pow, y_rstd)
                    if (k + -1).within(NT):
                        rstd_on_pool(pool, k + -1, os_[(k + -1).half], o_stats, o_eps, o_pow, o_rstd)
                    if (k + -2).within(NT):
                        rstd_on_pool(pool, k + -2, zs[(k + -2).half], z_stats, z_eps, z_pow, z_rstd)

                for_tiles(pool, NT, 1, 2, step)

            @block.scalar
            def _(act):
                credit(act, y_norm, u_gelu, ag_turned_sb, z_norm, z_turned_sb, hidden_sb)

                def step(k):
                    t = k + -3
                    if t.within(NT):
                        act.wait_ge(z_turned, t.done)
                        act.wait_ge(hidden, t.done - 1)
                        act.wait_ge(logits, t.done - 1)
                        nc.scalar.copy(zT[:], ps_zT[:]).then_inc(z_turned_sb, 1)
                    t = k + -1
                    if t.within(NT):
                        act.wait_ge(u_ready, t.done)
                        nc.scalar.activation(upd_sb[t.half][:], upd_sb[t.half][:], ACT.Gelu).then_inc(u_gelu, 1)
                    t = k + 1
                    if t.within(NT):
                        act.wait_ge(ag_turned, t.done)
                        act.wait_ge(upd, t.freed)
                        nc.scalar.copy(agT[t.half][:], ps_agT[t.half][:]).then_inc(ag_turned_sb, 1)
                        act.wait_ge(y_rstd, t.done)
                        act.wait_ge(o_ready, t.freed)
                        nc.scalar.activation(yn[t.half][:], y_t[t.half][:], ACT.Identity, bias=ys[t.half][:, 4:5],
                                             scale=ys[t.half][:, 3:4]).then_inc(y_norm, 1)
                    t = k + -2
                    if t.within(NT):
                        act.wait_ge(z_rstd, t.done)
                        act.wait_ge(z_turned, t.freed)
                        act.wait_ge(table_stored[t.half], t.landed_before)
                        nc.scalar.activation(z[t.half][:], node_slot(t), ACT.Identity, bias=zs[t.half][:, 4:5],
                                             scale=zs[t.half][:, 3:4]).then_inc(z_norm, 1)
                    t = k + -3
                    if t.within(NT):
                        act.wait_ge(hidden, t.done)
                        act.wait_ge(hidden_stored[t.half], t.landed_before)
                        nc.scalar.copy(hid[t.half][:], ps_hidden[0:H, 0:P]).then_inc(hidden_sb, 1)

                for_tiles(act, NT, 1, 3, step)

            @block.vector
            def _(dve):
                credit(dve, y_raw, y_stats, o_raw, o_stats, z_raw, z_stats, deg_max, deg_inv, u_ready, o_ready,
                       o_gamma, x1_ready, logit_sb)
                dve.wait_ge(c2_in, 96)

                def stats(t, data, six, raw, two_, stats_done, free):
                    alone(dve)
                    nc.vector.bn_stats(six[t.half][:], data).then_inc(raw, 1)
                    dve.wait_ge(raw, t.done)
                    dve.wait_ge(free, t.freed)
                    alone(dve)
                    nc.vector.bn_aggr(two_[t.half][:, 0:2], six[t.half][:]).then_inc(stats_done, 1)

                def step(k):
                    t = k + -1
                    if t.within(NT):
                        b = t.half
                        dve.wait_ge(upd, t.done)
                        dve.wait_ge(left_biased, t.done)
                        dve.wait_ge(deg_inv, t.done)
                        dve.wait_ge(x1_ready, t.freed)
                        nc.vector.scalar_tensor_tensor(upd_sb[b][:], ps_upd[b][:], deg[b][:, 1:2], node_slot(t),
                                                       ALU.mult, ALU.add).then_inc(u_ready, 1)
                    t = k + -2
                    if t.within(NT):
                        b = t.half
                        dve.wait_ge(o_rstd, t.done)
                        nc.vector.scalar_tensor_tensor(upd_sb[b][:], upd_sb[b][:], os_[b][:, 0:1], gamma_sb[:],
                                                       ALU.subtract, ALU.mult).then_inc(o_gamma, 1)
                        dve.wait_ge(o_gamma, t.done)
                        dve.wait_ge(res_ready, t.done)
                        nc.vector.scalar_tensor_tensor(node_slot(t), upd_sb[b][:], os_[b][:, 3:4], res[b][:],
                                                       ALU.mult, ALU.add).then_inc(x1_ready, 1)
                    t = k + -1
                    if t.within(NT):
                        dve.wait_ge(u_gelu, t.done)
                        dve.wait_ge(y_norm, t.done)
                        nc.vector.tensor_tensor(upd_sb[t.half][:], upd_sb[t.half][:], yn[t.half][:], ALU.add).then_inc(o_ready, 1)
                    t = k + 1
                    if t.within(NT):
                        dve.wait_ge(y_in[t.half], t.landed)
                        stats(t, y_t[t.half][:], ys6, y_raw, ys, y_stats, y_norm)
                        dve.wait_ge(ag_in[t.half], t.landed)
                        dve.wait_ge(u_ready, t.freed)
                        nc.vector.tensor_scalar(deg[t.half][:, 0:1], ag[t.half][:, D:D + 1], 1.0, None, ALU.max).then_inc(deg_max, 1)
                    t = k + -1
                    if t.within(NT):
                        dve.wait_ge(o_ready, t.done)
                        stats(t, upd_sb[t.half][:], os6, o_raw, os_, o_stats, x1_ready)
                    t = k + 1
                    if t.within(NT):
                        dve.wait_ge(deg_max, t.done)
                        nc.vector.reciprocal(deg[t.half][:, 1:2], deg[t.half][:, 0:1]).then_inc(deg_inv, 1)
                    t = k + -2
                    if t.within(NT):
                        dve.wait_ge(x1_ready, t.done)
                        stats(t, node_slot(t), zs6, z_raw, zs, z_stats, z_norm)
                    t = k + -4
                    if t.within(NT):
                        dve.wait_ge(logits, t.done)
                        dve.wait_ge(logit_stored[t.half], t.landed_before)
                        nc.vector.tensor_copy(lg[t.half][:], ps_logits[t.half][:, 0:E]).then_inc(logit_sb, 1)

                for_tiles(dve, NT, 1, 4, step)

            @block.tensor
            def _(pe):
                credit(pe, ag_turned, upd, z_turned, hidden, logits)
                pe.wait_ge(c2_in, 96)

                def step(k):
                    t = k + -3
                    if t.within(NT):
                        pe.wait_ge(z_norm, t.done)
                        pe.wait_ge(z_turned_sb, t.done - 1)
                        for c in range(DC):
                            mm = nc.tensor.transpose(ps_zT[:, c * P:(c + 1) * P], z[t.half][:, c * P:(c + 1) * P], ident[:])
                        mm.then_inc(z_turned, 1)
                    if k.within(NT):
                        b = k.half
                        pe.wait_ge(ag_turned_sb, k.done)
                        pe.wait_ge(u_ready, k.freed)
                        for c in range(DC):
                            mm = nc.tensor.matmul(ps_upd[b][:], agT[b][:, c * P:(c + 1) * P], fused_sb[:, c, :],
                                                  start=(c == 0), stop=(c == DC - 1))
                        mm.then_inc(upd, 1)
                    t = k + 1
                    if t.within(NT):
                        pe.wait_ge(ag_in[t.half], t.landed)
                        pe.wait_ge(ag_turned_sb, t.freed)
                        for c in range(DC):
                            mm = nc.tensor.transpose(ps_agT[t.half][:, c * P:(c + 1) * P], ag[t.half][:, c * P:(c + 1) * P], ident[:])
                        mm.then_inc(ag_turned, 1)
                    t = k + -3
                    if t.within(NT):
                        b = t.half
                        pe.wait_ge(z_turned_sb, t.done)
                        pe.wait_ge(hidden_sb, t.done - 1)
                        for c in range(DC):
                            mm = nc.tensor.matmul(ps_hidden[0:H, 0:P], sw1_sb[:, c, :], zT[:, c * P:(c + 1) * P],
                                                  start=(c == 0), stop=(c == DC - 1))
                        mm.then_inc(hidden, 1)
                        pe.wait_ge(logit_sb, t.freed)
                        for c in range(DC):
                            mm = nc.tensor.matmul(ps_logits[b][:, 0:E], zT[:, c * P:(c + 1) * P], gate_sb[:, c, :],
                                                  start=(c == 0), stop=(c == DC - 1))
                        mm.then_inc(logits, 1)

                for_tiles(pe, NT, 1, 3, step)

        BITS = 30
        PER_BIT = 3
        LOOPED = (NT - 1) // PER_BIT
        assert LOOPED * PER_BIT == NT - 1 and LOOPED < BITS
        c3_in, h_in, prob_stored, search_in = sem("c3_in"), [sem(f"h_in{j}") for j in range(PER_BIT)], sem("prob_stored"), sem("search_in")
        p3_pool, p3_dve, p3_act, p3_pe = sem("p3_pool"), sem("p3_dve"), sem("p3_act"), sem("p3_pe")
        cand_ready, count_ready, total_ready, keep_ready, bit_ready, kth_ready = [
            sem(s) for s in ("cand_ready", "count_ready", "total_ready", "keep_ready", "bit_ready", "kth_ready")]
        h_gelu, shared, out_ready, out_stored = sem("h_gelu"), sem("shared"), sem("out_ready"), sem("out_stored")
        rank_stored, ends_stored = sem("rank_stored"), sem("ends_stored")
        fin_dve, fin_pe = sem("fin_dve"), sem("fin_pe")

        with ExitStack() as scope, nc.Block() as block:
            lg = sb("lg3", [P, NT, E], scope=scope)
            prob = sb("prob", [P, (NT + 7) // 8 * 8, E], scope=scope)
            stat = sb("stat", [P, NT], scope=scope)
            turned = sb("turned", [P, (NT + 7) // 8, P], scope=scope)
            same_e = sb("same_e", [P, P], scope=scope)
            earlier_c = sb("earlier_c", [P, P], scope=scope)
            search = sb("search", [P, CL], scope=scope)
            hits = sb("hits", [P, CL], scope=scope)
            ties = sb("ties", [P, CL], scope=scope)
            one = sb("one", [P, 1], scope=scope)
            cand, kth, bit, keep = [sb(n, [P, 1], I32, scope) for n in ("cand", "kth", "bit", "keep")]
            count, n_gt, need = [sb(n, [P, 1], scope=scope) for n in ("count", "n_gt", "need")]
            ends = sb("ends", [P, RQ], scope=scope)
            sw2_sb = sb("sw2_sb", [H + 1, D], scope=scope)
            sb1_sb = sb("sb1_sb", [H, 1], scope=scope)
            hid = [sb(f"hid3{j}", [H + 1, P], scope=scope) for j in range(PER_BIT)]
            BLOCKS = (NT + 7) // 8
            ps_turn, ps_shared, ps_count = bank[0:2], bank[2:5], bank[5]

            def out_rows(n, last):
                return out[(NT - 1) * P:N, :] if last else out[bass.ds(n * P, P), :]

            def block_tiles(b):
                return min(8, NT - 8 * b)

            @block.sync
            def _(sp):
                sp.dma_start(lg[:].rearrange("p t e -> p (t e)"), logit_d).then_inc(c3_in, 16)
                sp.dma_start(sw2_sb[0:H, :], sw2).then_inc(c3_in, 16)
                sp.dma_start(sw2_sb[H:H + 1, :], sb2).then_inc(c3_in, 16)
                sp.dma_start(sb1_sb[:], sb1).then_inc(c3_in, 16)
                for b in range(BLOCKS):
                    sp.wait_ge(p3_act, b + 2)
                    for t in range(block_tiles(b)):
                        col = (8 * b + t) * P
                        sp.dma_start(prob_d[:, col:col + P], turned[t * E:(t + 1) * E, b, :]).then_inc(prob_stored, 16)
                sp.wait_ge(prob_stored, 16 * NT)
                sp.dma_start(search[:], prob_d.rearrange("e (c l) -> (e c) l", c=CH)).then_inc(search_in, 16)
                sp.dma_start(table.rearrange("(t p) w -> p t w", p=P)[:, :, D:TW], prob[:, 0:NT, :]).then_inc(prob_stored, 16)

                def tiles(i, js):
                    for j in js:
                        n = i * PER_BIT + j
                        sp.wait_ge(shared, n + 1)
                        sp.dma_start(hid[j][0:H, :], hidden_d[:, bass.ds(n * P, P)]).then_inc(h_in[j], 16)
                    for j in js:
                        n = i * PER_BIT + j
                        last = isinstance(n, int) and n == NT - 1
                        sp.wait_ge(out_ready, n + PER_BIT + 1)
                        sp.dma_start(out_rows(n, last), nodes[0:TAIL if last else P, bass.ds(n * D, D)]).then_inc(out_stored, 16)

                with sp.Fori(0, LOOPED) as i:
                    tiles(i, range(PER_BIT))
                tiles(LOOPED, [0])
                sp.wait_ge(fin_dve, 12)
                sp.dma_start(rank_d.rearrange("(r q) l -> r (q l)", r=P), ties[:]).then_inc(rank_stored, 16)
                sp.dma_start(ends_d.rearrange("a (r q) -> (a r) q", r=P), ends[:]).then_inc(ends_stored, 16)
                sp.wait_ge(prob_stored, 16 * (NT + 1))
                sp.wait_ge(out_stored, 16 * NT)
                sp.wait_ge(rank_stored, 16)
                sp.wait_ge(ends_stored, 16)

            @block.gpsimd
            def _(pool):
                nc.gpsimd.memset(same_e[:], 1.0).then_inc(p3_pool, 1)
                pool.wait_ge(p3_pool, 1)
                view = same_e[:].rearrange("p (e c) -> p e c", c=CH)
                nc.gpsimd.affine_select(out=view, in_=view, compare_op=ALU.is_ge, fill=0.0, base=0,
                                        pattern=[[-CH, E], [0, CH]], channel_multiplier=1).then_inc(p3_pool, 1)
                pool.wait_ge(p3_pool, 2)
                nc.gpsimd.affine_select(out=view, in_=view, compare_op=ALU.is_ge, fill=0.0, base=CH - 1,
                                        pattern=[[CH, E], [0, CH]], channel_multiplier=-1).then_inc(p3_pool, 1)
                pool.wait_ge(p3_pool, 3)
                nc.gpsimd.affine_select(out=earlier_c[:], in_=same_e[:], compare_op=ALU.is_gt, fill=0.0, base=0,
                                        pattern=[[1, P]], channel_multiplier=-1).then_inc(p3_pool, 1)
                pool.wait_ge(p3_dve, 5)
                nc.gpsimd.affine_select(out=prob[:, NT - 1, :], in_=prob[:, NT - 1, :], compare_op=ALU.is_ge, fill=-1.0,
                                        base=TAIL - 1, pattern=[[0, E]], channel_multiplier=-1).then_inc(p3_pool, 1)

            @block.scalar
            def _(act):
                act.wait_ge(p3_dve, 2)
                nc.scalar.activation(prob[:, 0:NT, :], lg[:], ACT.Exp).then_inc(p3_act, 1)
                for b in range(BLOCKS):
                    act.wait_ge(p3_pe, b + 1)
                    nc.scalar.copy(turned[:, b, :], ps_turn[b % 2][:, 0:P]).then_inc(p3_act, 1)

                def tiles(i, js):
                    for j in js:
                        act.wait_ge(h_in[j], i * 16 + 16)
                        act.activation(hid[j][0:H, :], hid[j][0:H, :], ACT.Gelu_apprx_tanh, bias=sb1_sb[:]).then_inc(h_gelu, 1)

                with act.Fori(0, LOOPED) as i:
                    tiles(i, range(PER_BIT))
                tiles(LOOPED, [0])

            @block.vector
            def _(dve):
                dve.sem_inc(out_ready, PER_BIT)
                for s in (kth_ready, bit_ready, keep_ready):
                    dve.sem_inc(s, 1)
                step = [0]

                def chain(ins, s=p3_dve):
                    step[0] += 1
                    ins.then_inc(s, 1)
                    dve.wait_ge(s, step[0])

                for h in hid:
                    nc.vector.memset(h[H:H + 1, :], 1.0)
                nc.vector.memset(one[:], 1.0)
                nc.vector.memset(kth[:], 0)
                nc.vector.memset(bit[:], 1 << (BITS - 1))
                nc.vector.memset(prob[:, NT:, :], -1.0)
                dve.wait_ge(c3_in, 64)
                nc.vector.memset(keep[:], 0)
                chain(nc.vector.tensor_reduce(stat[:], lg[:], AX_X, ALU.max))
                chain(nc.vector.tensor_tensor(lg[:], lg[:], stat[:].unsqueeze(2).to_broadcast([P, NT, E]), ALU.subtract))
                dve.wait_ge(p3_act, 1)
                chain(nc.vector.tensor_reduce(stat[:], prob[:, 0:NT, :], AX_X, ALU.add))
                chain(nc.vector.reciprocal(stat[:], stat[:]))
                chain(nc.vector.tensor_tensor(prob[:, 0:NT, :], prob[:, 0:NT, :], stat[:].unsqueeze(2).to_broadcast([P, NT, E]), ALU.mult))
                dve.wait_ge(search_in, 16)

                def search_step(n):
                    dve.wait_ge(kth_ready, n + 1)
                    dve.wait_ge(bit_ready, n + 1)
                    nc.vector.tensor_tensor(cand[:], kth[:], bit[:], ALU.bitwise_or).then_inc(cand_ready, 1)
                    dve.wait_ge(cand_ready, n + 1)
                    dve.wait_ge(total_ready, n + 1)
                    nc.vector.tensor_scalar(hits[:], search[:], cand[:].bitcast(F32), 0.0, ALU.is_ge, ALU.add,
                                            accum_out=count[:]).then_inc(count_ready, 1)
                    dve.wait_ge(total_ready, n + 2)
                    nc.vector.tensor_scalar(keep[:], ps_count[:, 0:1], CAP - 0.5, None, ALU.is_ge).then_inc(keep_ready, 1)
                    dve.wait_ge(keep_ready, n + 2)
                    alone(dve)
                    nc.vector.copy_predicated(kth[:], keep[:], cand[:]).then_inc(kth_ready, 1)
                    nc.vector.tensor_scalar(bit[:], bit[:], 1, None, ALU.logical_shift_right).then_inc(bit_ready, 1)

                def tiles(i, js):
                    for j in js:
                        n = i * PER_BIT + j
                        dve.wait_ge(shared, n + PER_BIT + 1)
                        slot = nodes[:, bass.ds(n * D, D)]
                        nc.vector.tensor_tensor(slot, slot, ps_shared[j][:], ALU.add).then_inc(out_ready, 1)

                with dve.Fori(0, LOOPED) as i:
                    search_step(i)
                    tiles(i, range(PER_BIT))
                tiles(LOOPED, [0])
                for n in range(LOOPED, BITS):
                    search_step(n)
                dve.wait_ge(kth_ready, BITS + 1)
                step[0] = 0
                kth_f = kth[:].bitcast(F32)

                def fin(ins):
                    chain(ins, fin_dve)

                def scan(out_, in_, start):
                    return nc.vector.tensor_tensor_scan(out_, one[:].to_broadcast([P, CL]), in_, start, ALU.mult, ALU.add)

                fin(nc.vector.tensor_scalar(hits[:], search[:], kth_f, 0.0, ALU.is_gt, ALU.add, accum_out=n_gt[:]))
                fin(nc.vector.tensor_scalar(search[:], search[:], kth_f, None, ALU.is_equal))
                fin(scan(ties[:], search[:], 0.0))
                fin(nc.vector.tensor_copy(count[:], ties[:, CL - 1:CL]))
                dve.wait_ge(fin_pe, 2)
                fin(nc.vector.tensor_scalar(need[:], ps_count[:, 4:5], -1.0, float(CAP), ALU.mult, ALU.add))
                fin(nc.vector.tensor_tensor(need[:], need[:], ps_count[:, 8:9], ALU.subtract))
                fin(nc.vector.scalar_tensor_tensor(search[:], ties[:], need[:], search[:], ALU.is_le, ALU.mult))
                fin(nc.vector.tensor_tensor(hits[:], hits[:], search[:], ALU.add))
                fin(nc.vector.tensor_reduce(count[:], hits[:], AX_X, ALU.add))
                dve.wait_ge(fin_pe, 3)
                fin(nc.vector.tensor_copy(need[:], ps_count[:, 12:13]))
                fin(scan(ties[:], hits[:], need[:]))
                fin(nc.vector.tensor_copy(ends[:], ties[:].rearrange("p (q l) -> p q l", q=RQ)[:, :, RL - 1]))

            @block.tensor
            def _(pe):
                pe.sem_inc(shared, PER_BIT)
                pe.sem_inc(total_ready, 1)
                pe.wait_ge(p3_pool, 5)
                for b in range(BLOCKS):
                    if b >= 2:
                        pe.wait_ge(p3_act, b)
                    nc.tensor.transpose(ps_turn[b % 2][:, 0:P], prob[:, 8 * b:8 * b + 8, :].rearrange("p t e -> p (t e)"),
                                        ident[:]).then_inc(p3_pe, 1)
                pe.wait_ge(c3_in, 64)

                def total(n):
                    pe.wait_ge(count_ready, n + 1)
                    pe.wait_ge(keep_ready, n + 1)
                    nc.tensor.matmul(ps_count[:, 0:1], same_e[:], count[:], start=True, stop=True).then_inc(total_ready, 1)

                def tiles(i, js):
                    for j in js:
                        n = i * PER_BIT + j
                        pe.wait_ge(h_gelu, n + 1)
                        pe.wait_ge(out_ready, n + 1)
                        nc.tensor.matmul(ps_shared[j][:], hid[j][:], sw2_sb[:], start=True, stop=True).then_inc(shared, 1)

                with pe.Fori(0, LOOPED) as i:
                    tiles(i, range(PER_BIT))
                    total(i)
                tiles(LOOPED, [0])
                for n in range(LOOPED, BITS):
                    total(n)
                pe.wait_ge(fin_dve, 4)
                pe.wait_ge(keep_ready, BITS + 1)
                nc.tensor.matmul(ps_count[:, 4:5], same_e[:], n_gt[:], start=True, stop=True).then_inc(fin_pe, 1)
                nc.tensor.matmul(ps_count[:, 8:9], earlier_c[:], count[:], start=True, stop=True).then_inc(fin_pe, 1)
                pe.wait_ge(fin_dve, 9)
                nc.tensor.matmul(ps_count[:, 12:13], earlier_c[:], count[:], start=True, stop=True).then_inc(fin_pe, 1)

        nodes_scope.close()
        c4_in, c4_pool = sem("c4_in"), sem("c4_pool")
        we_in, rank_in, tok_in, added = pair_of("we_in"), pair_of("rank_in"), pair_of("tok_in"), pair_of("added")
        row_cmp, row_sum, row_idx_ready, tok_cmp, tok_sum, tok_idx_ready, add_idx_ready, score_ready = [
            sem(s) for s in ("row_cmp", "row_sum", "row_idx_ready", "tok_cmp", "tok_sum", "tok_idx_ready", "add_idx_ready", "score_ready")]
        e_turned, e_turned_sb, e_hidden, e_gelu, e_out, e_scaled = [
            sem(s) for s in ("e_turned", "e_turned_sb", "e_hidden", "e_gelu", "e_out", "e_scaled")]
        G = SLOT_G
        NA = D // SLOT_P * SLOT_P
        NA = min(NA, CAP - SLOT_P)

        class Item:

            def __init__(self, k, g):
                self.half = (k.half * G + g) % 2
                self.done = k.n * G + (g + 1 + 2 * G)
                self.freed = k.n * G + (g - 1 + 2 * G)
                self.expert_freed = k.n * G + G

        def all_landed(k):
            return (k.pair + 1) * (16 * G)

        def all_landed_before(k):
            return k.pair * (16 * G)

        with ExitStack() as scope, nc.Block() as block:
            def two(name, shape, dt=F32):
                return [sb(f"{name}{b}", shape, dt, scope) for b in range(2)]

            ends_all = sb("ends_all", [SLOT_P, E * RR], scope=scope)
            slot = sb("slot", [SLOT_P, G], scope=scope)
            first_row = sb("first_row", [SLOT_P, E], scope=scope)
            cmp_row = sb("cmp_row", [SLOT_P, G, RR], scope=scope)
            cmp_tok = sb("cmp_tok", [SLOT_P, G, RL], scope=scope)
            n_row, n_tok = two("n_row", [SLOT_P, G]), two("n_tok", [SLOT_P, G])
            row_idx, tok_idx, add_idx = two("row_idx", [SLOT_P, G], I32), two("tok_idx", [SLOT_P, G], I32), two("add_idx", [SLOT_P, G], I32)
            ranks, toks, score = two("ranks", [SLOT_P, G, RL]), two("toks", [SLOT_P, G, TW]), two("score", [SLOT_P, G])
            w1_sb, w2_sb, b1_sb = two("w1_sb", [P, DC, H]), two("w2_sb", [H + 1, D]), two("b1_sb", [H, 1])
            tokT, hT, y = two("tokT", [P, DC, CAP]), two("hT", [H + 1, CAP]), two("y", [SLOT_P, G, D])
            ps_turn, ps_hid, ps_out = bank[0:2], bank[2:4], bank[4:6]

            @block.sync
            def _(sp):
                sp.dma_start(ends_all[:], ends_d.rearrange("a n -> (a n)").partition_broadcast(SLOT_P)).then_inc(c4_in, 16)

                def weights(k):
                    b, e = k.half, bass.ds(k.n, 1)
                    sp.wait_ge(e_out, Item(k, 0).expert_freed)
                    sp.dma_start(w1_sb[b][:], w1[e].rearrange("a (c p) h -> p (a c) h", p=P)).then_inc(we_in[b], 16)
                    sp.dma_start(w2_sb[b][0:H, :], w2[e].rearrange("a h n -> (a h) n")).then_inc(we_in[b], 16)
                    sp.dma_start(w2_sb[b][H:H + 1, :], b2[e, :]).then_inc(we_in[b], 16)
                    sp.dma_start(b1_sb[b][:], b1[e].rearrange("a h o -> (a h) o")).then_inc(we_in[b], 16)

                for_tiles(sp, E, 0, 1, lambda k: weights(k) if k.within(E) else None)

            @block.gpsimd
            def _(pool):
                nc.gpsimd.iota(slot[:], pattern=[[SLOT_P, G]], base=0, channel_multiplier=1,
                               allow_small_or_imprecise_dtypes=True).then_inc(c4_pool, 1)
                nc.gpsimd.iota(first_row[:], pattern=[[RR, E]], base=0, channel_multiplier=0,
                               allow_small_or_imprecise_dtypes=True).then_inc(c4_pool, 1)

                def step(k):
                    t = k + 2
                    if t.within(E):
                        b = t.half
                        pool.wait_ge(tok_idx_ready, t.done)
                        pool.wait_ge(e_turned, Item(t, 0).expert_freed)
                        pool.wait_ge(score_ready, t.freed)
                        alone(pool)
                        for g in range(G):
                            nc.gpsimd.indirect_dma_start(
                                toks[b][:, g, :], None, table, bass.IndirectOffsetOnAxis(tok_idx[b][:, g:g + 1], 0),
                            ).then_inc(tok_in[b], 16)
                    t = k + 3
                    if t.within(E):
                        b = t.half
                        pool.wait_ge(row_idx_ready, t.done)
                        alone(pool)
                        for g in range(G):
                            nc.gpsimd.indirect_dma_start(
                                ranks[b][:, g, :], None, rank_d, bass.IndirectOffsetOnAxis(row_idx[b][:, g:g + 1], 0),
                            ).then_inc(rank_in[b], 16)
                    if k.within(E):
                        b = k.half
                        pool.wait_ge(e_scaled, Item(k, G - 1).done)
                        pool.wait_ge(add_idx_ready, k.done)
                        t = k + -1
                        if not (k.static and k.n == 0):
                            pool.wait_ge(added[t.half], all_landed(t))
                        alone(pool)
                        for g in range(G):
                            nc.gpsimd.indirect_dma_start(
                                out, bass.IndirectOffsetOnAxis(add_idx[b][:, g:g + 1], 0), y[b][:, g, :], None,
                                compute_op=ALU.add).then_inc(added[b], 16)

                for_tiles(pool, E, 3, 1, step)
                for t in (At((E - 2) // 2, (E - 2) % 2), At((E - 1) // 2, (E - 1) % 2)):
                    pool.wait_ge(added[t.half], all_landed(t))

            @block.scalar
            def _(act):
                act.sem_inc(e_turned_sb, 2 * G)
                credit(act, e_gelu)

                def step(k):
                    if k.within(E):
                        b = k.half
                        act.wait_ge(we_in[b], (k.pair + 1) * 64)
                        act.wait_ge(e_hidden, k.done)
                        act.wait_ge(e_out, Item(k, 0).expert_freed)
                        nc.scalar.activation(hT[b][0:H, 0:NA], ps_hid[0][0:H, 0:NA], ACT.Gelu_apprx_tanh, bias=b1_sb[b][:])
                        nc.scalar.activation(hT[b][0:H, NA:CAP], ps_hid[1][0:H, 0:CAP - NA], ACT.Gelu_apprx_tanh,
                                             bias=b1_sb[b][:]).then_inc(e_gelu, 1)
                    t = k + 1
                    if t.within(E):
                        for g in range(G):
                            it = Item(t, g)
                            act.wait_ge(e_turned, it.done)
                            act.wait_ge(e_hidden, t.freed)
                            nc.scalar.copy(tokT[t.half][:, :, g * SLOT_P:(g + 1) * SLOT_P],
                                           ps_turn[it.half][:].rearrange("p (c q) -> p c q", c=DC)[:, :, 0:SLOT_P]).then_inc(e_turned_sb, 1)

                for_tiles(act, E, 1, 1, step)

            @block.vector
            def _(dve):
                credit(dve, row_cmp, row_sum, row_idx_ready, tok_cmp, tok_sum, tok_idx_ready, add_idx_ready, score_ready)
                dve.sem_inc(e_scaled, 2 * G)
                for b in range(2):
                    nc.vector.memset(hT[b][H:H + 1, :], 1.0).then_inc(c4_pool, 1)
                dve.wait_ge(c4_in, 16)
                dve.wait_ge(c4_pool, 4)

                def step(k):
                    if k.within(E):
                        dve.wait_ge(added[k.half], all_landed_before(k))
                        nc.vector.tensor_copy(add_idx[k.half][:], tok_idx[k.half][:]).then_inc(add_idx_ready, 1)
                    t = k + 2
                    if t.within(E):
                        b = t.half
                        dve.wait_ge(rank_in[b], all_landed(t))
                        nc.vector.tensor_tensor(cmp_tok[:], ranks[b][:], slot[:].unsqueeze(2).to_broadcast([SLOT_P, G, RL]),
                                                ALU.is_le).then_inc(tok_cmp, 1)
                        dve.wait_ge(tok_cmp, t.done)
                        nc.vector.tensor_reduce(n_tok[b][:], cmp_tok[:], AX_X, ALU.add).then_inc(tok_sum, 1)
                        dve.wait_ge(tok_sum, t.done)
                        dve.wait_ge(tok_in[b], all_landed_before(t))
                        nc.vector.scalar_tensor_tensor(tok_idx[b][:], n_row[b][:], float(RL), n_tok[b][:],
                                                       ALU.mult, ALU.add).then_inc(tok_idx_ready, 1)
                    t = k + 3
                    if t.within(E):
                        b = t.half
                        row_ends = ends_all[:, bass.ds(t.n * RR, RR)]
                        nc.vector.tensor_tensor(cmp_row[:], row_ends.unsqueeze(1).to_broadcast([SLOT_P, G, RR]),
                                                slot[:].unsqueeze(2).to_broadcast([SLOT_P, G, RR]), ALU.is_le).then_inc(row_cmp, 1)
                        dve.wait_ge(row_cmp, t.done)
                        nc.vector.tensor_reduce(n_row[b][:], cmp_row[:], AX_X, ALU.add).then_inc(row_sum, 1)
                        dve.wait_ge(row_sum, t.done)
                        dve.wait_ge(rank_in[b], all_landed_before(t))
                        nc.vector.tensor_scalar(row_idx[b][:], n_row[b][:], first_row[:, bass.ds(t.n, 1)], None,
                                                ALU.add).then_inc(row_idx_ready, 1)
                    t = k + 1
                    if t.within(E):
                        b = t.half
                        dve.wait_ge(e_scaled, Item(t, 0).expert_freed)
                        dve.wait_ge(tok_in[b], all_landed(t))
                        nc.vector.tensor_copy(score[b][:], toks[b][:, :, bass.ds(t.n + D, 1)].rearrange("p g o -> p (g o)")).then_inc(score_ready, 1)
                    if k.within(E):
                        b = k.half
                        dve.wait_ge(score_ready, k.done)
                        for g in range(G):
                            it = Item(k, g)
                            dve.wait_ge(e_out, it.done)
                            nc.vector.tensor_scalar(y[b][:, g, :], ps_out[it.half][0:SLOT_P, :], score[b][:, g:g + 1], None,
                                                    ALU.mult).then_inc(e_scaled, 1)

                for_tiles(dve, E, 3, 1, step)

            @block.tensor
            def _(pe):
                credit(pe, e_hidden)
                pe.sem_inc(e_turned, 2 * G)
                pe.sem_inc(e_out, 2 * G)

                def step(k):
                    if k.within(E):
                        b = k.half
                        pe.wait_ge(we_in[b], (k.pair + 1) * 64)
                        pe.wait_ge(e_turned_sb, Item(k, G - 1).done)
                        pe.wait_ge(e_gelu, k.done - 1)
                        for bank_, lo, hi in ((ps_hid[0], 0, NA), (ps_hid[1], NA, CAP)):
                            for c in range(DC):
                                mm = nc.tensor.matmul(bank_[0:H, 0:hi - lo], w1_sb[b][:, c, :], tokT[b][:, c, lo:hi],
                                                      start=(c == 0), stop=(c == DC - 1))
                        mm.then_inc(e_hidden, 1)
                    t = k + 1
                    if t.within(E):
                        for g in range(G):
                            it = Item(t, g)
                            pe.wait_ge(tok_in[t.half], all_landed(t))
                            pe.wait_ge(e_turned_sb, it.freed)
                            for c in range(DC):
                                mm = nc.tensor.transpose(ps_turn[it.half][:, c * P:c * P + SLOT_P],
                                                         toks[t.half][:, g, c * P:(c + 1) * P], ident[0:SLOT_P, 0:SLOT_P])
                            mm.then_inc(e_turned, 1)
                    if k.within(E):
                        b = k.half
                        pe.wait_ge(e_gelu, k.done)
                        for g in range(G):
                            it = Item(k, g)
                            pe.wait_ge(e_scaled, it.freed)
                            nc.tensor.matmul(ps_out[it.half][0:SLOT_P, :], hT[b][:, g * SLOT_P:(g + 1) * SLOT_P], w2_sb[b][:],
                                             start=True, stop=True).then_inc(e_out, 1)

                for_tiles(pe, E, 1, 1, step)


def kernel(**inputs):
    import numpy as _np
    import concourse.bacc as _bacc
    from concourse import mybir as _mybir
    from concourse.bass_utils import run_bass_kernel_spmd as _run

    a = {name.replace("L0_gnn_", "").replace("L0_ffn_", "ffn_"): _np.asarray(v) for name, v in inputs.items()}
    n, d = a["x"].shape
    tiles = -(-n // 128)
    pad = tiles * 128 - n
    src = _np.concatenate([a["src"], _np.zeros(pad, a["src"].dtype)]).reshape(tiles, 128).T
    dst = _np.concatenate([a["dst"], _np.full(pad, n, a["dst"].dtype)])
    laid = {
        "x": a["x"], "src": src, "dst": dst, "dst_c": dst.reshape(tiles, 128).T, "edge_attr": a["edge_attr_512"],
        "Wm": a["Wm"], "bm": a["bm"].reshape(-1, 128).T, "WuT": a["Wu"].T, "bu": a["bu"],
        "gamma": a["gamma"], "beta": a["beta"], "gate": a["ffn_gate_w"],
        "w1": a["ffn_w1"], "b1": a["ffn_b1"].reshape(*a["ffn_b1"].shape, 1), "w2": a["ffn_w2"], "b2": a["ffn_b2"],
        "sw1": a["ffn_sw1"], "sb1": a["ffn_sb1"].reshape(-1, 1), "sw2": a["ffn_sw2"], "sb2": a["ffn_sb2"].reshape(1, -1),
    }
    nc = _bacc.Bacc("TRN2", target_bir_lowering=False, num_devices=1)
    arrays, args = {}, []
    for name, v in laid.items():
        v = _np.ascontiguousarray(v)
        arrays[f"in_{name}"] = v
        args.append(nc.dram_tensor(f"in_{name}", v.shape, _mybir.dt.from_np(v.dtype), kind="ExternalInput").ap())
    args.append(nc.dram_tensor("out_0", (n, d), _mybir.dt.float32, kind="ExternalOutput").ap())
    gnn_then_expert_choice_ffn(nc, *args)
    r = _run(nc, [arrays], core_ids=[0])
    return r.results[0]["out_0"]
```

```python
from contextlib import ExitStack

import concourse.bass as bass
from concourse import mybir

P = 128
ALU = mybir.AluOpType
ACT = mybir.ActivationFunctionType
F32 = mybir.dt.float32
I32 = mybir.dt.int32
BF16 = mybir.dt.bfloat16
AX_X = mybir.AxisListType.X
EPS = 1e-5
CREDIT = 2


class At:

    def __init__(self, pair, half):
        self.pair, self.half = pair, half

    def __add__(self, d):
        return At(self.pair + (self.half + d) // 2, (self.half + d) % 2)

    @property
    def n(self):
        return self.pair * 2 + self.half

    @property
    def static(self):
        return isinstance(self.pair, int)

    def within(self, count):
        return not self.static or 0 <= self.n < count

    @property
    def done(self):
        return self.n + CREDIT + 1

    @property
    def freed(self):
        return self.n + 1

    @property
    def landed(self):
        return (self.pair + 1) * 16

    @property
    def landed_before(self):
        return self.pair * 16


def alone(eng):
    eng.nop(nofuse=True)


def for_tiles(eng, count, lead, lag, step):
    first = (lag + 1) // 2 * 2
    pairs_end = (count - lead) // 2
    for k in range(-lead, first):
        step(At(k // 2, k % 2))
    with eng.Fori(first // 2, pairs_end) as pair:
        step(At(pair, 0))
        step(At(pair, 1))
    for k in range(2 * pairs_end, count + lag):
        step(At(k // 2, k % 2))


def gnn_then_expert_choice_ffn(nc, x, src, dst, dst_c, edge_attr, WmN, bm, WuT, bu, gamma, beta,
                               gate, w1, b1, w2, b2, sw1, sb1, sw2, sb2, out):
    N, D = x.shape
    EDGES = edge_attr.shape[0]
    DC = D // P
    _, NT = src.shape
    TAIL = N - (NT - 1) * P
    assert EDGES == N and NT * P >= N
    E, _, H = w1.shape
    CAP = N // E
    SLOT_P = 125
    SLOT_G = CAP // SLOT_P
    assert SLOT_P * SLOT_G == CAP and D == DC * P
    TOK = NT * P
    CH = P // E
    TPC = -(-NT // CH)
    CL = TPC * P
    RQ = P // CH
    RL = CL // RQ
    assert RQ * RL == CL
    AW = D + 1
    TW = D + E
    AROWS = P * (N // P + 2)
    ZERO_ROWS = 8
    assert AROWS // P % ZERO_ROWS == 0
    ZEROED = 16 * (AROWS // P // ZERO_ROWS)
    TRASH = N + 1
    assert TRASH + P <= AROWS

    agg = nc.dram_tensor("agg", (AROWS, AW), F32, kind="Internal").ap()
    fused_w_d = nc.dram_tensor("fused_w_d", (P, DC * D), F32, kind="Internal").ap()
    fused_b_d = nc.dram_tensor("fused_b_d", (P, D), F32, kind="Internal").ap()
    fused_b3_d = nc.dram_tensor("fused_b3_d", (3, D), BF16, kind="Internal").ap()
    table = nc.dram_tensor("table", (TOK, TW), F32, kind="Internal").ap()
    hidden_d = nc.dram_tensor("hidden_d", (H, TOK), F32, kind="Internal").ap()
    rank_d = nc.dram_tensor("rank_d", (E, P, RL + 1), F32, kind="Internal").ap()

    with ExitStack() as whole:
        def sb(name, shape, dt=F32, scope=whole):
            return scope.enter_context(nc.sbuf_tensor(name, shape, dt))

        def sem(name):
            return whole.enter_context(nc.semaphore(name))

        def pair_of(name):
            return [sem(f"{name}0"), sem(f"{name}1")]

        bank = [whole.enter_context(nc.psum_tensor(f"bank{i}", [P, 512], F32)) for i in range(8)]

        ident = sb("ident", [P, P])
        neg_half = sb("neg_half", [P, 1])
        nodes_scope = whole.enter_context(ExitStack())
        nodes = sb("nodes", [P, NT * D], scope=nodes_scope)

        def node_slot(t):
            return nodes[:, bass.ds(t.n * D, D)]

        def rows(ap, t, last):
            return ap[(NT - 1) * P:(NT - 1) * P + TAIL, :] if last else ap[bass.ds(t.n * P, P), :]

        zeros_done, const_in, fused_stored = sem("zeros_done"), sem("const_in"), sem("fused_stored")
        p0_pool, p0_dve, p0_pe, fused_copied, parts_ready = [sem(s) for s in ("p0_pool", "p0_dve", "p0_pe", "fused_copied", "parts_ready")]
        with ExitStack() as scope, nc.Block() as block:
            zeros = nodes[:, NT * D - AW:NT * D]
            bm_col = sb("bm_col", [P, DC], scope=scope)
            bm_wide = sb("bm_wide", [P, DC, P], scope=scope)
            wm_sb = nodes[:, 0:DC * D].rearrange("p (c n) -> p c n", c=DC)
            wur_sb = nodes[:, DC * D:2 * DC * D].rearrange("p (c n) -> p c n", c=DC)
            fused_sb = nodes[:, 2 * DC * D:3 * DC * D].rearrange("p (c n) -> p c n", c=DC)
            fused_b_sb = nodes[:, 3 * DC * D:3 * DC * D + D]
            part = [sb(f"part{n}", [1, D], BF16, scope) for n in range(3)]
            rest = [sb(f"rest{n}", [1, D], scope=scope) for n in range(2)]

            @block.sync
            def _(sp):
                sp.dma_start(wm_sb, WmN.rearrange("(c p) n -> p c n", p=P)).then_inc(const_in, 16)
                sp.dma_start(wur_sb, WuT[D:2 * D, :].rearrange("(c p) n -> p c n", p=P)).then_inc(const_in, 16)
                sp.dma_start(bm_col[:], bm).then_inc(const_in, 16)
                sp.wait_ge(fused_copied, DC + 1)
                sp.dma_start(fused_w_d, nodes[:, 2 * DC * D:3 * DC * D]).then_inc(fused_stored, 16)
                sp.dma_start(fused_b_d, fused_b_sb).then_inc(fused_stored, 16)
                sp.wait_ge(parts_ready, 5)
                for n in range(3):
                    sp.dma_start(fused_b3_d[n:n + 1, :], part[n][:]).then_inc(fused_stored, 16)
                sp.wait_ge(fused_stored, 16 * 5)

            @block.gpsimd
            def _(pool):
                nc.gpsimd.memset(ident[:], 0.0).then_inc(p0_pool, 1)
                nc.gpsimd.memset(neg_half[:], -0.5)
                pool.wait_ge(p0_pool, 1)
                nc.gpsimd.affine_select(out=ident[:], in_=ident[:], compare_op=ALU.not_equal, fill=1.0, base=0,
                                        pattern=[[-1, P]], channel_multiplier=1).then_inc(p0_pool, 1)

            @block.scalar
            def _(act):
                act.wait_ge(p0_dve, 1)
                empty = agg.rearrange("(p r) w -> p r w", p=P)
                for r in range(0, AROWS // P, ZERO_ROWS):
                    act.dma_start(empty[:, r:r + ZERO_ROWS, :],
                                  zeros.unsqueeze(1).to_broadcast([P, ZERO_ROWS, AW])).then_inc(zeros_done, 16)

            @block.vector
            def _(dve):
                nc.vector.memset(zeros, 0.0).then_inc(p0_dve, 1)
                dve.wait_ge(const_in, 48)
                nc.vector.tensor_copy(bm_wide[:], bm_col[:].unsqueeze(2).to_broadcast([P, DC, P])).then_inc(p0_dve, 1)
                for c in range(DC + 1):
                    dve.wait_ge(p0_pe, c + 1)
                    nc.vector.tensor_copy(fused_sb[:, c, :] if c < DC else fused_b_sb, bank[c][:]).then_inc(fused_copied, 1)
                left_over = fused_b_sb[0:1, :]
                dve.wait_ge(fused_copied, DC + 1)
                for n in range(3):
                    nc.vector.tensor_copy(part[n][:], left_over).then_inc(parts_ready, 1)
                    if n < 2:
                        dve.wait_ge(parts_ready, 2 * n + 1)
                        nc.vector.tensor_tensor(rest[n][:], left_over, part[n][:], ALU.subtract).then_inc(parts_ready, 1)
                        dve.wait_ge(parts_ready, 2 * n + 2)
                        left_over = rest[n][:]

            @block.tensor
            def _(pe):
                pe.wait_ge(const_in, 48)
                for c in range(DC):
                    for j in range(DC):
                        last = nc.tensor.matmul(bank[c][:], wm_sb[:, j, c * P:(c + 1) * P], wur_sb[:, j, :],
                                                start=(j == 0), stop=(j == DC - 1))
                    last.then_inc(p0_pe, 1)
                pe.wait_ge(p0_dve, 2)
                for j in range(DC):
                    last = nc.tensor.matmul(bank[DC][:], bm_wide[:, j, :], wur_sb[:, j, :], start=(j == 0), stop=(j == DC - 1))
                last.then_inc(p0_pe, 1)

        w1_in = sem("w1_in")
        x_in, xg_in, ea_in, dr_in = pair_of("x_in"), pair_of("xg_in"), pair_of("ea_in"), pair_of("dr_in")
        scattered = pair_of("scattered")
        p1_const = sem("p1_const")
        src_picked = sem("src_picked")
        x_raw, x_stats, x_eps, x_rstd = sem("x_raw"), sem("x_stats"), sem("x_eps"), sem("x_rstd")
        g_raw, g_stats, g_eps, g_rstd = sem("g_raw"), sem("g_stats"), sem("g_eps"), sem("g_rstd")
        x_norm, x_turned, x_turned_sb = sem("x_norm"), sem("x_turned"), sem("x_turned_sb")
        g_norm, msg_ready, same_ready, earlier = sem("g_norm"), sem("msg_ready"), sem("same_ready"), sem("earlier")
        idx_step, idx_ready = sem("idx_step"), sem("idx_ready")
        sums, sums_sb, left, left_sb = sem("sums"), sem("sums_sb"), sem("left"), sem("left_sb")

        def rstd_on_pool(pool, t, stats, stats_done, eps_sem, out_sem, bias_sem=None):
            pool.wait_ge(stats_done, t.done)
            alone(pool)
            nc.gpsimd.tensor_scalar(stats[:, 2:3], stats[:, 1:2], EPS, None, ALU.add).then_inc(eps_sem, 1)
            pool.wait_ge(eps_sem, t.done)
            nc.gpsimd.tensor_tensor(stats[:, 3:4], stats[:, 2:3], neg_half[:], ALU.pow).then_inc(out_sem, 1)
            if bias_sem is not None:
                pool.wait_ge(out_sem, t.done)
                alone(pool)
                nc.gpsimd.tensor_scalar(stats[:, 4:5], stats[:, 0:1], stats[:, 3:4], -1.0, ALU.mult, ALU.mult).then_inc(bias_sem, 1)

        def credit(eng, *sems):
            for s in sems:
                eng.sem_inc(s, CREDIT)

        with ExitStack() as scope, nc.Block() as block:
            def two(name, shape, dt=F32):
                return [sb(f"{name}{b}", shape, dt, scope) for b in range(2)]

            wul_sb = sb("wul_sb", [P, DC, D], scope=scope)
            bu_sb = sb("bu_sb", [P, D], scope=scope)
            fused_b_sb = sb("fused_b_sb", [P, D], scope=scope)
            src_col = sb("src_col", [P, NT], I32, scope)
            dst_col = sb("dst_col", [P, NT], I32, scope)
            dst_f = sb("dst_f", [P, NT], scope=scope)
            to_trash = sb("to_trash", [P, NT], scope=scope)
            trash_row = sb("trash_row", [P, 1], scope=scope)
            before = sb("before", [P, P], scope=scope)
            x_t, xg, ea = two("x_t", [P, D]), two("xg", [P, D]), two("ea", [P, D])
            dst_row = two("dst_row", [P, P], I32)
            src_idx, dst_idx = two("src_idx", [P, 1], I32), two("dst_idx", [P, 1], I32)
            xs6, gs6 = two("xs6", [P, 6]), two("gs6", [P, 6])
            xs, gs = two("xs", [P, 5]), two("gs", [P, 5])
            xn, msg, xT = two("xn", [P, D]), two("msg", [P, D]), two("xT", [P, D])
            same, prior, n_prior, moved = two("same", [P, P]), sb("prior", [P, P], scope=scope), two("n_prior", [P, 1]), two("moved", [P, 1])
            sum_sb, degree = two("sum_sb", [P, AW]), two("degree", [P, 1])
            ps_turn, ps_left, ps_sum = bank[0:2], bank[2:4], bank[4:6]

            @block.sync
            def _(sp):
                sp.dma_start(src_col[:], src).then_inc(w1_in, 16)
                sp.dma_start(dst_col[:], dst_c).then_inc(w1_in, 16)
                sp.dma_start(wul_sb[:], WuT[0:D, :].rearrange("(c p) n -> p c n", p=P)).then_inc(w1_in, 16)
                sp.dma_start(bu_sb[:], bu.partition_broadcast(P)).then_inc(w1_in, 16)
                sp.dma_start(fused_b_sb[:], fused_b_d).then_inc(w1_in, 16)

                def loads(t):
                    last = t.static and t.n == NT - 1
                    r = TAIL if last else P
                    sp.wait_ge(x_norm, t.freed)
                    sp.dma_start(x_t[t.half][0:r, :], rows(x, t, last)).then_inc(x_in[t.half], 16)
                    sp.wait_ge(same_ready, t.freed)
                    alone(sp)
                    sp.dma_start(dst_row[t.half][:], dst[bass.ds(t.n * P, P)].partition_broadcast(P)).then_inc(dr_in[t.half], 16)
                    sp.wait_ge(msg_ready, t.freed)
                    sp.dma_start(ea[t.half][0:r, :], rows(edge_attr, t, last)).then_inc(ea_in[t.half], 16)

                for_tiles(sp, NT, 0, 0, loads)

            @block.gpsimd
            def _(pool):
                nc.gpsimd.memset(before[:], 1.0).then_inc(p1_const, 1)
                nc.gpsimd.iota(trash_row[:], pattern=[[0, 1]], base=TRASH, channel_multiplier=1,
                               allow_small_or_imprecise_dtypes=True).then_inc(p1_const, 1)
                pool.wait_ge(p1_const, 1)
                nc.gpsimd.affine_select(out=before[:], in_=before[:], compare_op=ALU.is_gt, fill=0.0, base=0,
                                        pattern=[[-1, P]], channel_multiplier=1).then_inc(p1_const, 1)
                credit(pool, src_picked, x_eps, x_rstd, g_eps, g_rstd)
                pool.wait_ge(w1_in, 80)

                def step(k):
                    t = k + 2
                    if t.within(NT):
                        pool.wait_ge(xg_in[t.half], t.landed_before)
                        nc.gpsimd.tensor_copy(src_idx[t.half][:], src_col[:, bass.ds(t.n, 1)]).then_inc(src_picked, 1)
                        pool.wait_ge(src_picked, t.done)
                        pool.wait_ge(g_norm, t.freed)
                        alone(pool)
                        nc.gpsimd.indirect_dma_start(
                            xg[t.half][:], None, x, bass.IndirectOffsetOnAxis(src_idx[t.half][:], 0),
                        ).then_inc(xg_in[t.half], 16)
                    t = k + -1
                    if t.within(NT):
                        pool.wait_ge(sums_sb, t.done)
                        pool.wait_ge(idx_ready, t.done)
                        if t.static and t.n == 0:
                            pool.wait_ge(zeros_done, ZEROED)
                        else:
                            before_t = t + -1
                            pool.wait_ge(scattered[before_t.half], before_t.landed)
                        alone(pool)
                        nc.gpsimd.indirect_dma_start(
                            agg, bass.IndirectOffsetOnAxis(dst_idx[t.half][:], 0), sum_sb[t.half][:], None,
                            compute_op=ALU.add).then_inc(scattered[t.half], 16)
                    t = k + 1
                    if t.within(NT):
                        rstd_on_pool(pool, t, gs[t.half], g_stats, g_eps, g_rstd)
                    t = k + 2
                    if t.within(NT):
                        rstd_on_pool(pool, t, xs[t.half], x_stats, x_eps, x_rstd)

                for_tiles(pool, NT, 2, 2, step)
                for t in (At((NT - 2) // 2, (NT - 2) % 2), At((NT - 1) // 2, (NT - 1) % 2)):
                    pool.wait_ge(scattered[t.half], t.landed)

            @block.scalar
            def _(act):
                credit(act, x_turned_sb, sums_sb)

                def step(k):
                    t = k + -1
                    if t.within(NT):
                        act.wait_ge(sums, t.done)
                        act.wait_ge(scattered[t.half], t.landed_before)
                        nc.scalar.copy(sum_sb[t.half][:, D:D + 1], degree[t.half][:])
                        nc.scalar.copy(sum_sb[t.half][:, 0:D], ps_sum[t.half][:]).then_inc(sums_sb, 1)
                    t = k + 1
                    if t.within(NT):
                        act.wait_ge(x_turned, t.done)
                        act.wait_ge(left, t.freed)
                        nc.scalar.copy(xT[t.half][:], ps_turn[t.half][:]).then_inc(x_turned_sb, 1)

                for_tiles(act, NT, 1, 4, step)

            @block.vector
            def _(dve):
                credit(dve, x_raw, x_stats, g_raw, g_stats, x_norm, g_norm, msg_ready, same_ready, earlier, idx_step, idx_ready, left_sb)
                dve.wait_ge(w1_in, 80)
                dve.wait_ge(p1_const, 3)
                nc.vector.tensor_copy(dst_f[:], dst_col[:]).then_inc(p1_const, 1)
                dve.wait_ge(p1_const, 4)
                nc.vector.tensor_scalar(to_trash[:], dst_f[:], -1.0, trash_row[:], ALU.mult, ALU.add).then_inc(p1_const, 1)
                nc.vector.tensor_tensor(bu_sb[:], bu_sb[:], fused_b_sb[:], ALU.add).then_inc(p1_const, 1)
                dve.wait_ge(p1_const, 6)

                def stats(t, data, arrived, six, raw, two_, stats_done, free):
                    dve.wait_ge(arrived[t.half], t.landed)
                    alone(dve)
                    nc.vector.bn_stats(six[t.half][:], data[t.half][:]).then_inc(raw, 1)
                    dve.wait_ge(raw, t.done)
                    dve.wait_ge(free, t.freed)
                    alone(dve)
                    nc.vector.bn_aggr(two_[t.half][:, 0:2], six[t.half][:]).then_inc(stats_done, 1)

                def step(k):
                    t = k + -1
                    if t.within(NT):
                        dve.wait_ge(left, t.done)
                        dve.wait_ge(idx_step, t.done)
                        nc.vector.tensor_tensor(node_slot(t), ps_left[t.half][:], bu_sb[:], ALU.add).then_inc(left_sb, 1)
                        dve.wait_ge(scattered[t.half], t.landed_before)
                        nc.vector.tensor_tensor(dst_idx[t.half][:], moved[t.half][:], dst_f[:, bass.ds(t.n, 1)], ALU.add).then_inc(idx_ready, 1)
                    t = k + 1
                    b, column = t.half, bass.ds(t.n, 1)
                    if k.within(NT):
                        dve.wait_ge(g_rstd, k.done)
                        dve.wait_ge(sums, k.freed)
                        nc.vector.tensor_scalar(msg[k.half][:], xg[k.half][:], gs[k.half][:, 0:1], gs[k.half][:, 3:4],
                                                ALU.subtract, ALU.mult).then_inc(g_norm, 1)
                    if t.within(NT):
                        dve.wait_ge(x_rstd, t.done)
                        dve.wait_ge(x_turned, t.freed)
                        nc.vector.tensor_scalar(xn[b][:], x_t[b][:], xs[b][:, 0:1], xs[b][:, 3:4],
                                                ALU.subtract, ALU.mult).then_inc(x_norm, 1)
                    if k.within(NT):
                        dve.wait_ge(g_norm, k.done)
                        dve.wait_ge(ea_in[k.half], k.landed)
                        nc.vector.tensor_tensor(msg[k.half][:], msg[k.half][:], ea[k.half][:], ALU.add).then_inc(msg_ready, 1)
                    if t.within(NT):
                        dve.wait_ge(dr_in[b], t.landed)
                        dve.wait_ge(sums, t.freed)
                        dve.wait_ge(sums_sb, t.freed)
                        nc.vector.tensor_scalar(same[b][:], dst_row[b][:], dst_f[:, column], 0.0, ALU.is_equal, ALU.add,
                                                accum_out=degree[b][:]).then_inc(same_ready, 1)
                        dve.wait_ge(same_ready, t.done)
                        nc.vector.tensor_tensor_reduce(out=prior[:], in0=same[b][:], in1=before[:], scale=1.0, scalar=0.0,
                                                       op0=ALU.mult, op1=ALU.add, accum_out=n_prior[b][:]).then_inc(earlier, 1)
                        stats(t, xg, xg_in, gs6, g_raw, gs, g_stats, g_norm)
                    t2 = k + 2
                    if t2.within(NT):
                        stats(t2, x_t, x_in, xs6, x_raw, xs, x_stats, x_norm)
                    if t.within(NT):
                        dve.wait_ge(earlier, t.done)
                        nc.vector.tensor_scalar(moved[b][:], n_prior[b][:], 1.0, to_trash[:, column], ALU.min, ALU.mult).then_inc(idx_step, 1)

                for_tiles(dve, NT, 2, 4, step)

            @block.tensor
            def _(pe):
                credit(pe, x_turned, left, sums)
                pe.wait_ge(w1_in, 80)

                def step(k):
                    b = k.half
                    if k.within(NT):
                        pe.wait_ge(x_turned_sb, k.done)
                        pe.wait_ge(left_sb, k.freed)
                        for c in range(DC):
                            mm = nc.tensor.matmul(ps_left[b][:], xT[b][:, c * P:(c + 1) * P], wul_sb[:, c, :],
                                                  start=(c == 0), stop=(c == DC - 1))
                        mm.then_inc(left, 1)
                    t = k + 1
                    if t.within(NT):
                        pe.wait_ge(x_norm, t.done)
                        pe.wait_ge(x_turned_sb, t.freed)
                        for c in range(DC):
                            mm = nc.tensor.transpose(ps_turn[t.half][:, c * P:(c + 1) * P], xn[t.half][:, c * P:(c + 1) * P], ident[:])
                        mm.then_inc(x_turned, 1)
                    if k.within(NT):
                        pe.wait_ge(msg_ready, k.done)
                        pe.wait_ge(same_ready, k.done)
                        pe.wait_ge(sums_sb, k.freed)
                        nc.tensor.matmul(ps_sum[b][:], same[b][:], msg[b][:], start=True, stop=True).then_inc(sums, 1)

                for_tiles(pe, NT, 1, 0, step)

        c2_in = sem("c2_in")
        ag_in, y_in, xr_in = pair_of("ag_in"), pair_of("y_in"), pair_of("xr_in")
        table_stored, hidden_stored = pair_of("table_stored"), pair_of("hidden_stored")
        ag_turned, ag_turned_sb, upd = sem("ag_turned"), sem("ag_turned_sb"), sem("upd")
        deg_max, deg_inv, deg_turned, no_edge_ready = sem("deg_max"), sem("deg_inv"), sem("deg_turned"), sem("no_edge_ready")
        y_raw, y_stats, y_eps, y_rstd, y_bias, y_norm = [sem(f"y_{s}") for s in ("raw", "stats", "eps", "rstd", "bias", "norm")]
        o_raw, o_stats, o_eps, o_rstd = [sem(f"o_{s}") for s in ("raw", "stats", "eps", "rstd")]
        z_raw, z_stats, z_eps, z_rstd, z_bias = [sem(f"z_{s}") for s in ("raw", "stats", "eps", "rstd", "bias")]
        u_ready, u_gelu, o_ready, o_gamma, x1_ready, res_ready = [sem(s) for s in ("u_ready", "u_gelu", "o_ready", "o_gamma", "x1_ready", "res_ready")]
        z_norm, z_turned, z_turned_sb, hidden, logits, hidden_sb, logit_sb = [
            sem(s) for s in ("z_norm", "z_turned", "z_turned_sb", "hidden", "logits", "hidden_sb", "logit_sb")]

        logit_scope = whole.enter_context(ExitStack())
        lg = sb("lg", [P, NT, E], scope=logit_scope)
        with ExitStack() as scope, nc.Block() as block:
            def two(name, shape, dt=F32):
                return [sb(f"{name}{b}", shape, dt, scope) for b in range(2)]

            fused_sb = sb("fused_sb", [P, DC, D], scope=scope)
            fused_b3 = sb("fused_b3", [3, D], BF16, scope)
            no_edge = two("no_edge", [3, P], BF16)
            gamma_sb, beta_sb = [sb(n, [P, D], scope=scope) for n in ("gamma_sb", "beta_sb")]
            sw1_sb = sb("sw1_sb", [P, DC, H], scope=scope)
            gate_sb = sb("gate_sb", [P, DC, E], scope=scope)
            ag, agT = two("ag", [P, AW]), sb("agT", [P, D], scope=scope)
            y_t, yn, res = two("y_t", [P, D]), two("yn", [P, D]), two("res", [P, D])
            upd_sb, z, zT = two("upd_sb", [P, D]), two("z", [P, D]), sb("zT", [P, D], scope=scope)
            deg = two("deg", [P, 2])
            ys6, os6, zs6 = two("ys6", [P, 6]), two("os6", [P, 6]), two("zs6", [P, 6])
            ys, os_, zs = two("ys", [P, 5]), two("os_", [P, 5]), two("zs", [P, 5])
            hid = two("hid", [H, P])
            ps_agT, ps_upd, ps_zT, ps_hidden, ps_logits, ps_deg = bank[0], bank[1:3], bank[3], bank[4], bank[5:7], bank[7]

            @block.sync
            def _(sp):
                sp.dma_start(fused_sb[:].rearrange("p c n -> p (c n)"), fused_w_d).then_inc(c2_in, 16)
                sp.dma_start(fused_b3[:], fused_b3_d).then_inc(c2_in, 16)
                sp.dma_start(gamma_sb[:], gamma.partition_broadcast(P)).then_inc(c2_in, 16)
                sp.dma_start(beta_sb[:], beta.partition_broadcast(P)).then_inc(c2_in, 16)
                sp.dma_start(sw1_sb[:], sw1.rearrange("(c p) n -> p c n", p=P)).then_inc(c2_in, 16)
                sp.dma_start(gate_sb[:], gate.rearrange("(c p) n -> p c n", p=P)).then_inc(c2_in, 16)

                def step(k):
                    t = k + 2
                    if t.within(NT):
                        sp.wait_ge(ag_turned, t.freed)
                        sp.wait_ge(deg_turned, t.freed)
                        sp.wait_ge(deg_max, t.freed)
                        alone(sp)
                        sp.dma_start(ag[t.half][:], agg[bass.ds(t.n * P, P), :]).then_inc(ag_in[t.half], 16)
                    t = k + 3
                    if t.within(NT):
                        last = t.static and t.n == NT - 1
                        sp.wait_ge(y_norm, t.freed)
                        sp.dma_start(y_t[t.half][0:TAIL if last else P, :], rows(x, t, last)).then_inc(y_in[t.half], 16)
                    t = k
                    if t.within(NT):
                        last = t.static and t.n == NT - 1
                        sp.wait_ge(x1_ready, t.freed)
                        sp.dma_start(res[t.half][0:TAIL if last else P, :], rows(x, t, last)).then_inc(xr_in[t.half], 16)
                    t = k + -3
                    if t.within(NT):
                        sp.wait_ge(z_norm, t.done)
                        sp.dma_start(table[bass.ds(t.n * P, P), 0:D], z[t.half][:]).then_inc(table_stored[t.half], 16)
                    t = k + -6
                    if t.within(NT):
                        sp.wait_ge(hidden_sb, t.done)
                        sp.dma_start(hidden_d[:, bass.ds(t.n * P, P)], hid[t.half][:]).then_inc(hidden_stored[t.half], 16)

                for_tiles(sp, NT, 4, 6, step)
                for t in (At((NT - 2) // 2, (NT - 2) % 2), At((NT - 1) // 2, (NT - 1) % 2)):
                    for s in (table_stored, hidden_stored):
                        sp.wait_ge(s[t.half], t.landed)

            @block.gpsimd
            def _(pool):
                credit(pool, y_eps, y_rstd, y_bias, o_eps, o_rstd, z_eps, z_rstd, z_bias, res_ready)
                pool.wait_ge(c2_in, 96)

                def step(k):
                    t = k + -1
                    if t.within(NT):
                        rstd_on_pool(pool, t, os_[t.half], o_stats, o_eps, o_rstd)
                    t = k + -2
                    if t.within(NT):
                        rstd_on_pool(pool, t, zs[t.half], z_stats, z_eps, z_rstd, z_bias)
                    t = k + -1
                    if t.within(NT):
                        b = t.half
                        pool.wait_ge(xr_in[b], t.landed)
                        nc.gpsimd.tensor_tensor(res[b][:], res[b][:], beta_sb[:], ALU.add).then_inc(res_ready, 1)
                    t = k + 2
                    if t.within(NT):
                        rstd_on_pool(pool, t, ys[t.half], y_stats, y_eps, y_rstd, y_bias)

                for_tiles(pool, NT, 2, 2, step)

            @block.scalar
            def _(act):
                credit(act, y_norm, u_gelu, ag_turned_sb, z_norm, z_turned_sb, hidden_sb)

                def step(k):
                    t = k + -3
                    if t.within(NT):
                        act.wait_ge(z_bias, t.done)
                        act.wait_ge(z_turned, t.freed)
                        act.wait_ge(table_stored[t.half], t.landed_before)
                        nc.scalar.activation(z[t.half][:], node_slot(t), ACT.Identity, bias=zs[t.half][:, 4:5],
                                             scale=zs[t.half][:, 3:4]).then_inc(z_norm, 1)
                    t = k + 1
                    if t.within(NT):
                        act.wait_ge(ag_turned, t.done)
                        act.wait_ge(upd, t.done - 1)
                        nc.scalar.copy(agT[:], ps_agT[:]).then_inc(ag_turned_sb, 1)
                    t = k + -1
                    if t.within(NT):
                        act.wait_ge(u_ready, t.done)
                        nc.scalar.activation(upd_sb[t.half][:], upd_sb[t.half][:], ACT.Gelu).then_inc(u_gelu, 1)
                    t = k + 1
                    if t.within(NT):
                        act.wait_ge(y_bias, t.done)
                        act.wait_ge(o_ready, t.freed)
                        nc.scalar.activation(yn[t.half][:], y_t[t.half][:], ACT.Identity, bias=ys[t.half][:, 4:5],
                                             scale=ys[t.half][:, 3:4]).then_inc(y_norm, 1)
                    t = k + -5
                    if t.within(NT):
                        act.wait_ge(hidden, t.done)
                        act.wait_ge(hidden_stored[t.half], t.landed_before)
                        nc.scalar.copy(hid[t.half][:], ps_hidden[0:H, 0:P]).then_inc(hidden_sb, 1)
                    t = k + -4
                    if t.within(NT):
                        act.wait_ge(z_turned, t.done)
                        act.wait_ge(logits, t.done - 1)
                        nc.scalar.copy(zT[:], ps_zT[:]).then_inc(z_turned_sb, 1)

                for_tiles(act, NT, 1, 7, step)

            @block.vector
            def _(dve):
                credit(dve, y_raw, y_stats, o_raw, o_stats, z_raw, z_stats, deg_max, deg_inv, no_edge_ready,
                       u_ready, o_ready, o_gamma, x1_ready, logit_sb)
                dve.wait_ge(c2_in, 96)

                def stats(t, data, six, raw, two_, stats_done, free):
                    alone(dve)
                    nc.vector.bn_stats(six[t.half][:], data).then_inc(raw, 1)
                    dve.wait_ge(raw, t.done)
                    dve.wait_ge(free, t.freed)
                    alone(dve)
                    nc.vector.bn_aggr(two_[t.half][:, 0:2], six[t.half][:]).then_inc(stats_done, 1)

                def step(k):
                    t = k + -1
                    if t.within(NT):
                        b = t.half
                        dve.wait_ge(upd, t.done)
                        dve.wait_ge(deg_inv, t.done)
                        dve.wait_ge(x1_ready, t.freed)
                        nc.vector.scalar_tensor_tensor(upd_sb[b][:], ps_upd[b][:], deg[b][:, 1:2], node_slot(t),
                                                       ALU.mult, ALU.add).then_inc(u_ready, 1)
                    t = k + 1
                    if t.within(NT):
                        b = t.half
                        dve.wait_ge(deg_turned, t.done)
                        dve.wait_ge(upd, t.freed)
                        nc.vector.tensor_scalar(no_edge[b][:], ps_deg[0:3, 0:P], 0.0, -1.0, ALU.is_equal, ALU.mult).then_inc(no_edge_ready, 1)
                        dve.wait_ge(u_ready, t.freed)
                        nc.vector.tensor_scalar(deg[b][:, 0:1], ag[b][:, D:D + 1], 1.0, None, ALU.max).then_inc(deg_max, 1)
                    t = k + -2
                    if t.within(NT):
                        b = t.half
                        dve.wait_ge(o_rstd, t.done)
                        nc.vector.scalar_tensor_tensor(upd_sb[b][:], upd_sb[b][:], os_[b][:, 0:1], gamma_sb[:],
                                                       ALU.subtract, ALU.mult).then_inc(o_gamma, 1)
                        dve.wait_ge(o_gamma, t.done)
                        dve.wait_ge(res_ready, t.done)
                        nc.vector.scalar_tensor_tensor(node_slot(t), upd_sb[b][:], os_[b][:, 3:4], res[b][:],
                                                       ALU.mult, ALU.add).then_inc(x1_ready, 1)
                    t = k + 1
                    if t.within(NT):
                        dve.wait_ge(deg_max, t.done)
                        nc.vector.reciprocal(deg[t.half][:, 1:2], deg[t.half][:, 0:1]).then_inc(deg_inv, 1)
                    t = k + -1
                    if t.within(NT):
                        dve.wait_ge(u_gelu, t.done)
                        dve.wait_ge(y_norm, t.done)
                        nc.vector.tensor_tensor(upd_sb[t.half][:], upd_sb[t.half][:], yn[t.half][:], ALU.add).then_inc(o_ready, 1)
                    t = k + -6
                    if t.within(NT):
                        dve.wait_ge(logits, t.done)
                        nc.vector.tensor_copy(lg[:, bass.ds(t.n, 1), :].rearrange("p a e -> p (a e)"), ps_logits[t.half][:, 0:E]).then_inc(logit_sb, 1)
                    t = k + -1
                    if t.within(NT):
                        dve.wait_ge(o_ready, t.done)
                        stats(t, upd_sb[t.half][:], os6, o_raw, os_, o_stats, x1_ready)
                    t = k + -2
                    if t.within(NT):
                        dve.wait_ge(x1_ready, t.done)
                        stats(t, node_slot(t), zs6, z_raw, zs, z_stats, z_norm)
                    t = k + 2
                    if t.within(NT):
                        dve.wait_ge(y_in[t.half], t.landed)
                        stats(t, y_t[t.half][:], ys6, y_raw, ys, y_stats, y_norm)

                for_tiles(dve, NT, 2, 6, step)

            @block.tensor
            def _(pe):
                credit(pe, ag_turned, deg_turned, upd, z_turned, hidden, logits)
                pe.wait_ge(c2_in, 96)

                def step(k):
                    t = k + 1
                    if t.within(NT):
                        b = t.half
                        pe.wait_ge(ag_in[b], t.landed)
                        pe.wait_ge(ag_turned_sb, t.done - 1)
                        for c in range(DC):
                            mm = nc.tensor.transpose(ps_agT[:, c * P:(c + 1) * P], ag[b][:, c * P:(c + 1) * P], ident[:])
                        mm.then_inc(ag_turned, 1)
                        pe.wait_ge(no_edge_ready, t.done - 1)
                        nc.tensor.transpose(ps_deg[0:3, 0:P], ag[b][:, D:D + 1].to_broadcast([P, 3]), ident[:]).then_inc(deg_turned, 1)
                    if k.within(NT):
                        b = k.half
                        pe.wait_ge(ag_turned_sb, k.done)
                        pe.wait_ge(u_ready, k.freed)
                        for c in range(DC):
                            nc.tensor.matmul(ps_upd[b][:], agT[:, c * P:(c + 1) * P], fused_sb[:, c, :],
                                             start=(c == 0), stop=False)
                        pe.wait_ge(no_edge_ready, k.done)
                        nc.tensor.matmul(ps_upd[b][:], no_edge[b][:], fused_b3[:], start=False, stop=True).then_inc(upd, 1)
                    t = k + -5
                    if t.within(NT):
                        b = t.half
                        pe.wait_ge(z_turned_sb, t.done)
                        pe.wait_ge(hidden_sb, t.done - 1)
                        for c in range(DC):
                            mm = nc.tensor.matmul(ps_hidden[0:H, 0:P], sw1_sb[:, c, :], zT[:, c * P:(c + 1) * P],
                                                  start=(c == 0), stop=(c == DC - 1))
                        mm.then_inc(hidden, 1)
                        pe.wait_ge(logit_sb, t.freed)
                        for c in range(DC):
                            mm = nc.tensor.matmul(ps_logits[b][:, 0:E], zT[:, c * P:(c + 1) * P], gate_sb[:, c, :],
                                                  start=(c == 0), stop=(c == DC - 1))
                        mm.then_inc(logits, 1)
                    t = k + -4
                    if t.within(NT):
                        pe.wait_ge(z_norm, t.done)
                        pe.wait_ge(z_turned_sb, t.done - 1)
                        for c in range(DC):
                            mm = nc.tensor.transpose(ps_zT[:, c * P:(c + 1) * P], z[t.half][:, c * P:(c + 1) * P], ident[:])
                        mm.then_inc(z_turned, 1)

                for_tiles(pe, NT, 1, 5, step)

        BITS = 30
        TRI = 3
        NTRI = -(-NT // TRI)
        assert NT == (NTRI - 1) * TRI + 1 and NTRI < BITS
        TURN = 4
        c3_in, h_in, prob_stored = sem("c3_in"), pair_of("h_in"), sem("prob_stored")
        p3_pool, p3_dve, p3_act, p3_pe = sem("p3_pool"), sem("p3_dve"), sem("p3_act"), sem("p3_pe")
        cand_ready, count_ready, total_ready, keep_ready, bit_ready, kth_ready = [
            sem(s) for s in ("cand_ready", "count_ready", "total_ready", "keep_ready", "bit_ready", "kth_ready")]
        h_gelu, shared, added_dve, added_pool, copied, out_stored = [
            sem(s) for s in ("h_gelu", "shared", "added_dve", "added_pool", "copied", "out_stored")]
        rank_stored, fin_dve, fin_pe = sem("rank_stored"), sem("fin_dve"), sem("fin_pe")

        TB = CH * TPC
        with ExitStack() as scope, nc.Block() as block:
            prob = sb("prob", [P, TB, E], scope=scope)
            stat = sb("stat", [P, NT], scope=scope)
            mine = sb("mine", [P, E], scope=scope)
            same_e = sb("same_e", [P, P], scope=scope)
            earlier_c = sb("earlier_c", [P, P], scope=scope)
            search = sb("search", [P, CL], scope=scope)
            marks = sb("marks", [P, RQ * (RL + 1)], scope=scope)
            ties = sb("ties", [P, CL], scope=scope)
            hits = marks[:, 0:CL]
            one = sb("one", [P, 1], scope=scope)
            cand, kth, bit, keep = [sb(n, [P, 1], I32, scope) for n in ("cand", "kth", "bit", "keep")]
            count, n_gt, need = [sb(n, [P, 1], scope=scope) for n in ("count", "n_gt", "need")]
            sw2_sb = sb("sw2_sb", [H + 1, D], scope=scope)
            sb1_sb = sb("sb1_sb", [H, 1], scope=scope)
            hid = [sb(f"hid3{b}", [H + 1, TRI * P], scope=scope) for b in range(2)]
            tmp = [sb(f"tmp3{b}", [P, (TRI - 1) * D], scope=scope) for b in range(2)]
            ps_shared, ps_turn, ps_count = [bank[0:3], bank[3:6]], bank[5:8], bank[6]

            def is_last(t):
                return t.static and t.n == NTRI - 1

            @block.sync
            def _(sp):
                sp.dma_start(sw2_sb[0:H, :], sw2).then_inc(c3_in, 16)
                sp.dma_start(sw2_sb[H:H + 1, :], sb2).then_inc(c3_in, 16)
                sp.dma_start(sb1_sb[:], sb1).then_inc(c3_in, 16)

                def step(k):
                    t = k + 2
                    if t.within(NTRI):
                        b, tokens = t.half, P if is_last(t) else TRI * P
                        sp.wait_ge(shared, t.freed)
                        alone(sp)
                        sp.dma_start(hid[b][0:H, 0:tokens], hidden_d[:, bass.ds(t.n * (TRI * P), tokens)]).then_inc(h_in[b], 16)
                    if k.within(NTRI):
                        sp.wait_ge(added_dve, k.done)
                        if is_last(k):
                            sp.dma_start(out[(NT - 1) * P:N, :], nodes[0:TAIL, (NT - 1) * D:NT * D]).then_inc(out_stored, 16)
                        else:
                            sp.wait_ge(added_pool, k.done)
                            alone(sp)
                            sp.dma_start(out[bass.ds(k.n * (TRI * P), TRI * P), :].rearrange("(a p) n -> p a n", p=P),
                                         nodes[:, bass.ds(k.n * (TRI * D), TRI * D)].rearrange("p (a n) -> p a n", a=TRI)).then_inc(out_stored, 16)

                for_tiles(sp, NTRI, 2, 0, step)
                sp.wait_ge(fin_dve, 14)
                for c in range(CH):
                    sp.dma_start(rank_d[:, c * RQ:(c + 1) * RQ, :].rearrange("e q l -> e (q l)"),
                                 marks[c * E:(c + 1) * E, :]).then_inc(rank_stored, 16)
                sp.wait_ge(out_stored, 16 * NTRI)
                sp.wait_ge(rank_stored, 16 * CH)

            @block.gpsimd
            def _(pool):
                credit(pool, added_pool)
                pool.wait_ge(p3_dve, 2)
                nc.gpsimd.affine_select(out=earlier_c[:], in_=same_e[:], compare_op=ALU.is_gt, fill=0.0, base=0,
                                        pattern=[[1, P]], channel_multiplier=-1).then_inc(p3_pool, 1)
                pool.wait_ge(p3_dve, 7)
                nc.gpsimd.affine_select(out=prob[:, NT - 1, :], in_=prob[:, NT - 1, :], compare_op=ALU.is_ge, fill=-1.0,
                                        base=TAIL - 1, pattern=[[0, E]], channel_multiplier=-1).then_inc(p3_pool, 1)
                pool.wait_ge(p3_pool, 2)
                pool.dma_start(table.rearrange("(t p) w -> p t w", p=P)[:, :, D:TW], prob[:, 0:NT, :]).then_inc(prob_stored, 16)

                def step(k):
                    if k.within(NTRI - 1):
                        rest = nodes[:, bass.ds(k.n * (TRI * D) + D, (TRI - 1) * D)]
                        pool.wait_ge(copied, k.done)
                        nc.gpsimd.tensor_tensor(rest, rest, tmp[k.half][:], ALU.add).then_inc(added_pool, 1)

                for_tiles(pool, NTRI - 1, 0, 0, step)
                pool.wait_ge(prob_stored, 16)

            @block.scalar
            def _(act):
                credit(act, h_gelu, copied)
                act.wait_ge(p3_dve, 4)
                nc.scalar.activation(prob[:, 0:NT, :], lg[:, 0:NT, :], ACT.Exp).then_inc(p3_act, 1)
                act.wait_ge(c3_in, 48)
                act.wait_ge(p3_pool, 2)
                nc.scalar.copy(ties[:].rearrange("p (j c e) -> p j c e", j=TPC, c=CH),
                               prob[:].rearrange("p (c j) e -> p j c e", j=TPC)).then_inc(p3_act, 1)
                for j in range(0, TPC, TURN):
                    n = min(TURN, TPC - j)
                    act.wait_ge(p3_pe, j // TURN + 1)
                    nc.scalar.copy(search[:, j * P:(j + n) * P], ps_turn[j // TURN][:, 0:n * P]).then_inc(p3_act, 1)

                def step(k):
                    t = k + 1
                    if t.within(NTRI):
                        b, tokens = t.half, P if is_last(t) else TRI * P
                        act.wait_ge(h_in[b], t.landed)
                        nc.scalar.activation(hid[b][0:H, 0:tokens], hid[b][0:H, 0:tokens], ACT.Gelu_apprx_tanh,
                                             bias=sb1_sb[:]).then_inc(h_gelu, 1)
                    if k.within(NTRI - 1):
                        b = k.half
                        act.wait_ge(shared, k.done)
                        act.wait_ge(added_pool, k.freed)
                        for j in range(1, TRI):
                            ins = nc.scalar.copy(tmp[b][:, (j - 1) * D:j * D], ps_shared[b][j][:])
                        ins.then_inc(copied, 1)

                for_tiles(act, NTRI, 2, 0, step)

            @block.vector
            def _(dve):
                credit(dve, added_dve)
                for s in (kth_ready, bit_ready, keep_ready):
                    dve.sem_inc(s, 1)
                step_n = [0]

                def chain(ins, s=p3_dve):
                    step_n[0] += 1
                    ins.then_inc(s, 1)
                    dve.wait_ge(s, step_n[0])

                for h in hid:
                    nc.vector.memset(h[H:H + 1, :], 1.0)
                nc.vector.memset(one[:], 1.0)
                nc.vector.memset(kth[:], 0)
                nc.vector.memset(bit[:], 1 << (BITS - 1))
                nc.vector.memset(prob[:, NT:, :], -1.0)
                nc.vector.memset(keep[:], 0)
                chain(nc.vector.tensor_reduce(mine[:], ident[:].rearrange("p (c e) -> p e c", e=E), AX_X, ALU.add))
                chain(nc.vector.tensor_copy(same_e[:].rearrange("p (c e) -> p c e", e=E), mine[:].unsqueeze(1).to_broadcast([P, CH, E])))
                chain(nc.vector.tensor_reduce(stat[:], lg[:, 0:NT, :], AX_X, ALU.max))
                chain(nc.vector.tensor_tensor(lg[:, 0:NT, :], lg[:, 0:NT, :], stat[:].unsqueeze(2).to_broadcast([P, NT, E]), ALU.subtract))
                dve.wait_ge(p3_act, 1)
                chain(nc.vector.tensor_reduce(stat[:], prob[:, 0:NT, :], AX_X, ALU.add))
                chain(nc.vector.reciprocal(stat[:], stat[:]))
                chain(nc.vector.tensor_tensor(prob[:, 0:NT, :], prob[:, 0:NT, :], stat[:].unsqueeze(2).to_broadcast([P, NT, E]), ALU.mult))
                dve.wait_ge(p3_act, 5)

                def count_reached(n):
                    dve.wait_ge(kth_ready, n + 1)
                    dve.wait_ge(bit_ready, n + 1)
                    nc.vector.tensor_tensor(cand[:], kth[:], bit[:], ALU.bitwise_or).then_inc(cand_ready, 1)
                    dve.wait_ge(cand_ready, n + 1)
                    dve.wait_ge(total_ready, n + 1)
                    nc.vector.tensor_scalar(hits, search[:], cand[:].bitcast(F32), 0.0, ALU.is_ge, ALU.add,
                                            accum_out=count[:]).then_inc(count_ready, 1)
                    nc.vector.tensor_scalar(bit[:], bit[:], 1, None, ALU.logical_shift_right).then_inc(bit_ready, 1)

                def keep_bit(n):
                    dve.wait_ge(total_ready, n + 2)
                    nc.vector.tensor_scalar(keep[:], ps_count[:, 0:1], CAP - 0.5, None, ALU.is_ge).then_inc(keep_ready, 1)
                    dve.wait_ge(keep_ready, n + 2)
                    alone(dve)
                    nc.vector.copy_predicated(kth[:], keep[:], cand[:]).then_inc(kth_ready, 1)

                def step(k):
                    if k.within(NTRI):
                        count_reached(k.n)
                        dve.wait_ge(shared, k.done)
                        first = nodes[:, bass.ds(k.n * (TRI * D), D)]
                        nc.vector.tensor_tensor(first, first, ps_shared[k.half][0][:], ALU.add).then_inc(added_dve, 1)
                        keep_bit(k.n)

                for_tiles(dve, NTRI, 0, 0, step)
                for n in range(NTRI, BITS):
                    count_reached(n)
                    keep_bit(n)
                dve.wait_ge(kth_ready, BITS + 1)
                step_n[0] = 0
                kth_f = kth[:].bitcast(F32)

                def fin(ins):
                    chain(ins, fin_dve)

                def scan(out_, in_, start):
                    return nc.vector.tensor_tensor_scan(out_, one[:].to_broadcast([P, CL]), in_, start, ALU.mult, ALU.add)

                fin(nc.vector.tensor_scalar(hits, search[:], kth_f, 0.0, ALU.is_gt, ALU.add, accum_out=n_gt[:]))
                fin(nc.vector.tensor_scalar(search[:], search[:], kth_f, None, ALU.is_equal))
                fin(scan(ties[:], search[:], 0.0))
                fin(nc.vector.tensor_copy(count[:], ties[:, CL - 1:CL]))
                dve.wait_ge(fin_pe, 2)
                fin(nc.vector.tensor_scalar(need[:], ps_count[:, 4:5], -1.0, float(CAP), ALU.mult, ALU.add))
                fin(nc.vector.tensor_tensor(need[:], need[:], ps_count[:, 8:9], ALU.subtract))
                fin(nc.vector.scalar_tensor_tensor(search[:], ties[:], need[:], search[:], ALU.is_le, ALU.mult))
                fin(nc.vector.tensor_tensor(hits, hits, search[:], ALU.add))
                fin(nc.vector.tensor_reduce(count[:], hits, AX_X, ALU.add))
                dve.wait_ge(fin_pe, 3)
                fin(nc.vector.tensor_copy(need[:], ps_count[:, 12:13]))
                fin(scan(ties[:], hits, need[:]))
                row = marks[:].rearrange("p (q l) -> p q l", q=RQ)
                row_ties = ties[:].rearrange("p (q l) -> p q l", q=RQ)
                fin(nc.vector.tensor_copy(row[:, :, 1:RL + 1], row_ties))
                fin(nc.vector.tensor_copy(row[:, 1:RQ, 0:1], row_ties[:, 0:RQ - 1, RL - 1:RL]))
                fin(nc.vector.tensor_copy(marks[:, 0:1], need[:]))

            @block.tensor
            def _(pe):
                credit(pe, shared)
                pe.sem_inc(total_ready, 1)
                pe.wait_ge(p3_act, 2)
                for j in range(TPC):
                    turn = nc.tensor.transpose(ps_turn[j // TURN][:, j % TURN * P:(j % TURN + 1) * P],
                                               ties[:, j * P:(j + 1) * P], ident[:])
                    if j % TURN == TURN - 1 or j == TPC - 1:
                        turn.then_inc(p3_pe, 1)
                pe.wait_ge(p3_act, 5)
                pe.wait_ge(c3_in, 48)

                def total(n):
                    pe.wait_ge(count_ready, n + 1)
                    pe.wait_ge(keep_ready, n + 1)
                    nc.tensor.matmul(ps_count[:, 0:1], same_e[:], count[:], start=True, stop=True).then_inc(total_ready, 1)

                def step(k):
                    if k.within(NTRI):
                        b = k.half
                        pe.wait_ge(h_gelu, k.done)
                        pe.wait_ge(added_dve, k.freed)
                        pe.wait_ge(copied, k.freed)
                        for j in range(1 if is_last(k) else TRI):
                            mm = nc.tensor.matmul(ps_shared[b][j][:], hid[b][:, j * P:(j + 1) * P], sw2_sb[:], start=True, stop=True)
                        mm.then_inc(shared, 1)
                        total(k.n)

                for_tiles(pe, NTRI, 0, 0, step)
                for n in range(NTRI, BITS):
                    total(n)
                pe.wait_ge(fin_dve, 4)
                pe.wait_ge(keep_ready, BITS + 1)
                nc.tensor.matmul(ps_count[:, 4:5], same_e[:], n_gt[:], start=True, stop=True).then_inc(fin_pe, 1)
                nc.tensor.matmul(ps_count[:, 8:9], earlier_c[:], count[:], start=True, stop=True).then_inc(fin_pe, 1)
                pe.wait_ge(fin_dve, 9)
                nc.tensor.matmul(ps_count[:, 12:13], earlier_c[:], count[:], start=True, stop=True).then_inc(fin_pe, 1)

        logit_scope.close()
        nodes_scope.close()
        we_in, rank_in, tok_in, added = pair_of("we_in"), pair_of("rank_in"), pair_of("tok_in"), pair_of("added")
        c4_pool, c4_dve = sem("c4_pool"), sem("c4_dve")
        started, in_row, row_picked, tok_cmp, tok_sum, tok_idx_ready, add_idx_ready, score_ready = [
            sem(s) for s in ("started", "in_row", "row_picked", "tok_cmp", "tok_sum", "tok_idx_ready", "add_idx_ready", "score_ready")]
        e_turned, e_turned_sb, e_hidden, e_gelu, e_out, e_scaled = [
            sem(s) for s in ("e_turned", "e_turned_sb", "e_hidden", "e_gelu", "e_out", "e_scaled")]
        G = SLOT_G
        NA = min(D // SLOT_P * SLOT_P, CAP - SLOT_P)

        class Item:

            def __init__(self, k, g):
                self.half = (k.half * G + g) % 2
                self.done = k.n * G + (g + 1 + 2 * G)
                self.freed = k.n * G + (g - 1 + 2 * G)
                self.expert_freed = k.n * G + G

        def all_landed(k):
            return (k.pair + 1) * (16 * G)

        def all_landed_before(k):
            return k.pair * (16 * G)

        with ExitStack() as scope, nc.Block() as block:
            def two(name, shape, dt=F32):
                return [sb(f"{name}{b}", shape, dt, scope) for b in range(2)]

            slot = sb("slot", [SLOT_P, G], scope=scope)
            slots = sb("slots", [P, CAP], scope=scope)
            cmp_tok = sb("cmp_tok", [SLOT_P, G, RL], scope=scope)
            ge_start, row_of = sb("ge_start", [P, CAP], scope=scope), two("row_of", [P, CAP])
            n_tok = two("n_tok", [SLOT_P, G])
            tok_idx, add_idx = two("tok_idx", [SLOT_P, G], I32), two("add_idx", [SLOT_P, G], I32)
            ranks = two("ranks", [P, RL + 2])
            toks, score = two("toks", [SLOT_P, G, TW]), two("score", [SLOT_P, G])
            w1_sb, w2_sb, b1_sb = two("w1_sb", [P, DC, H]), two("w2_sb", [H + 1, D]), two("b1_sb", [H, 1])
            tokT, hT, y = two("tokT", [P, DC, CAP]), two("hT", [H + 1, CAP]), two("y", [SLOT_P, G, D])
            ps_turn, ps_hid, ps_out, ps_row = bank[0:2], bank[2:4], bank[4:6], bank[6]
            row_view = ps_row[0:SLOT_P, 0:G * (RL + 1)].rearrange("p (g l) -> p g l", g=G)

            @block.sync
            def _(sp):
                def step(k):
                    t = k + 4
                    if t.within(E):
                        b = t.half
                        sp.wait_ge(row_picked, t.freed)
                        sp.wait_ge(in_row, t.freed)
                        alone(sp)
                        sp.dma_start(ranks[b][:, 0:RL + 1], rank_d[bass.ds(t.n, 1)].rearrange("a r l -> (a r) l")).then_inc(rank_in[b], 16)
                    t = k + 1
                    if t.within(E):
                        b, e = t.half, bass.ds(t.n, 1)
                        sp.wait_ge(e_out, Item(t, 0).expert_freed)
                        sp.dma_start(w1_sb[b][:], w1[e].rearrange("a (c p) h -> p (a c) h", p=P)).then_inc(we_in[b], 16)
                        sp.dma_start(w2_sb[b][0:H, :], w2[e].rearrange("a h n -> (a h) n")).then_inc(we_in[b], 16)
                        sp.dma_start(w2_sb[b][H:H + 1, :], b2[e, :]).then_inc(we_in[b], 16)
                        sp.dma_start(b1_sb[b][:], b1[e].rearrange("a h o -> (a h) o")).then_inc(we_in[b], 16)

                for_tiles(sp, E, 4, 0, step)

            @block.gpsimd
            def _(pool):
                nc.gpsimd.iota(slots[:], pattern=[[1, CAP]], base=0, channel_multiplier=0,
                               allow_small_or_imprecise_dtypes=True).then_inc(c4_pool, 1)
                nc.gpsimd.iota(slot[:], pattern=[[SLOT_P, G]], base=0, channel_multiplier=1,
                               allow_small_or_imprecise_dtypes=True).then_inc(c4_pool, 1)
                for b in range(2):
                    nc.gpsimd.iota(ranks[b][:, RL + 1:RL + 2], pattern=[[0, 1]], base=0, channel_multiplier=RL,
                                   allow_small_or_imprecise_dtypes=True).then_inc(c4_pool, 1)

                def step(k):
                    t = k + 2
                    if t.within(E):
                        b = t.half
                        pool.wait_ge(tok_idx_ready, t.done)
                        pool.wait_ge(e_turned, Item(t, 0).expert_freed)
                        pool.wait_ge(score_ready, t.freed)
                        alone(pool)
                        for g in range(G):
                            nc.gpsimd.indirect_dma_start(
                                toks[b][:, g, :], None, table, bass.IndirectOffsetOnAxis(tok_idx[b][:, g:g + 1], 0),
                            ).then_inc(tok_in[b], 16)
                    if k.within(E):
                        b = k.half
                        pool.wait_ge(e_scaled, Item(k, G - 1).done)
                        pool.wait_ge(add_idx_ready, k.done)
                        t = k + -1
                        if not (k.static and k.n == 0):
                            pool.wait_ge(added[t.half], all_landed(t))
                        alone(pool)
                        for g in range(G):
                            nc.gpsimd.indirect_dma_start(
                                out, bass.IndirectOffsetOnAxis(add_idx[b][:, g:g + 1], 0), y[b][:, g, :], None,
                                compute_op=ALU.add).then_inc(added[b], 16)

                for_tiles(pool, E, 2, 1, step)
                for t in (At((E - 2) // 2, (E - 2) % 2), At((E - 1) // 2, (E - 1) % 2)):
                    pool.wait_ge(added[t.half], all_landed(t))

            @block.scalar
            def _(act):
                act.sem_inc(e_turned_sb, 2 * G)
                credit(act, e_gelu)

                def step(k):
                    if k.within(E):
                        b = k.half
                        act.wait_ge(we_in[b], (k.pair + 1) * 64)
                        act.wait_ge(e_hidden, k.done)
                        act.wait_ge(e_out, Item(k, 0).expert_freed)
                        nc.scalar.activation(hT[b][0:H, 0:NA], ps_hid[0][0:H, 0:NA], ACT.Gelu_apprx_tanh, bias=b1_sb[b][:])
                        nc.scalar.activation(hT[b][0:H, NA:CAP], ps_hid[1][0:H, 0:CAP - NA], ACT.Gelu_apprx_tanh,
                                             bias=b1_sb[b][:]).then_inc(e_gelu, 1)
                    t = k + 1
                    if t.within(E):
                        for g in range(G):
                            it = Item(t, g)
                            act.wait_ge(e_turned, it.done)
                            act.wait_ge(e_hidden, t.freed)
                            nc.scalar.copy(tokT[t.half][:, :, g * SLOT_P:(g + 1) * SLOT_P],
                                           ps_turn[it.half][:].rearrange("p (c q) -> p c q", c=DC)[:, :, 0:SLOT_P]).then_inc(e_turned_sb, 1)

                for_tiles(act, E, 1, 1, step)

            @block.vector
            def _(dve):
                credit(dve, started, in_row, tok_cmp, tok_sum, tok_idx_ready, add_idx_ready, score_ready)
                dve.sem_inc(e_scaled, 2 * G)
                for b in range(2):
                    nc.vector.memset(hT[b][H:H + 1, :], 1.0).then_inc(c4_dve, 1)
                dve.wait_ge(c4_dve, 2)
                dve.wait_ge(c4_pool, 4)

                def step(k):
                    if k.within(E):
                        dve.wait_ge(added[k.half], all_landed_before(k))
                        nc.vector.tensor_copy(add_idx[k.half][:], tok_idx[k.half][:]).then_inc(add_idx_ready, 1)
                    t = k + 2
                    if t.within(E):
                        b = t.half
                        dve.wait_ge(row_picked, t.done)
                        nc.vector.tensor_tensor(cmp_tok[:], row_view[:, :, 0:RL], slot[:].unsqueeze(2).to_broadcast([SLOT_P, G, RL]),
                                                ALU.is_le).then_inc(tok_cmp, 1)
                        dve.wait_ge(tok_cmp, t.done)
                        nc.vector.tensor_reduce(n_tok[b][:], cmp_tok[:], AX_X, ALU.add).then_inc(tok_sum, 1)
                        dve.wait_ge(tok_sum, t.done)
                        dve.wait_ge(add_idx_ready, t.freed)
                        dve.wait_ge(tok_in[b], all_landed_before(t))
                        nc.vector.tensor_tensor(tok_idx[b][:], row_view[:, :, RL:RL + 1].rearrange("p g o -> p (g o)"), n_tok[b][:],
                                                ALU.add).then_inc(tok_idx_ready, 1)
                    t = k + 3
                    if t.within(E):
                        b = t.half
                        dve.wait_ge(rank_in[b], t.landed)
                        nc.vector.tensor_scalar(ge_start[:], slots[:], ranks[b][:, 0:1], None, ALU.is_ge).then_inc(started, 1)
                        dve.wait_ge(started, t.done)
                        dve.wait_ge(row_picked, t.freed)
                        nc.vector.scalar_tensor_tensor(row_of[b][:], slots[:], ranks[b][:, RL:RL + 1], ge_start[:],
                                                       ALU.is_lt, ALU.mult).then_inc(in_row, 1)
                    if k.within(E):
                        b = k.half
                        dve.wait_ge(e_scaled, Item(k, 0).expert_freed)
                        dve.wait_ge(tok_in[b], all_landed(k))
                        nc.vector.tensor_copy(score[b][:], toks[b][:, :, bass.ds(k.n + D, 1)].rearrange("p g o -> p (g o)")).then_inc(score_ready, 1)
                        dve.wait_ge(score_ready, k.done)
                        for g in range(G):
                            it = Item(k, g)
                            dve.wait_ge(e_out, it.done)
                            nc.vector.tensor_scalar(y[b][:, g, :], ps_out[it.half][0:SLOT_P, :], score[b][:, g:g + 1], None,
                                                    ALU.mult).then_inc(e_scaled, 1)

                for_tiles(dve, E, 3, 1, step)

            @block.tensor
            def _(pe):
                credit(pe, e_hidden, row_picked)
                pe.sem_inc(e_turned, 2 * G)
                pe.sem_inc(e_out, 2 * G)
                pe.wait_ge(c4_pool, 4)
                pe.wait_ge(c4_dve, 2)

                def step(k):
                    if k.within(E):
                        b = k.half
                        pe.wait_ge(we_in[b], (k.pair + 1) * 64)
                        pe.wait_ge(e_turned_sb, Item(k, G - 1).done)
                        pe.wait_ge(e_gelu, k.done - 1)
                        for bank_, lo, hi in ((ps_hid[0], 0, NA), (ps_hid[1], NA, CAP)):
                            for c in range(DC):
                                mm = nc.tensor.matmul(bank_[0:H, 0:hi - lo], w1_sb[b][:, c, :], tokT[b][:, c, lo:hi],
                                                      start=(c == 0), stop=(c == DC - 1))
                        mm.then_inc(e_hidden, 1)
                    t = k + 1
                    if t.within(E):
                        for g in range(G):
                            it = Item(t, g)
                            pe.wait_ge(tok_in[t.half], all_landed(t))
                            pe.wait_ge(e_turned_sb, it.freed)
                            for c in range(DC):
                                mm = nc.tensor.transpose(ps_turn[it.half][:, c * P:c * P + SLOT_P],
                                                         toks[t.half][:, g, c * P:(c + 1) * P], ident[0:SLOT_P, 0:SLOT_P])
                            mm.then_inc(e_turned, 1)
                    if k.within(E):
                        b = k.half
                        pe.wait_ge(e_gelu, k.done)
                        for g in range(G):
                            it = Item(k, g)
                            pe.wait_ge(e_scaled, it.freed)
                            nc.tensor.matmul(ps_out[it.half][0:SLOT_P, :], hT[b][:, g * SLOT_P:(g + 1) * SLOT_P], w2_sb[b][:],
                                             start=True, stop=True).then_inc(e_out, 1)
                    t = k + 3
                    if t.within(E):
                        b = t.half
                        pe.wait_ge(in_row, t.done)
                        pe.wait_ge(tok_idx_ready, t.done - 1)
                        for g in range(G):
                            mm = nc.tensor.matmul(ps_row[0:SLOT_P, g * (RL + 1):(g + 1) * (RL + 1)],
                                                  row_of[b][:, g * SLOT_P:(g + 1) * SLOT_P], ranks[b][:, 1:RL + 2], start=True, stop=True)
                        mm.then_inc(row_picked, 1)

                for_tiles(pe, E, 3, 1, step)


def kernel(**inputs):
    import numpy as _np
    import concourse.bacc as _bacc
    from concourse import mybir as _mybir
    from concourse.bass_utils import run_bass_kernel_spmd as _run

    a = {name.replace("L0_gnn_", "").replace("L0_ffn_", "ffn_"): _np.asarray(v) for name, v in inputs.items()}
    n, d = a["x"].shape
    tiles = -(-n // 128)
    pad = tiles * 128 - n
    src = _np.concatenate([a["src"], _np.zeros(pad, a["src"].dtype)]).reshape(tiles, 128).T
    dst = _np.concatenate([a["dst"], _np.full(pad, n, a["dst"].dtype)])
    laid = {
        "x": a["x"], "src": src, "dst": dst, "dst_c": dst.reshape(tiles, 128).T, "edge_attr": a["edge_attr_512"],
        "Wm": a["Wm"], "bm": a["bm"].reshape(-1, 128).T, "WuT": a["Wu"].T, "bu": a["bu"],
        "gamma": a["gamma"], "beta": a["beta"], "gate": a["ffn_gate_w"],
        "w1": a["ffn_w1"], "b1": a["ffn_b1"].reshape(*a["ffn_b1"].shape, 1), "w2": a["ffn_w2"], "b2": a["ffn_b2"],
        "sw1": a["ffn_sw1"], "sb1": a["ffn_sb1"].reshape(-1, 1), "sw2": a["ffn_sw2"], "sb2": a["ffn_sb2"].reshape(1, -1),
    }
    nc = _bacc.Bacc("TRN2", target_bir_lowering=False, num_devices=1)
    arrays, args = {}, []
    for name, v in laid.items():
        v = _np.ascontiguousarray(v)
        arrays[f"in_{name}"] = v
        args.append(nc.dram_tensor(f"in_{name}", v.shape, _mybir.dt.from_np(v.dtype), kind="ExternalInput").ap())
    args.append(nc.dram_tensor("out_0", (n, d), _mybir.dt.float32, kind="ExternalOutput").ap())
    gnn_then_expert_choice_ffn(nc, *args)
    r = _run(nc, [arrays], core_ids=[0])
    return r.results[0]["out_0"]
```

```python
from contextlib import ExitStack

import concourse.bass as bass
from concourse import mybir

P = 128
ALU = mybir.AluOpType
ACT = mybir.ActivationFunctionType
F32 = mybir.dt.float32
I32 = mybir.dt.int32
BF16 = mybir.dt.bfloat16
AX_X = mybir.AxisListType.X
EPS = 1e-5
CREDIT = 2


class At:

    def __init__(self, pair, half):
        self.pair, self.half = pair, half

    def __add__(self, d):
        return At(self.pair + (self.half + d) // 2, (self.half + d) % 2)

    @property
    def n(self):
        return self.pair * 2 + self.half

    @property
    def static(self):
        return isinstance(self.pair, int)

    def within(self, count):
        return not self.static or 0 <= self.n < count

    @property
    def done(self):
        return self.n + CREDIT + 1

    @property
    def freed(self):
        return self.n + 1

    @property
    def landed(self):
        return (self.pair + 1) * 16

    @property
    def landed_before(self):
        return self.pair * 16


def alone(eng):
    eng.nop(nofuse=True)


def for_tiles(eng, count, lead, lag, step, start=None, pairs=2):
    start = -lead if start is None else start
    first = max((lag + 1) // 2, (start + 1) // 2)
    end = first + ((count - lead) // 2 - first) // pairs * pairs
    for k in range(start, 2 * first):
        step(At(k // 2, k % 2))
    with eng.Fori(0, (end - first) // pairs) as i:
        for p in range(pairs):
            step(At(i * pairs + (first + p), 0))
            step(At(i * pairs + (first + p), 1))
    for k in range(2 * end, count + lag):
        step(At(k // 2, k % 2))


def gnn_then_expert_choice_ffn(nc, x, src, dst, dst_c, edge_attr, WmN, bm, WuT, bu, gamma, beta,
                               gate, w1, b1, w2, b2, sw1, sb1, sw2, sb2, out):
    N, D = x.shape
    EDGES = edge_attr.shape[0]
    DC = D // P
    _, NT = src.shape
    TAIL = N - (NT - 1) * P
    assert EDGES == N and NT * P >= N
    E, _, H = w1.shape
    CAP = N // E
    SLOT_P = 125
    SLOT_G = CAP // SLOT_P
    assert SLOT_P * SLOT_G == CAP and D == DC * P
    TOK = NT * P
    CH = P // E
    TPC = -(-NT // CH)
    CL = TPC * P
    RQ = P // CH
    RL = CL // RQ
    assert RQ * RL == CL
    AW = D + 1
    TW = D + E
    AROWS = P * (N // P + 2)
    ZERO_ROWS = 4
    assert AROWS // P % ZERO_ROWS == 0
    ZEROED = 16 * (AROWS // P // ZERO_ROWS)
    TRASH = N + 1
    assert TRASH + P <= AROWS

    agg = nc.dram_tensor("agg", (AROWS, AW), F32, kind="Internal").ap()
    fused_w_d = nc.dram_tensor("fused_w_d", (P, DC * D), F32, kind="Internal").ap()
    fused_b3_d = nc.dram_tensor("fused_b3_d", (3, D), BF16, kind="Internal").ap()
    table = nc.dram_tensor("table", (TOK, TW), F32, kind="Internal").ap()
    hidden_d = nc.dram_tensor("hidden_d", (P, NT * H), F32, kind="Internal").ap()
    rank_d = nc.dram_tensor("rank_d", (E, P, RL + 1), F32, kind="Internal").ap()

    with ExitStack() as whole:
        def sb(name, shape, dt=F32, scope=whole):
            return scope.enter_context(nc.sbuf_tensor(name, shape, dt))

        def sem(name):
            return whole.enter_context(nc.semaphore(name))

        def pair_of(name):
            return [sem(f"{name}0"), sem(f"{name}1")]

        bank = [whole.enter_context(nc.psum_tensor(f"bank{i}", [P, 512], F32)) for i in range(8)]

        ident = sb("ident", [P, P])
        neg_half = sb("neg_half", [P, 1])
        nodes_scope = whole.enter_context(ExitStack())
        nodes = sb("nodes", [P, NT * D], scope=nodes_scope)

        x_stat_scope = whole.enter_context(ExitStack())
        x_stat = sb("x_stat", [P, NT, 2], scope=x_stat_scope)

        def x_stat_of(t):
            return x_stat[:, bass.ds(t.n, 1), :].rearrange("p o s -> p (o s)")

        def node_slot(t):
            return nodes[:, bass.ds(t.n * D, D)]

        def rows(ap, t, last):
            return ap[(NT - 1) * P:(NT - 1) * P + TAIL, :] if last else ap[bass.ds(t.n * P, P), :]

        FILLS = AROWS // P // ZERO_ROWS
        FILLS_FIRST = 8
        NODES_AHEAD = 10
        fill_at = {n - NODES_AHEAD - 1: [] for n in range(NODES_AHEAD + 1)}
        for n in range(FILLS - FILLS_FIRST):
            fill_at[n * len(fill_at) // (FILLS - FILLS_FIRST) - NODES_AHEAD - 1].append(n + FILLS_FIRST)
        zeros = nodes[:, NT * D - AW:NT * D]

        def fill_zeros(act, part_):
            r = part_ * ZERO_ROWS
            act.dma_start(agg.rearrange("(p r) w -> p r w", p=P)[:, r:r + ZERO_ROWS, :],
                          zeros.unsqueeze(1).to_broadcast([P, ZERO_ROWS, AW])).then_inc(zeros_done, 16)

        zeros_done, const_in, fused_stored = sem("zeros_done"), sem("const_in"), sem("fused_stored")
        p0_pool, p0_dve, p0_pe, fused_copied, parts_ready = [sem(s) for s in ("p0_pool", "p0_dve", "p0_pe", "fused_copied", "parts_ready")]
        x_in = pair_of("x_in")
        w1_in = sem("w1_in")
        p1_scope = whole.enter_context(ExitStack())
        wul_sb = sb("wul_sb", [P, DC, D], scope=p1_scope)
        bu_sb = sb("bu_sb", [P, D], scope=p1_scope)
        src_col = sb("src_col", [P, NT], I32, p1_scope)
        dst_col = sb("dst_col", [P, NT], I32, p1_scope)
        x_t = [sb(f"x_t{b}", [P, D], scope=p1_scope) for b in range(2)]
        with ExitStack() as scope, nc.Block() as block:
            bm_col = sb("bm_col", [P, DC], scope=scope)
            bm_wide = sb("bm_wide", [P, DC, P], scope=scope)
            wm_sb = nodes[:, 0:DC * D].rearrange("p (c n) -> p c n", c=DC)
            wur_sb = nodes[:, DC * D:2 * DC * D].rearrange("p (c n) -> p c n", c=DC)
            fused_sb = nodes[:, 2 * DC * D:3 * DC * D].rearrange("p (c n) -> p c n", c=DC)
            fused_b_sb = nodes[:, 3 * DC * D:3 * DC * D + D]
            parts_at = 3 * DC * D + D
            part = [nodes[0:1, parts_at + n * D // 2:parts_at + (n + 1) * D // 2].bitcast(BF16) for n in range(3)]
            rest = [sb(f"rest{n}", [1, D], scope=scope) for n in range(2)]

            @block.sync
            def _(sp):
                sp.dma_start(wm_sb, WmN.rearrange("(c p) n -> p c n", p=P)).then_inc(const_in, 16)
                sp.dma_start(wur_sb, WuT[D:2 * D, :].rearrange("(c p) n -> p c n", p=P)).then_inc(const_in, 16)
                sp.dma_start(bm_col[:], bm).then_inc(const_in, 16)
                sp.dma_start(src_col[:], src).then_inc(w1_in, 16)
                sp.dma_start(dst_col[:], dst_c).then_inc(w1_in, 16)
                sp.dma_start(wul_sb[:], WuT[0:D, :].rearrange("(c p) n -> p c n", p=P)).then_inc(w1_in, 16)
                sp.dma_start(bu_sb[:], bu.partition_broadcast(P)).then_inc(w1_in, 16)
                for b in range(2):
                    sp.dma_start(x_t[b][:], x[b * P:(b + 1) * P, :]).then_inc(x_in[b], 16)
                sp.wait_ge(fused_copied, DC)
                sp.dma_start(fused_w_d, nodes[:, 2 * DC * D:3 * DC * D]).then_inc(fused_stored, 16)
                sp.wait_ge(parts_ready, 5)
                for n in range(3):
                    sp.dma_start(fused_b3_d[n:n + 1, :], part[n]).then_inc(fused_stored, 16)

            @block.gpsimd
            def _(pool):
                nc.gpsimd.memset(ident[:], 0.0).then_inc(p0_pool, 1)
                nc.gpsimd.memset(neg_half[:], -0.5)
                pool.wait_ge(p0_pool, 1)
                nc.gpsimd.affine_select(out=ident[:], in_=ident[:], compare_op=ALU.not_equal, fill=1.0, base=0,
                                        pattern=[[-1, P]], channel_multiplier=1).then_inc(p0_pool, 1)

            @block.scalar
            def _(act):
                act.wait_ge(p0_dve, 1)
                act.wait_ge(const_in, 48)
                for part_ in range(FILLS_FIRST):
                    fill_zeros(act, part_)

            @block.vector
            def _(dve):
                nc.vector.memset(zeros, 0.0).then_inc(p0_dve, 1)
                dve.wait_ge(const_in, 48)
                nc.vector.tensor_copy(bm_wide[:], bm_col[:].unsqueeze(2).to_broadcast([P, DC, P])).then_inc(p0_dve, 1)
                for c in range(DC + 1):
                    dve.wait_ge(p0_pe, c + 1)
                    nc.vector.tensor_copy(fused_sb[:, c, :] if c < DC else fused_b_sb, bank[c][:]).then_inc(fused_copied, 1)
                left_over = fused_b_sb[0:1, :]
                dve.wait_ge(fused_copied, DC + 1)
                for n in range(3):
                    nc.vector.tensor_copy(part[n], left_over).then_inc(parts_ready, 1)
                    if n < 2:
                        dve.wait_ge(parts_ready, 2 * n + 1)
                        nc.vector.tensor_tensor(rest[n][:], left_over, part[n], ALU.subtract).then_inc(parts_ready, 1)
                        dve.wait_ge(parts_ready, 2 * n + 2)
                        left_over = rest[n][:]
                dve.wait_ge(w1_in, 64)
                nc.vector.tensor_tensor(bu_sb[:], bu_sb[:], fused_b_sb, ALU.add).then_inc(p0_dve, 1)

            @block.tensor
            def _(pe):
                pe.wait_ge(const_in, 48)
                for c in range(DC):
                    for j in range(DC):
                        last = nc.tensor.matmul(bank[c][:], wm_sb[:, j, c * P:(c + 1) * P], wur_sb[:, j, :],
                                                start=(j == 0), stop=(j == DC - 1))
                    last.then_inc(p0_pe, 1)
                pe.wait_ge(p0_dve, 2)
                for j in range(DC):
                    last = nc.tensor.matmul(bank[DC][:], bm_wide[:, j, :], wur_sb[:, j, :], start=(j == 0), stop=(j == DC - 1))
                last.then_inc(p0_pe, 1)

        xg_in, ea_in, dr_in = pair_of("xg_in"), pair_of("ea_in"), pair_of("dr_in")
        scattered = pair_of("scattered")
        p1_const = sem("p1_const")
        src_picked = sem("src_picked")
        x_raw, x_stats, x_eps, x_rstd = sem("x_raw"), sem("x_stats"), sem("x_eps"), sem("x_rstd")
        g_raw, g_stats, g_eps, g_rstd = sem("g_raw"), sem("g_stats"), sem("g_eps"), sem("g_rstd")
        x_kept, x_norm, x_turned, x_turned_sb = sem("x_kept"), sem("x_norm"), sem("x_turned"), sem("x_turned_sb")
        g_norm, msg_ready, same_ready, earlier = sem("g_norm"), sem("msg_ready"), sem("same_ready"), sem("earlier")
        idx_step, idx_ready = sem("idx_step"), sem("idx_ready")
        sums, sums_sb, left, left_sb = sem("sums"), sem("sums_sb"), sem("left"), sem("left_sb")

        def rstd_on_pool(pool, t, stats, stats_done, eps_sem, out_sem, bias_sem=None):
            pool.wait_ge(stats_done, t.done)
            alone(pool)
            nc.gpsimd.tensor_scalar(stats[:, 1:2], stats[:, 1:2], EPS, None, ALU.add).then_inc(eps_sem, 1)
            pool.wait_ge(eps_sem, t.done)
            alone(pool)
            nc.gpsimd.tensor_tensor(stats[:, 1:2], stats[:, 1:2], neg_half[:], ALU.pow).then_inc(out_sem, 1)
            if bias_sem is not None:
                pool.wait_ge(out_sem, t.done)
                alone(pool)
                nc.gpsimd.tensor_scalar(stats[:, 2:3], stats[:, 0:1], stats[:, 1:2], -1.0, ALU.mult, ALU.mult).then_inc(bias_sem, 1)

        def credit(eng, *sems):
            for s in sems:
                eng.sem_inc(s, CREDIT)

        with ExitStack() as scope, nc.Block() as block:
            def two(name, shape, dt=F32):
                return [sb(f"{name}{b}", shape, dt, scope) for b in range(2)]

            dst_f = sb("dst_f", [P, NT], scope=scope)
            to_trash = sb("to_trash", [P, NT], scope=scope)
            trash_row = sb("trash_row", [P, 1], scope=scope)
            before = sb("before", [P, P], scope=scope)
            xg, ea = two("xg", [P, D]), two("ea", [P, D])
            dst_row = two("dst_row", [P, P], I32)
            src_idx, dst_idx = two("src_idx", [P, 1], I32), two("dst_idx", [P, 1], I32)
            xs6, gs6 = two("xs6", [P, 6]), two("gs6", [P, 6])
            xs, gs = two("xs", [P, 2]), two("gs", [P, 2])
            xn, msg, xT = two("xn", [P, D]), two("msg", [P, D]), two("xT", [P, D])
            same, prior, n_prior, moved = two("same", [P, P]), sb("prior", [P, P], scope=scope), two("n_prior", [P, 1]), two("moved", [P, 1], I32)
            sum_sb, degree = two("sum_sb", [P, AW]), two("degree", [P, 1])
            ps_turn, ps_left, ps_sum = bank[0:2], bank[2:4], bank[4:6]

            @block.sync
            def _(sp):
                def loads(t):
                    ahead = t + NODES_AHEAD
                    if ahead.within(NT) and not (ahead.static and ahead.n < 2):
                        node_rows(ahead)
                    if t.within(NT):
                        edge_rows(t)

                def node_rows(t):
                    last = t.static and t.n == NT - 1
                    sp.wait_ge(x_norm, t.freed)
                    sp.dma_start(x_t[t.half][0:TAIL if last else P, :], rows(x, t, last)).then_inc(x_in[t.half], 16)

                def edge_rows(t):
                    last = t.static and t.n == NT - 1
                    r = TAIL if last else P
                    sp.wait_ge(same_ready, t.freed)
                    alone(sp)
                    sp.dma_start(dst_row[t.half][:], dst[bass.ds(t.n * P, P)].partition_broadcast(P)).then_inc(dr_in[t.half], 16)
                    sp.wait_ge(msg_ready, t.freed)
                    sp.dma_start(ea[t.half][0:r, :], rows(edge_attr, t, last)).then_inc(ea_in[t.half], 16)

                for_tiles(sp, NT, NODES_AHEAD + 1, 0, loads)

            @block.gpsimd
            def _(pool):
                nc.gpsimd.memset(before[:], 1.0).then_inc(p1_const, 1)
                nc.gpsimd.iota(trash_row[:], pattern=[[0, 1]], base=TRASH, channel_multiplier=1,
                               allow_small_or_imprecise_dtypes=True).then_inc(p1_const, 1)
                pool.wait_ge(p1_const, 1)
                nc.gpsimd.affine_select(out=before[:], in_=before[:], compare_op=ALU.is_gt, fill=0.0, base=0,
                                        pattern=[[-1, P]], channel_multiplier=1).then_inc(p1_const, 1)
                credit(pool, idx_ready, src_picked, x_eps, x_rstd, g_eps, g_rstd)

                def step(k):
                    t = k + 2
                    if t.within(NT):
                        pool.wait_ge(xg_in[t.half], t.landed_before)
                        nc.gpsimd.tensor_copy(src_idx[t.half][:], src_col[:, bass.ds(t.n, 1)]).then_inc(src_picked, 1)
                        pool.wait_ge(src_picked, t.done)
                        pool.wait_ge(g_norm, t.freed)
                        alone(pool)
                        nc.gpsimd.indirect_dma_start(
                            xg[t.half][:], None, x, bass.IndirectOffsetOnAxis(src_idx[t.half][:], 0),
                        ).then_inc(xg_in[t.half], 16)
                    t = k + -1
                    if t.within(NT):
                        pool.wait_ge(idx_step, t.done)
                        pool.wait_ge(scattered[t.half], t.landed_before)
                        nc.gpsimd.tensor_tensor(dst_idx[t.half][:], moved[t.half][:], dst_col[:, bass.ds(t.n, 1)], ALU.add).then_inc(idx_ready, 1)
                        pool.wait_ge(sums_sb, t.done)
                        pool.wait_ge(idx_ready, t.done)
                        if t.static and t.n == 0:
                            pool.wait_ge(zeros_done, ZEROED)
                        else:
                            before_t = t + -1
                            pool.wait_ge(scattered[before_t.half], before_t.landed)
                        alone(pool)
                        nc.gpsimd.indirect_dma_start(
                            agg, bass.IndirectOffsetOnAxis(dst_idx[t.half][:], 0), sum_sb[t.half][:], None,
                            compute_op=ALU.add).then_inc(scattered[t.half], 16)
                    t = k + 1
                    if t.within(NT):
                        rstd_on_pool(pool, t, gs[t.half], g_stats, g_eps, g_rstd)
                    t = k + (NODES_AHEAD + 2)
                    if t.within(NT):
                        rstd_on_pool(pool, t, xs[t.half], x_stats, x_eps, x_rstd)

                for_tiles(pool, NT, NODES_AHEAD + 2, 2, step)
                for t in (At((NT - 2) // 2, (NT - 2) % 2), At((NT - 1) // 2, (NT - 1) % 2)):
                    pool.wait_ge(scattered[t.half], t.landed)

            @block.scalar
            def _(act):
                credit(act, x_turned_sb, sums_sb, x_kept)

                def step(k):
                    if k.static and k.n in fill_at:
                        for part_ in fill_at[k.n]:
                            fill_zeros(act, part_)
                    t = k + (NODES_AHEAD + 1)
                    if t.within(NT):
                        act.wait_ge(x_rstd, t.done)
                        nc.scalar.copy(x_stat_of(t), xs[t.half][:]).then_inc(x_kept, 1)
                    t = k + -1
                    if t.within(NT):
                        act.wait_ge(sums, t.done)
                        act.wait_ge(scattered[t.half], t.landed_before)
                        nc.scalar.copy(sum_sb[t.half][:, D:D + 1], degree[t.half][:])
                        nc.scalar.copy(sum_sb[t.half][:, 0:D], ps_sum[t.half][:]).then_inc(sums_sb, 1)
                    t = k + (NODES_AHEAD + 1)
                    if t.within(NT):
                        act.wait_ge(x_turned, t.done)
                        act.wait_ge(left, t.freed)
                        nc.scalar.copy(xT[t.half][:], ps_turn[t.half][:]).then_inc(x_turned_sb, 1)

                for_tiles(act, NT, NODES_AHEAD + 1, 4, step)

            @block.vector
            def _(dve):
                credit(dve, x_raw, x_stats, g_raw, g_stats, x_norm, g_norm, msg_ready, same_ready, earlier, idx_step, left_sb)
                dve.wait_ge(p1_const, 3)
                nc.vector.tensor_copy(dst_f[:], dst_col[:]).then_inc(p1_const, 1)
                dve.wait_ge(p1_const, 4)
                nc.vector.tensor_scalar(to_trash[:], dst_f[:], -1.0, trash_row[:], ALU.mult, ALU.add).then_inc(p1_const, 1)
                dve.wait_ge(p1_const, 5)

                def raw_stats(t, data, arrived, six, raw):
                    dve.wait_ge(arrived[t.half], t.landed)
                    alone(dve)
                    nc.vector.bn_stats(six[t.half][:], data[t.half][:]).then_inc(raw, 1)

                def stats(t, six, raw, into, stats_done, free):
                    dve.wait_ge(raw, t.done)
                    for s in free:
                        dve.wait_ge(s, t.freed)
                    alone(dve)
                    nc.vector.bn_aggr(into[:, 0:2], six[t.half][:]).then_inc(stats_done, 1)

                def step(k):
                    t = k + 1
                    b, column = t.half, bass.ds(t.n, 1)
                    if k.within(NT):
                        dve.wait_ge(g_rstd, k.done)
                        dve.wait_ge(sums, k.freed)
                        nc.vector.tensor_scalar(msg[k.half][:], xg[k.half][:], gs[k.half][:, 0:1], gs[k.half][:, 1:2],
                                                ALU.subtract, ALU.mult).then_inc(g_norm, 1)
                    ahead = t + NODES_AHEAD
                    if ahead.within(NT):
                        a = ahead.half
                        dve.wait_ge(x_rstd, ahead.done)
                        dve.wait_ge(x_turned, ahead.freed)
                        nc.vector.tensor_scalar(xn[a][:], x_t[a][:], xs[a][:, 0:1], xs[a][:, 1:2],
                                                ALU.subtract, ALU.mult).then_inc(x_norm, 1)
                    if k.within(NT):
                        dve.wait_ge(g_norm, k.done)
                        dve.wait_ge(ea_in[k.half], k.landed)
                        nc.vector.tensor_tensor(msg[k.half][:], msg[k.half][:], ea[k.half][:], ALU.add).then_inc(msg_ready, 1)
                    if t.within(NT):
                        raw_stats(t, xg, xg_in, gs6, g_raw)
                    t2 = k + (NODES_AHEAD + 2)
                    if t2.within(NT):
                        raw_stats(t2, x_t, x_in, xs6, x_raw)
                    if t.within(NT):
                        dve.wait_ge(dr_in[b], t.landed)
                        dve.wait_ge(sums, t.freed)
                        dve.wait_ge(sums_sb, t.freed)
                        nc.vector.tensor_scalar(same[b][:], dst_row[b][:], dst_f[:, column], 0.0, ALU.is_equal, ALU.add,
                                                accum_out=degree[b][:]).then_inc(same_ready, 1)
                    if t.within(NT):
                        stats(t, gs6, g_raw, gs[t.half], g_stats, [g_norm])
                    if t2.within(NT):
                        stats(t2, xs6, x_raw, xs[t2.half], x_stats, [x_norm, x_kept])
                    if t.within(NT):
                        dve.wait_ge(same_ready, t.done)
                        nc.vector.tensor_tensor_reduce(out=prior[:], in0=same[b][:], in1=before[:], scale=1.0, scalar=0.0,
                                                       op0=ALU.mult, op1=ALU.add, accum_out=n_prior[b][:]).then_inc(earlier, 1)
                    prev = k + (NODES_AHEAD - 1)
                    if prev.within(NT):
                        dve.wait_ge(left, prev.done)
                        if prev.static and prev.n == 0:
                            dve.wait_ge(fused_stored, 64)
                        nc.vector.tensor_tensor(node_slot(prev), ps_left[prev.half][:], bu_sb[:], ALU.add).then_inc(left_sb, 1)
                    if t.within(NT):
                        dve.wait_ge(earlier, t.done)
                        dve.wait_ge(idx_ready, t.freed)
                        nc.vector.tensor_scalar(moved[b][:], n_prior[b][:], 1.0, to_trash[:, column], ALU.min, ALU.mult).then_inc(idx_step, 1)

                for_tiles(dve, NT, NODES_AHEAD + 2, 4, step)

            @block.tensor
            def _(pe):
                credit(pe, x_turned, left, sums)

                def step(k):
                    t = k + (NODES_AHEAD + 1)
                    if t.within(NT):
                        pe.wait_ge(x_norm, t.done)
                        pe.wait_ge(x_turned_sb, t.freed)
                        for c in range(DC):
                            mm = nc.tensor.transpose(ps_turn[t.half][:, c * P:(c + 1) * P], xn[t.half][:, c * P:(c + 1) * P], ident[:])
                        mm.then_inc(x_turned, 1)
                    t = k + NODES_AHEAD
                    if t.within(NT):
                        b = t.half
                        pe.wait_ge(x_turned_sb, t.done)
                        pe.wait_ge(left_sb, t.freed)
                        for c in range(DC):
                            mm = nc.tensor.matmul(ps_left[b][:], xT[b][:, c * P:(c + 1) * P], wul_sb[:, c, :],
                                                  start=(c == 0), stop=(c == DC - 1))
                        mm.then_inc(left, 1)
                    b = k.half
                    if k.within(NT):
                        pe.wait_ge(msg_ready, k.done)
                        pe.wait_ge(same_ready, k.done)
                        pe.wait_ge(sums_sb, k.freed)
                        nc.tensor.matmul(ps_sum[b][:], same[b][:], msg[b][:], start=True, stop=True).then_inc(sums, 1)

                for_tiles(pe, NT, NODES_AHEAD + 1, 0, step)

        p1_scope.close()

        c2_in = sem("c2_in")
        ag_in, y_in, xr_in = pair_of("ag_in"), pair_of("y_in"), pair_of("xr_in")
        table_stored, hidden_stored = pair_of("table_stored"), pair_of("hidden_stored")
        ag_turned, ag_turned_sb, upd = sem("ag_turned"), sem("ag_turned_sb"), sem("upd")
        deg_max, deg_inv, deg_turned, no_edge_ready = sem("deg_max"), sem("deg_inv"), sem("deg_turned"), sem("no_edge_ready")
        y_bias, y_norm = sem("y_bias"), sem("y_norm")
        o_raw, o_stats, o_eps, o_rstd = [sem(f"o_{s}") for s in ("raw", "stats", "eps", "rstd")]
        z_raw, z_stats, z_eps, z_rstd, z_bias = [sem(f"z_{s}") for s in ("raw", "stats", "eps", "rstd", "bias")]
        u_ready, u_gelu, o_ready, o_gamma, x1_ready, res_ready = [sem(s) for s in ("u_ready", "u_gelu", "o_ready", "o_gamma", "x1_ready", "res_ready")]
        z_norm, z_turned, z_turned_sb, heads, hidden_sb = [
            sem(s) for s in ("z_norm", "z_turned", "z_turned_sb", "heads", "hidden_sb")]

        logit_scope = whole.enter_context(ExitStack())
        lg = sb("lg", [P, NT, E], scope=logit_scope)
        with ExitStack() as scope, nc.Block() as block:
            def two(name, shape, dt=F32):
                return [sb(f"{name}{b}", shape, dt, scope) for b in range(2)]

            fused_sb = sb("fused_sb", [P, DC, D], scope=scope)
            fused_b3 = sb("fused_b3", [3, D], BF16, scope)
            no_edge = two("no_edge", [3, P], BF16)
            gamma_sb, beta_sb = [sb(n, [P, D], scope=scope) for n in ("gamma_sb", "beta_sb")]
            heads_sb = sb("heads_sb", [P, DC, H + E], scope=scope)
            ag, agT = two("ag", [P, AW]), sb("agT", [P, D], scope=scope)
            y_t, yn, res = two("y_t", [P, D]), two("yn", [P, D]), two("res", [P, D])
            upd_sb, z, zT = two("upd_sb", [P, D]), two("z", [P, D]), sb("zT", [P, D], scope=scope)
            deg = two("deg", [P, 2])
            os6, zs6 = two("os6", [P, 6]), two("zs6", [P, 6])
            os_, zs = two("os_", [P, 2]), two("zs", [P, 3])
            hid = two("hid", [P, H])
            ps_agT, ps_upd, ps_zT, ps_heads, ps_deg = bank[0], bank[1:3], bank[3], bank[4:6], bank[6:8]

            @block.sync
            def _(sp):
                sp.dma_start(fused_sb[:].rearrange("p c n -> p (c n)"), fused_w_d).then_inc(c2_in, 16)
                sp.dma_start(fused_b3[:], fused_b3_d).then_inc(c2_in, 16)
                sp.dma_start(gamma_sb[:], gamma.partition_broadcast(P)).then_inc(c2_in, 16)
                sp.dma_start(beta_sb[:], beta.partition_broadcast(P)).then_inc(c2_in, 16)
                sp.dma_start(heads_sb[:, :, 0:H], sw1.rearrange("(c p) n -> p c n", p=P)).then_inc(c2_in, 16)
                sp.dma_start(heads_sb[:, :, H:H + E], gate.rearrange("(c p) n -> p c n", p=P)).then_inc(c2_in, 16)

                def step(k):
                    t = k + -3
                    if t.within(NT):
                        sp.wait_ge(z_norm, t.done)
                        sp.dma_start(table[bass.ds(t.n * P, P), 0:D], z[t.half][:]).then_inc(table_stored[t.half], 16)
                    t = k
                    if t.within(NT):
                        last = t.static and t.n == NT - 1
                        sp.wait_ge(x1_ready, t.freed)
                        sp.dma_start(res[t.half][0:TAIL if last else P, :], rows(x, t, last)).then_inc(xr_in[t.half], 16)
                    t = k + 3
                    if t.within(NT):
                        sp.wait_ge(ag_turned, t.freed)
                        sp.wait_ge(deg_turned, t.freed)
                        sp.wait_ge(deg_max, t.freed)
                        alone(sp)
                        sp.dma_start(ag[t.half][:], agg[bass.ds(t.n * P, P), :]).then_inc(ag_in[t.half], 16)
                    t = k + 2
                    if t.within(NT):
                        last = t.static and t.n == NT - 1
                        sp.wait_ge(y_norm, t.freed)
                        sp.dma_start(y_t[t.half][0:TAIL if last else P, :], rows(x, t, last)).then_inc(y_in[t.half], 16)
                    t = k + -6
                    if t.within(NT):
                        sp.wait_ge(hidden_sb, t.done)
                        sp.dma_start(hidden_d[:, bass.ds(t.n * H, H)], hid[t.half][:]).then_inc(hidden_stored[t.half], 16)

                for_tiles(sp, NT, 4, 6, step)
                for t in (At((NT - 2) // 2, (NT - 2) % 2), At((NT - 1) // 2, (NT - 1) % 2)):
                    for s in (table_stored, hidden_stored):
                        sp.wait_ge(s[t.half], t.landed)

            @block.gpsimd
            def _(pool):
                credit(pool, o_ready, o_eps, o_rstd, z_eps, z_rstd, z_bias, res_ready)
                pool.wait_ge(c2_in, 96)

                def step(k):
                    t = k + -1
                    if t.within(NT):
                        b = t.half
                        pool.wait_ge(xr_in[b], t.landed)
                        nc.gpsimd.tensor_tensor(res[b][:], res[b][:], beta_sb[:], ALU.add).then_inc(res_ready, 1)
                    t = k + -1
                    if t.within(NT):
                        pool.wait_ge(u_gelu, t.done)
                        pool.wait_ge(y_norm, t.done)
                        nc.gpsimd.tensor_tensor(upd_sb[t.half][:], upd_sb[t.half][:], yn[t.half][:], ALU.add).then_inc(o_ready, 1)
                    t = k + -2
                    if t.within(NT):
                        rstd_on_pool(pool, t, zs[t.half], z_stats, z_eps, z_rstd, z_bias)
                    t = k + -1
                    if t.within(NT):
                        rstd_on_pool(pool, t, os_[t.half], o_stats, o_eps, o_rstd)

                for_tiles(pool, NT, 0, 2, step)

            @block.scalar
            def _(act):
                act.wait_ge(y_bias, 1)
                credit(act, y_norm, u_gelu, ag_turned_sb, z_norm, z_turned_sb, hidden_sb)

                def step(k):
                    t = k + -5
                    if t.within(NT):
                        act.wait_ge(z_turned, t.done)
                        act.wait_ge(heads, t.done - 1)
                        nc.scalar.copy(zT[:], ps_zT[:]).then_inc(z_turned_sb, 1)
                    t = k + -3
                    if t.within(NT):
                        act.wait_ge(z_bias, t.done)
                        act.wait_ge(z_turned, t.freed)
                        act.wait_ge(table_stored[t.half], t.landed_before)
                        nc.scalar.activation(z[t.half][:], node_slot(t), ACT.Identity, bias=zs[t.half][:, 2:3],
                                             scale=zs[t.half][:, 1:2]).then_inc(z_norm, 1)
                    t = k + -1
                    if t.within(NT):
                        act.wait_ge(u_ready, t.done)
                        nc.scalar.activation(upd_sb[t.half][:], upd_sb[t.half][:], ACT.Gelu).then_inc(u_gelu, 1)
                    t = k + 1
                    if t.within(NT):
                        act.wait_ge(ag_turned, t.done)
                        act.wait_ge(upd, t.done - 1)
                        nc.scalar.copy(agT[:], ps_agT[:]).then_inc(ag_turned_sb, 1)
                    t = k
                    if t.within(NT):
                        act.wait_ge(y_in[t.half], t.landed)
                        act.wait_ge(o_ready, t.freed)
                        nc.scalar.activation(yn[t.half][:], y_t[t.half][:], ACT.Identity, bias=x_stat_of(t)[:, 0:1],
                                             scale=x_stat_of(t)[:, 1:2]).then_inc(y_norm, 1)
                    t = k + -5
                    if t.within(NT):
                        act.wait_ge(heads, t.done)
                        act.wait_ge(hidden_stored[t.half], t.landed_before)
                        nc.scalar.copy(lg[:, bass.ds(t.n, 1), :].rearrange("p a e -> p (a e)"), ps_heads[t.half][:, H:H + E])
                        nc.scalar.copy(hid[t.half][:], ps_heads[t.half][:, 0:H]).then_inc(hidden_sb, 1)

                for_tiles(act, NT, 1, 7, step)

            @block.vector
            def _(dve):
                credit(dve, o_raw, o_stats, z_raw, z_stats, deg_max, deg_inv, no_edge_ready,
                       u_ready, o_gamma, x1_ready)
                dve.wait_ge(c2_in, 96)
                nc.vector.scalar_tensor_tensor(x_stat[:, :, 0], x_stat[:, :, 0], -1.0, x_stat[:, :, 1],
                                               ALU.mult, ALU.mult).then_inc(y_bias, 1)

                def raw_stats(t, data, six, raw):
                    alone(dve)
                    nc.vector.bn_stats(six[t.half][:], data).then_inc(raw, 1)

                def stats(t, six, raw, two_, stats_done, free):
                    dve.wait_ge(raw, t.done)
                    dve.wait_ge(free, t.freed)
                    alone(dve)
                    nc.vector.bn_aggr(two_[t.half][:, 0:2], six[t.half][:]).then_inc(stats_done, 1)

                def step(k):
                    t = k + -1
                    if t.within(NT):
                        b = t.half
                        dve.wait_ge(upd, t.done)
                        dve.wait_ge(deg_inv, t.done)
                        dve.wait_ge(x1_ready, t.freed)
                        nc.vector.scalar_tensor_tensor(upd_sb[b][:], ps_upd[b][:], deg[b][:, 1:2], node_slot(t),
                                                       ALU.mult, ALU.add).then_inc(u_ready, 1)
                    t = k + -2
                    if t.within(NT):
                        b = t.half
                        dve.wait_ge(o_rstd, t.done)
                        nc.vector.scalar_tensor_tensor(upd_sb[b][:], upd_sb[b][:], os_[b][:, 0:1], gamma_sb[:],
                                                       ALU.subtract, ALU.mult).then_inc(o_gamma, 1)
                        dve.wait_ge(o_gamma, t.done)
                        dve.wait_ge(res_ready, t.done)
                        nc.vector.scalar_tensor_tensor(node_slot(t), upd_sb[b][:], os_[b][:, 1:2], res[b][:],
                                                       ALU.mult, ALU.add).then_inc(x1_ready, 1)
                    t = k + -2
                    if t.within(NT):
                        dve.wait_ge(x1_ready, t.done)
                        raw_stats(t, node_slot(t), zs6, z_raw)
                    t = k + 1
                    if t.within(NT):
                        b = t.half
                        dve.wait_ge(deg_turned, t.done)
                        dve.wait_ge(upd, t.freed)
                        nc.vector.tensor_scalar(no_edge[b][:], ps_deg[b][0:3, 0:P], 0.0, -1.0, ALU.is_equal, ALU.mult).then_inc(no_edge_ready, 1)
                        dve.wait_ge(u_ready, t.freed)
                        nc.vector.tensor_scalar(deg[b][:, 0:1], ag[b][:, D:D + 1], 1.0, None, ALU.max).then_inc(deg_max, 1)
                    t = k + -2
                    if t.within(NT):
                        stats(t, zs6, z_raw, zs, z_stats, z_norm)
                    t = k + 1
                    if t.within(NT):
                        dve.wait_ge(deg_max, t.done)
                        nc.vector.reciprocal(deg[t.half][:, 1:2], deg[t.half][:, 0:1]).then_inc(deg_inv, 1)
                    t = k + -1
                    if t.within(NT):
                        dve.wait_ge(o_ready, t.done)
                        raw_stats(t, upd_sb[t.half][:], os6, o_raw)
                    t = k + -1
                    if t.within(NT):
                        stats(t, os6, o_raw, os_, o_stats, x1_ready)

                for_tiles(dve, NT, 1, 4, step)

            @block.tensor
            def _(pe):
                credit(pe, ag_turned, deg_turned, upd, z_turned, heads)
                pe.wait_ge(c2_in, 96)

                def step(k):
                    t = k + 1
                    if t.within(NT):
                        b = t.half
                        pe.wait_ge(ag_in[b], t.landed)
                        pe.wait_ge(ag_turned_sb, t.done - 1)
                        for c in range(DC):
                            mm = nc.tensor.transpose(ps_agT[:, c * P:(c + 1) * P], ag[b][:, c * P:(c + 1) * P], ident[:])
                        mm.then_inc(ag_turned, 1)
                        pe.wait_ge(no_edge_ready, t.freed)
                        nc.tensor.transpose(ps_deg[b][0:3, 0:P], ag[b][:, D:D + 1].to_broadcast([P, 3]), ident[:]).then_inc(deg_turned, 1)
                    if k.within(NT):
                        b = k.half
                        pe.wait_ge(ag_turned_sb, k.done)
                        pe.wait_ge(u_ready, k.freed)
                        for c in range(DC):
                            nc.tensor.matmul(ps_upd[b][:], agT[:, c * P:(c + 1) * P], fused_sb[:, c, :],
                                             start=(c == 0), stop=False)
                        pe.wait_ge(no_edge_ready, k.done)
                        nc.tensor.matmul(ps_upd[b][:], no_edge[b][:], fused_b3[:], start=False, stop=True).then_inc(upd, 1)
                    t = k + -5
                    if t.within(NT):
                        b = t.half
                        pe.wait_ge(z_turned_sb, t.done)
                        pe.wait_ge(hidden_sb, t.freed)
                        for c in range(DC):
                            mm = nc.tensor.matmul(ps_heads[b][:, 0:H + E], zT[:, c * P:(c + 1) * P], heads_sb[:, c, :],
                                                  start=(c == 0), stop=(c == DC - 1))
                        mm.then_inc(heads, 1)
                    t = k + -4
                    if t.within(NT):
                        pe.wait_ge(z_norm, t.done)
                        pe.wait_ge(z_turned_sb, t.done - 1)
                        for c in range(DC):
                            mm = nc.tensor.transpose(ps_zT[:, c * P:(c + 1) * P], z[t.half][:, c * P:(c + 1) * P], ident[:])
                        mm.then_inc(z_turned, 1)

                for_tiles(pe, NT, 1, 5, step)

        BITS = 30
        TRI = 3
        NTRI = -(-NT // TRI)
        assert NT == (NTRI - 1) * TRI + 1 and NTRI < BITS
        TURN = 4
        AHEAD = 2
        c3_in, h_in, prob_stored = sem("c3_in"), pair_of("h_in"), sem("prob_stored")
        p3_sw2 = sem("p3_sw2")
        p3_pool, p3_dve, p3_act, p3_pe = sem("p3_pool"), sem("p3_dve"), sem("p3_act"), sem("p3_pe")
        cand_ready, count_ready, total_ready, keep_ready, bit_ready, kth_ready = [
            sem(s) for s in ("cand_ready", "count_ready", "total_ready", "keep_ready", "bit_ready", "kth_ready")]
        h_turned, h_gelu, shared, added_dve, added_pool, copied, out_stored = [
            sem(s) for s in ("h_turned", "h_gelu", "shared", "added_dve", "added_pool", "copied", "out_stored")]
        rank_stored, fin_dve, fin_pe = sem("rank_stored"), sem("fin_dve"), sem("fin_pe")

        TB = CH * TPC
        with ExitStack() as scope, nc.Block() as block:
            prob = sb("prob", [P, TB, E], scope=scope)
            stat = sb("stat", [P, NT], scope=scope)
            mine = sb("mine", [P, E], scope=scope)
            same_e = sb("same_e", [P, P], scope=scope)
            earlier_c = sb("earlier_c", [P, P], scope=scope)
            search = sb("search", [P, CL], scope=scope)
            marks = sb("marks", [P, RQ * (RL + 1)], scope=scope)
            ties = sb("ties", [P, CL], scope=scope)
            hits = marks[:, 0:CL]
            one = sb("one", [P, 1], scope=scope)
            cand, kth, bit, keep = [sb(n, [P, 1], I32, scope) for n in ("cand", "kth", "bit", "keep")]
            count, n_gt, need = [sb(n, [P, 1], scope=scope) for n in ("count", "n_gt", "need")]
            sw2_sb = sb("sw2_sb", [P, D], scope=scope)
            sb1_sb = sb("sb1_sb", [H, 1], scope=scope)
            hid = [sb(f"hid3{b}", [P, TRI * P], scope=scope) for b in range(2)]
            pre = [sb(f"pre3{b}", [P, TRI * H], scope=scope) for b in range(2)]
            tmp = [sb(f"tmp3{b}", [P, (TRI - 1) * D], scope=scope) for b in range(2)]
            ps_shared, ps_count, ps_hidT = [bank[0:3], bank[3:6]], bank[6], bank[7]
            ps_turn = [bank[6], bank[7], bank[6]]

            def is_last(t):
                return t.static and t.n == NTRI - 1

            @block.sync
            def _(sp):
                sp.dma_start(sb1_sb[:], sb1).then_inc(c3_in, 16)
                sp.wait_ge(p3_sw2, 1)
                sp.dma_start(sw2_sb[0:H, :], sw2).then_inc(c3_in, 16)
                sp.dma_start(sw2_sb[H:H + 1, :], sb2).then_inc(c3_in, 16)

                def step(k):
                    t = k + 3
                    if t.within(NTRI):
                        b, cols = t.half, H if is_last(t) else TRI * H
                        sp.wait_ge(h_turned, t.freed)
                        alone(sp)
                        sp.dma_start(pre[b][:, 0:cols], hidden_d[:, bass.ds(t.n * (TRI * H), cols)]).then_inc(h_in[b], 16)
                    t = k + -1
                    if t.within(NTRI):
                        sp.wait_ge(added_dve, t.done)
                        if is_last(t):
                            sp.dma_start(out[(NT - 1) * P:N, :], nodes[0:TAIL, (NT - 1) * D:NT * D]).then_inc(out_stored, 16)
                        else:
                            sp.wait_ge(added_pool, t.done)
                            alone(sp)
                            sp.dma_start(out[bass.ds(t.n * (TRI * P), TRI * P), :].rearrange("(a p) n -> p a n", p=P),
                                         nodes[:, bass.ds(t.n * (TRI * D), TRI * D)].rearrange("p (a n) -> p a n", a=TRI)).then_inc(out_stored, 16)

                for_tiles(sp, NTRI, 4, 1, step)
                sp.wait_ge(fin_dve, 12)
                for c in range(CH):
                    sp.dma_start(rank_d[:, c * RQ:(c + 1) * RQ, :].rearrange("e q l -> e (q l)"),
                                 marks[c * E:(c + 1) * E, :]).then_inc(rank_stored, 16)
                sp.wait_ge(out_stored, 16 * NTRI)
                sp.wait_ge(rank_stored, 16 * CH)

            @block.gpsimd
            def _(pool):
                credit(pool, added_pool)
                pool.wait_ge(p3_dve, 2)
                nc.gpsimd.affine_select(out=earlier_c[:], in_=same_e[:], compare_op=ALU.is_gt, fill=0.0, base=0,
                                        pattern=[[1, P]], channel_multiplier=-1).then_inc(p3_pool, 1)
                pool.wait_ge(p3_dve, 7)
                nc.gpsimd.affine_select(out=prob[:, NT - 1, :], in_=prob[:, NT - 1, :], compare_op=ALU.is_ge, fill=-1.0,
                                        base=TAIL - 1, pattern=[[0, E]], channel_multiplier=-1).then_inc(p3_pool, 1)

                def step(k):
                    if k.within(NTRI - 1):
                        rest = nodes[:, bass.ds(k.n * (TRI * D) + D, (TRI - 1) * D)]
                        pool.wait_ge(copied, k.done)
                        nc.gpsimd.tensor_tensor(rest, rest, tmp[k.half][:], ALU.add).then_inc(added_pool, 1)

                for_tiles(pool, NTRI - 1, 0, 0, step)

            @block.scalar
            def _(act):
                credit(act, h_gelu, copied)
                act.wait_ge(c3_in, 48)

                def gelu(t):
                    b, tokens = t.half, P if is_last(t) else TRI * P
                    act.wait_ge(h_turned, t.done)
                    act.wait_ge(shared, t.freed)
                    nc.scalar.activation(hid[b][0:H, 0:tokens], ps_hidT[0:H, 0:tokens], ACT.Gelu_apprx_tanh,
                                         bias=sb1_sb[:]).then_inc(h_gelu, 1)

                def copies(t):
                    b = t.half
                    act.wait_ge(shared, t.done)
                    act.wait_ge(added_pool, t.freed)
                    for j in range(1, TRI):
                        ins = nc.scalar.copy(tmp[b][:, (j - 1) * D:j * D], ps_shared[b][j][:])
                    ins.then_inc(copied, 1)

                gelu(At(0, 0))
                gelu(At(0, 1))
                act.wait_ge(p3_dve, 4)
                nc.scalar.activation(prob[:, 0:NT, :], lg[:, 0:NT, :], ACT.Exp).then_inc(p3_act, 1)
                copies(At(0, 0))
                gelu(At(1, 0))
                act.wait_ge(p3_pool, 2)
                nc.scalar.copy(ties[:].rearrange("p (j c e) -> p j c e", j=TPC, c=CH),
                               prob[:].rearrange("p (c j) e -> p j c e", j=TPC)).then_inc(p3_act, 1)
                act.dma_start(table.rearrange("(t p) w -> p t w", p=P)[:, :, D:TW], prob[:, 0:NT, :]).then_inc(prob_stored, 16)
                for j in range(0, TPC, TURN):
                    n = min(TURN, TPC - j)
                    act.wait_ge(p3_pe, j // TURN + 1)
                    nc.scalar.copy(search[:, j * P:(j + n) * P], ps_turn[j // TURN][:, 0:n * P]).then_inc(p3_act, 1)
                copies(At(0, 1))

                def step(k):
                    t = k + 1
                    if t.within(NTRI):
                        gelu(t)
                    if k.within(NTRI - 1):
                        copies(k)

                for_tiles(act, NTRI, 2, 0, step, start=AHEAD)
                act.wait_ge(prob_stored, 16)

            @block.vector
            def _(dve):
                credit(dve, added_dve)
                for s in (kth_ready, bit_ready, keep_ready):
                    dve.sem_inc(s, 1)
                step_n = [0]

                def chain(ins, s=p3_dve):
                    step_n[0] += 1
                    ins.then_inc(s, 1)
                    dve.wait_ge(s, step_n[0])

                nc.vector.memset(sw2_sb[:], 0.0).then_inc(p3_sw2, 1)
                for h in hid:
                    nc.vector.memset(h[H:P, :], 1.0)
                nc.vector.memset(one[:], 1.0)
                nc.vector.memset(kth[:], 0)
                nc.vector.memset(bit[:], 1 << (BITS - 1))
                nc.vector.memset(prob[:, NT:, :], -1.0)
                nc.vector.memset(keep[:], 0)
                chain(nc.vector.tensor_reduce(mine[:], ident[:].rearrange("p (c e) -> p e c", e=E), AX_X, ALU.add))
                chain(nc.vector.tensor_copy(same_e[:].rearrange("p (c e) -> p c e", e=E), mine[:].unsqueeze(1).to_broadcast([P, CH, E])))
                chain(nc.vector.tensor_reduce(stat[:], lg[:, 0:NT, :], AX_X, ALU.max))
                chain(nc.vector.tensor_tensor(lg[:, 0:NT, :], lg[:, 0:NT, :], stat[:].unsqueeze(2).to_broadcast([P, NT, E]), ALU.subtract))
                dve.wait_ge(p3_act, 1)
                chain(nc.vector.tensor_reduce(stat[:], prob[:, 0:NT, :], AX_X, ALU.add))
                chain(nc.vector.reciprocal(stat[:], stat[:]))
                chain(nc.vector.tensor_tensor(prob[:, 0:NT, :], prob[:, 0:NT, :], stat[:].unsqueeze(2).to_broadcast([P, NT, E]), ALU.mult))

                def add_first(t):
                    dve.wait_ge(shared, t.done)
                    first = nodes[:, bass.ds(t.n * (TRI * D), D)]
                    nc.vector.tensor_tensor(first, first, ps_shared[t.half][0][:], ALU.add).then_inc(added_dve, 1)

                add_first(At(0, 0))
                dve.wait_ge(p3_act, 5)

                def count_reached(n):
                    dve.wait_ge(kth_ready, n + 1)
                    dve.wait_ge(bit_ready, n + 1)
                    nc.vector.tensor_tensor(cand[:], kth[:], bit[:], ALU.bitwise_or).then_inc(cand_ready, 1)
                    dve.wait_ge(cand_ready, n + 1)
                    dve.wait_ge(total_ready, n + 1)
                    nc.vector.tensor_scalar(hits, search[:], cand[:].bitcast(F32), 0.0, ALU.is_ge, ALU.add,
                                            accum_out=count[:]).then_inc(count_ready, 1)
                    nc.vector.tensor_scalar(bit[:], bit[:], 1, None, ALU.logical_shift_right).then_inc(bit_ready, 1)

                def keep_bit(n):
                    dve.wait_ge(total_ready, n + 2)
                    nc.vector.tensor_scalar(keep[:], ps_count[:, 0:1], CAP - 0.5, None, ALU.is_ge).then_inc(keep_ready, 1)
                    dve.wait_ge(keep_ready, n + 2)
                    alone(dve)
                    nc.vector.copy_predicated(kth[:], keep[:], cand[:]).then_inc(kth_ready, 1)

                def step(k):
                    if k.within(NTRI):
                        count_reached(k.n - AHEAD)
                    t = k + -1
                    if t.within(NTRI):
                        add_first(t)
                    if k.within(NTRI):
                        keep_bit(k.n - AHEAD)

                for_tiles(dve, NTRI, 0, 1, step, start=AHEAD)
                for n in range(NTRI - AHEAD, BITS):
                    count_reached(n)
                    keep_bit(n)
                dve.wait_ge(kth_ready, BITS + 1)
                step_n[0] = 0
                kth_f = kth[:].bitcast(F32)

                def fin(ins):
                    chain(ins, fin_dve)

                def scan(out_, in_, start):
                    return nc.vector.tensor_tensor_scan(out_, one[:].to_broadcast([P, CL]), in_, start, ALU.mult, ALU.add)

                fin(nc.vector.tensor_scalar(hits, search[:], kth_f, 0.0, ALU.is_gt, ALU.add, accum_out=n_gt[:]))
                fin(nc.vector.tensor_scalar(search[:], search[:], kth_f, None, ALU.is_equal))
                fin(scan(ties[:], search[:], 0.0))
                fin(nc.vector.tensor_copy(count[:], ties[:, CL - 1:CL]))
                dve.wait_ge(fin_pe, 2)
                fin(nc.vector.tensor_scalar(need[:], ps_count[:, 4:5], -1.0, float(CAP), ALU.mult, ALU.add))
                fin(nc.vector.tensor_tensor(need[:], need[:], ps_count[:, 8:9], ALU.subtract))
                fin(nc.vector.scalar_tensor_tensor(search[:], ties[:], need[:], search[:], ALU.is_le, ALU.mult))
                fin(nc.vector.tensor_tensor_reduce(out=search[:], in0=hits, in1=search[:], scale=1.0, scalar=0.0, op0=ALU.add,
                                                   op1=ALU.add, accum_out=count[:]))
                dve.wait_ge(fin_pe, 3)
                fin(nc.vector.tensor_copy(need[:], ps_count[:, 12:13]))
                row = marks[:].rearrange("p (q l) -> p q l", q=RQ)
                row_ties = ties[:].rearrange("p (q l) -> p q l", q=RQ)
                fin(scan(ties[:], search[:], need[:]))
                nc.vector.tensor_copy(row[:, 1:RQ, 0:1], row_ties[:, 0:RQ - 1, RL - 1:RL])
                fin(nc.vector.tensor_copy(row[:, :, 1:RL + 1], row_ties))
                fin(nc.vector.tensor_copy(marks[:, 0:1], need[:]))

            @block.tensor
            def _(pe):
                credit(pe, shared, h_turned)
                pe.sem_inc(total_ready, 1)
                def total(n):
                    pe.wait_ge(count_ready, n + 1)
                    pe.wait_ge(keep_ready, n + 1)
                    nc.tensor.matmul(ps_count[:, 0:1], same_e[:], count[:], start=True, stop=True).then_inc(total_ready, 1)

                def turn_hidden(t):
                    pe.wait_ge(h_in[t.half], t.landed)
                    pe.wait_ge(h_gelu, t.done - 1)
                    alone(pe)
                    for j in range(1 if is_last(t) else TRI):
                        mm = nc.tensor.transpose(ps_hidT[0:H, j * P:(j + 1) * P], pre[t.half][:, j * H:(j + 1) * H], ident[:])
                    mm.then_inc(h_turned, 1)

                def second_layer(k):
                    b = k.half
                    pe.wait_ge(h_gelu, k.done)
                    pe.wait_ge(added_dve, k.freed)
                    pe.wait_ge(copied, k.freed)
                    for j in range(1 if is_last(k) else TRI):
                        mm = nc.tensor.matmul(ps_shared[b][j][:], hid[b][:, j * P:(j + 1) * P], sw2_sb[:], start=True, stop=True)
                    mm.then_inc(shared, 1)

                pe.wait_ge(c3_in, 48)
                pe.wait_ge(p3_dve, 1)
                turn_hidden(At(0, 0))
                for k in range(AHEAD):
                    turn_hidden(At(k // 2, k % 2) + 1)
                    second_layer(At(k // 2, k % 2))
                pe.wait_ge(p3_act, 2)
                pe.wait_ge(h_gelu, At(1, 0).done)
                for j in range(TPC):
                    if j == 2 * TURN:
                        pe.wait_ge(p3_act, 3)
                    turn = nc.tensor.transpose(ps_turn[j // TURN][:, j % TURN * P:(j % TURN + 1) * P],
                                               ties[:, j * P:(j + 1) * P], ident[:])
                    if j % TURN == TURN - 1 or j == TPC - 1:
                        turn.then_inc(p3_pe, 1)
                pe.wait_ge(p3_act, 5)

                def step(k):
                    t = k + 1
                    if t.within(NTRI):
                        turn_hidden(t)
                    if k.within(NTRI):
                        second_layer(k)
                        total(k.n - AHEAD)

                for_tiles(pe, NTRI, 2, 0, step, start=AHEAD)
                for n in range(NTRI - AHEAD, BITS):
                    total(n)
                pe.wait_ge(fin_dve, 4)
                pe.wait_ge(keep_ready, BITS + 1)
                nc.tensor.matmul(ps_count[:, 4:5], same_e[:], n_gt[:], start=True, stop=True).then_inc(fin_pe, 1)
                nc.tensor.matmul(ps_count[:, 8:9], earlier_c[:], count[:], start=True, stop=True).then_inc(fin_pe, 1)
                pe.wait_ge(fin_dve, 8)
                nc.tensor.matmul(ps_count[:, 12:13], earlier_c[:], count[:], start=True, stop=True).then_inc(fin_pe, 1)

        logit_scope.close()
        x_stat_scope.close()
        nodes_scope.close()
        we_in, rank_in, tok_in, added = pair_of("we_in"), pair_of("rank_in"), pair_of("tok_in"), pair_of("added")
        c4_pool, c4_dve = sem("c4_pool"), sem("c4_dve")
        started, in_row, row_picked, tok_cmp, tok_sum, tok_idx_ready, add_idx_ready, score_ready = [
            sem(s) for s in ("started", "in_row", "row_picked", "tok_cmp", "tok_sum", "tok_idx_ready", "add_idx_ready", "score_ready")]
        e_turned, e_turned_sb, e_hidden_most, e_hidden, e_gelu, e_out, e_scaled = [
            sem(s) for s in ("e_turned", "e_turned_sb", "e_hidden_most", "e_hidden", "e_gelu", "e_out", "e_scaled")]
        G = SLOT_G
        NA = min(D // SLOT_P * SLOT_P, CAP - SLOT_P)

        class Item:

            def __init__(self, k, g):
                self.half = (k.half * G + g) % 2
                self.done = k.n * G + (g + 1 + 2 * G)
                self.freed = k.n * G + (g - 1 + 2 * G)
                self.expert_freed = k.n * G + G

        def all_landed(k):
            return (k.pair + 1) * (16 * G)

        def all_landed_before(k):
            return k.pair * (16 * G)

        with ExitStack() as scope, nc.Block() as block:
            def two(name, shape, dt=F32):
                return [sb(f"{name}{b}", shape, dt, scope) for b in range(2)]

            slot = sb("slot", [SLOT_P, G], scope=scope)
            slots = sb("slots", [P, CAP], scope=scope)
            cmp_tok = sb("cmp_tok", [SLOT_P, G, RL], scope=scope)
            ge_start, row_of = sb("ge_start", [P, CAP], scope=scope), two("row_of", [P, CAP])
            n_tok = two("n_tok", [SLOT_P, G])
            tok_idx, add_idx = two("tok_idx", [SLOT_P, G], I32), two("add_idx", [SLOT_P, G], I32)
            ranks = two("ranks", [P, RL + 2])
            toks, score = two("toks", [SLOT_P, G, TW]), two("score", [SLOT_P, G])
            w1_sb, w2_sb, b1_sb = two("w1_sb", [P, DC, H]), two("w2_sb", [H + 1, D]), two("b1_sb", [H, 1])
            tokT, hT, y = two("tokT", [P, DC, CAP]), two("hT", [H + 1, CAP]), two("y", [SLOT_P, G, D])
            ps_turn, ps_hid, ps_out, ps_row = bank[0:2], bank[2:4], bank[4:6], bank[6]
            row_view = ps_row[0:SLOT_P, 0:G * (RL + 1)].rearrange("p (g l) -> p g l", g=G)

            @block.sync
            def _(sp):
                def step(k):
                    t = k + 4
                    if t.within(E):
                        b = t.half
                        sp.wait_ge(row_picked, t.freed)
                        sp.wait_ge(in_row, t.freed)
                        alone(sp)
                        sp.dma_start(ranks[b][:, 0:RL + 1], rank_d[bass.ds(t.n, 1)].rearrange("a r l -> (a r) l")).then_inc(rank_in[b], 16)
                    t = k + 1
                    if t.within(E):
                        b, e = t.half, bass.ds(t.n, 1)
                        sp.wait_ge(e_out, Item(t, 0).expert_freed)
                        sp.dma_start(w1_sb[b][:], w1[e].rearrange("a (c p) h -> p (a c) h", p=P)).then_inc(we_in[b], 16)
                        sp.dma_start(w2_sb[b][0:H, :], w2[e].rearrange("a h n -> (a h) n")).then_inc(we_in[b], 16)
                        sp.dma_start(w2_sb[b][H:H + 1, :], b2[e, :]).then_inc(we_in[b], 16)
                        sp.dma_start(b1_sb[b][:], b1[e].rearrange("a h o -> (a h) o")).then_inc(we_in[b], 16)

                for_tiles(sp, E, 4, 0, step)

            @block.gpsimd
            def _(pool):
                nc.gpsimd.iota(slots[:], pattern=[[1, CAP]], base=0, channel_multiplier=0,
                               allow_small_or_imprecise_dtypes=True).then_inc(c4_pool, 1)
                nc.gpsimd.iota(slot[:], pattern=[[SLOT_P, G]], base=0, channel_multiplier=1,
                               allow_small_or_imprecise_dtypes=True).then_inc(c4_pool, 1)
                for b in range(2):
                    nc.gpsimd.iota(ranks[b][:, RL + 1:RL + 2], pattern=[[0, 1]], base=0, channel_multiplier=RL,
                                   allow_small_or_imprecise_dtypes=True).then_inc(c4_pool, 1)

                def step(k):
                    t = k + 2
                    if t.within(E):
                        b = t.half
                        pool.wait_ge(tok_idx_ready, t.done)
                        pool.wait_ge(e_turned, Item(t, 0).expert_freed)
                        pool.wait_ge(score_ready, t.freed)
                        alone(pool)
                        for g in range(G):
                            nc.gpsimd.indirect_dma_start(
                                toks[b][:, g, :], None, table, bass.IndirectOffsetOnAxis(tok_idx[b][:, g:g + 1], 0),
                            ).then_inc(tok_in[b], 16)
                    if k.within(E):
                        b = k.half
                        pool.wait_ge(e_scaled, Item(k, G - 1).done)
                        pool.wait_ge(add_idx_ready, k.done)
                        t = k + -1
                        if not (k.static and k.n == 0):
                            pool.wait_ge(added[t.half], all_landed(t))
                        alone(pool)
                        for g in range(G):
                            nc.gpsimd.indirect_dma_start(
                                out, bass.IndirectOffsetOnAxis(add_idx[b][:, g:g + 1], 0), y[b][:, g, :], None,
                                compute_op=ALU.add).then_inc(added[b], 16)

                for_tiles(pool, E, 2, 1, step)
                for t in (At((E - 2) // 2, (E - 2) % 2), At((E - 1) // 2, (E - 1) % 2)):
                    pool.wait_ge(added[t.half], all_landed(t))

            @block.scalar
            def _(act):
                act.sem_inc(e_turned_sb, 2 * G)
                credit(act, e_gelu)

                def step(k):
                    if k.within(E):
                        b = k.half
                        act.wait_ge(we_in[b], (k.pair + 1) * 64)
                        act.wait_ge(e_hidden_most, k.done)
                        act.wait_ge(e_out, Item(k, 0).expert_freed)
                        nc.scalar.activation(hT[b][0:H, 0:NA], ps_hid[0][0:H, 0:NA], ACT.Gelu_apprx_tanh, bias=b1_sb[b][:])
                        act.wait_ge(e_hidden, k.done)
                        nc.scalar.activation(hT[b][0:H, NA:CAP], ps_hid[1][0:H, 0:CAP - NA], ACT.Gelu_apprx_tanh,
                                             bias=b1_sb[b][:]).then_inc(e_gelu, 1)
                    t = k + 1
                    if t.within(E):
                        for g in range(G):
                            it = Item(t, g)
                            act.wait_ge(e_turned, it.done)
                            act.wait_ge(e_hidden, t.freed)
                            nc.scalar.copy(tokT[t.half][:, :, g * SLOT_P:(g + 1) * SLOT_P],
                                           ps_turn[it.half][:].rearrange("p (c q) -> p c q", c=DC)[:, :, 0:SLOT_P]).then_inc(e_turned_sb, 1)

                for_tiles(act, E, 1, 1, step)

            @block.vector
            def _(dve):
                credit(dve, started, in_row, tok_cmp, tok_sum, tok_idx_ready, add_idx_ready, score_ready)
                dve.sem_inc(e_scaled, 2 * G)
                for b in range(2):
                    nc.vector.memset(hT[b][H:H + 1, :], 1.0).then_inc(c4_dve, 1)
                dve.wait_ge(c4_dve, 2)
                dve.wait_ge(c4_pool, 4)

                def step(k):
                    if k.within(E):
                        dve.wait_ge(added[k.half], all_landed_before(k))
                        nc.vector.tensor_copy(add_idx[k.half][:], tok_idx[k.half][:]).then_inc(add_idx_ready, 1)
                    t = k + 2
                    if t.within(E):
                        b = t.half
                        dve.wait_ge(row_picked, t.done)
                        nc.vector.tensor_tensor(cmp_tok[:], row_view[:, :, 0:RL], slot[:].unsqueeze(2).to_broadcast([SLOT_P, G, RL]),
                                                ALU.is_le).then_inc(tok_cmp, 1)
                        dve.wait_ge(tok_cmp, t.done)
                        nc.vector.tensor_reduce(n_tok[b][:], cmp_tok[:], AX_X, ALU.add).then_inc(tok_sum, 1)
                        dve.wait_ge(tok_sum, t.done)
                        dve.wait_ge(add_idx_ready, t.freed)
                        dve.wait_ge(tok_in[b], all_landed_before(t))
                        nc.vector.tensor_tensor(tok_idx[b][:], row_view[:, :, RL:RL + 1].rearrange("p g o -> p (g o)"), n_tok[b][:],
                                                ALU.add).then_inc(tok_idx_ready, 1)
                    t = k + 3
                    if t.within(E):
                        b = t.half
                        dve.wait_ge(rank_in[b], t.landed)
                        nc.vector.tensor_scalar(ge_start[:], slots[:], ranks[b][:, 0:1], None, ALU.is_ge).then_inc(started, 1)
                        dve.wait_ge(started, t.done)
                        dve.wait_ge(row_picked, t.freed)
                        nc.vector.scalar_tensor_tensor(row_of[b][:], slots[:], ranks[b][:, RL:RL + 1], ge_start[:],
                                                       ALU.is_lt, ALU.mult).then_inc(in_row, 1)
                    if k.within(E):
                        b = k.half
                        dve.wait_ge(e_scaled, Item(k, 0).expert_freed)
                        dve.wait_ge(tok_in[b], all_landed(k))
                        nc.vector.tensor_copy(score[b][:], toks[b][:, :, bass.ds(k.n + D, 1)].rearrange("p g o -> p (g o)")).then_inc(score_ready, 1)
                        dve.wait_ge(score_ready, k.done)
                        for g in range(G):
                            it = Item(k, g)
                            dve.wait_ge(e_out, it.done)
                            nc.vector.tensor_scalar(y[b][:, g, :], ps_out[it.half][0:SLOT_P, :], score[b][:, g:g + 1], None,
                                                    ALU.mult).then_inc(e_scaled, 1)

                for_tiles(dve, E, 3, 1, step)

            @block.tensor
            def _(pe):
                credit(pe, e_hidden_most, e_hidden, row_picked)
                pe.sem_inc(e_turned, 2 * G)
                pe.sem_inc(e_out, 2 * G)
                pe.wait_ge(c4_pool, 4)
                pe.wait_ge(c4_dve, 2)

                def hidden_layer(k):
                    b = k.half
                    pe.wait_ge(we_in[b], (k.pair + 1) * 64)
                    pe.wait_ge(e_turned_sb, Item(k, G - 1).done)
                    pe.wait_ge(e_gelu, k.done - 1)
                    for bank_, lo, hi, ready in ((ps_hid[0], 0, NA, e_hidden_most), (ps_hid[1], NA, CAP, e_hidden)):
                        for c in range(DC):
                            mm = nc.tensor.matmul(bank_[0:H, 0:hi - lo], w1_sb[b][:, c, :], tokT[b][:, c, lo:hi],
                                                  start=(c == 0), stop=(c == DC - 1))
                        mm.then_inc(ready, 1)

                def turn(t, g):
                    it = Item(t, g)
                    pe.wait_ge(tok_in[t.half], all_landed(t))
                    pe.wait_ge(e_turned_sb, it.freed)
                    for c in range(DC):
                        mm = nc.tensor.transpose(ps_turn[it.half][:, c * P:c * P + SLOT_P],
                                                 toks[t.half][:, g, c * P:(c + 1) * P], ident[0:SLOT_P, 0:SLOT_P])
                    mm.then_inc(e_turned, 1)

                def second_layer(k, g):
                    it = Item(k, g)
                    pe.wait_ge(e_gelu, k.done)
                    pe.wait_ge(e_scaled, it.freed)
                    nc.tensor.matmul(ps_out[it.half][0:SLOT_P, :], hT[k.half][:, g * SLOT_P:(g + 1) * SLOT_P], w2_sb[k.half][:],
                                     start=True, stop=True).then_inc(e_out, 1)

                def step(k):
                    if k.within(E):
                        hidden_layer(k)
                    t = k + 1
                    for g in range(G + 2):
                        if g >= 2 and k.within(E):
                            second_layer(k, g - 2)
                        if g < G and t.within(E):
                            turn(t, g)
                    t = k + 3
                    if t.within(E):
                        b = t.half
                        pe.wait_ge(in_row, t.done)
                        pe.wait_ge(tok_idx_ready, t.done - 1)
                        for g in range(G):
                            mm = nc.tensor.matmul(ps_row[0:SLOT_P, g * (RL + 1):(g + 1) * (RL + 1)],
                                                  row_of[b][:, g * SLOT_P:(g + 1) * SLOT_P], ranks[b][:, 1:RL + 2], start=True, stop=True)
                        mm.then_inc(row_picked, 1)

                for_tiles(pe, E, 3, 1, step)


def kernel(**inputs):
    import numpy as _np
    import concourse.bacc as _bacc
    from concourse import mybir as _mybir
    from concourse.bass_utils import run_bass_kernel_spmd as _run

    a = {name.replace("L0_gnn_", "").replace("L0_ffn_", "ffn_"): _np.asarray(v) for name, v in inputs.items()}
    n, d = a["x"].shape
    tiles = -(-n // 128)
    pad = tiles * 128 - n
    src = _np.concatenate([a["src"], _np.zeros(pad, a["src"].dtype)]).reshape(tiles, 128).T
    dst = _np.concatenate([a["dst"], _np.full(pad, n, a["dst"].dtype)])
    laid = {
        "x": a["x"], "src": src, "dst": dst, "dst_c": dst.reshape(tiles, 128).T, "edge_attr": a["edge_attr_512"],
        "Wm": a["Wm"], "bm": a["bm"].reshape(-1, 128).T, "WuT": a["Wu"].T, "bu": a["bu"],
        "gamma": a["gamma"], "beta": a["beta"], "gate": a["ffn_gate_w"],
        "w1": a["ffn_w1"], "b1": a["ffn_b1"].reshape(*a["ffn_b1"].shape, 1), "w2": a["ffn_w2"], "b2": a["ffn_b2"],
        "sw1": a["ffn_sw1"], "sb1": a["ffn_sb1"].reshape(-1, 1), "sw2": a["ffn_sw2"], "sb2": a["ffn_sb2"].reshape(1, -1),
    }
    nc = _bacc.Bacc("TRN2", target_bir_lowering=False, num_devices=1)
    arrays, args = {}, []
    for name, v in laid.items():
        v = _np.ascontiguousarray(v)
        arrays[f"in_{name}"] = v
        args.append(nc.dram_tensor(f"in_{name}", v.shape, _mybir.dt.from_np(v.dtype), kind="ExternalInput").ap())
    args.append(nc.dram_tensor("out_0", (n, d), _mybir.dt.float32, kind="ExternalOutput").ap())
    gnn_then_expert_choice_ffn(nc, *args)
    r = _run(nc, [arrays], core_ids=[0])
    return r.results[0]["out_0"]
```
